# Optimizing a Trainium2 kernel written in Bass

```python
import numpy as np
import jax
import jax.numpy as jnp

def _softmax(x, axis=-1):
    return jax.nn.softmax(x, axis=axis)

def _gelu(x):
    return jax.nn.gelu(x, approximate=True)

def _silu(x):
    return jax.nn.silu(x)

def _sigmoid(x):
    return jax.nn.sigmoid(x)

def _layernorm(x, axis=-1, eps=1e-05):
    m = jnp.mean(x, axis=axis, keepdims=True)
    v = jnp.var(x, axis=axis, keepdims=True)
    return (x - m) / jnp.sqrt(v + eps)

def _scatter_add(tgt, idx, src, axis=0):
    return tgt.at[idx].add(src)

def _segment_sum(src, seg, n):
    return jax.ops.segment_sum(src, seg, n)
kernel_name = 'mk_adaln_d2_jaxref_r8_93f8ba'

def setup_inputs(seed: int=0):
    np.random.seed(seed)
    _w = jnp.asarray

    def _L0_attn_setup():
        import math
        import jax, jax.numpy as jnp
        import numpy as np
        B, T, C = (2, 256, 128)
        HEADS = 16
        HD = C // HEADS

        def _rope_tables(seq_len, dim):
            pos = jnp.arange(seq_len, dtype=jnp.float32)
            freqs = 1.0 / 10000.0 ** (jnp.arange(0, dim, 2, dtype=jnp.float32) / dim)
            ang = pos[:, None] * freqs[None, :]
            return (jnp.sin(ang)[None, :, None, :], jnp.cos(ang)[None, :, None, :])

        def _apply_rope(t, sin, cos, dim):
            t1, t2 = (t[..., :dim // 2], t[..., dim // 2:])
            return jnp.concatenate([t1 * cos + t2 * sin, t1 * sin - t2 * cos], axis=-1)
        key = jax.random.key(seed)
        ks = jax.random.split(key, 5)
        s = 0.02
        return {'x': jax.random.normal(ks[0], (B, T, C), jnp.float32), 'Wq': jax.random.normal(ks[1], (C, C), jnp.float32) * s, 'bq': jnp.zeros((C,), jnp.float32), 'Wk': jax.random.normal(ks[2], (C, HD), jnp.float32) * s, 'bk': jnp.zeros((HD,), jnp.float32), 'Wv': jax.random.normal(ks[3], (C, HD), jnp.float32) * s, 'bv': jnp.zeros((HD,), jnp.float32), 'Wo': jax.random.normal(ks[4], (C, C), jnp.float32) * s, 'bo': jnp.zeros((C,), jnp.float32)}
    _L0_attn_in = _L0_attn_setup()

    def _L0_ffn_setup():
        import jax, jax.numpy as jnp
        import numpy as np
        B, S, M, E, DFF = (4, 256, 128, 8, 512)
        CAPACITY_FACTOR = 1.25

        def _top1_gate(tokens, wg, capacity):
            gates = jax.nn.softmax(tokens @ wg)
            expert_idx = jnp.argmax(gates, axis=-1)
            mask1 = jax.nn.one_hot(expert_idx, gates.shape[-1], dtype=gates.dtype)
            pos = jnp.sum(jnp.cumsum(mask1, axis=0) * mask1, axis=-1).astype(jnp.int32) - 1
            keep = (pos < capacity).astype(gates.dtype)
            mask1c = mask1 * keep[:, None]
            gates1 = jnp.sum(gates * mask1c, axis=-1)
            loc_oh = jax.nn.one_hot(pos, capacity, dtype=gates.dtype)
            combine = gates1[:, None, None] * mask1c[:, :, None] * loc_oh[:, None, :]
            dispatch = (combine > 0).astype(tokens.dtype)
            return (combine, dispatch)
        key = jax.random.key(seed)
        k = jax.random.split(key, 5)
        x = jax.random.normal(k[0], (B, S, M), dtype=jnp.float32)
        wg = jax.random.normal(k[1], (M, E), dtype=jnp.float32) * 0.02
        w1 = jax.random.normal(k[2], (E, M, DFF), dtype=jnp.float32) * 0.02
        b1 = jnp.zeros((E, DFF), dtype=jnp.float32)
        w2 = jax.random.normal(k[3], (E, DFF, M), dtype=jnp.float32) * 0.02
        b2 = jnp.zeros((E, M), dtype=jnp.float32)
        return {'x': x, 'wg': wg, 'w1': w1, 'b1': b1, 'w2': w2, 'b2': b2}
    _L0_ffn_in = _L0_ffn_setup()
    _L0_c = _w((lambda *s: np.random.randn(*s).astype(np.float32) * 0.05)(8, 128))
    _L0_wmod = _w((lambda *s: np.random.randn(*s).astype(np.float32) * 0.05)(128, 6 * 128) * 128 ** (-0.5))

    def _L1_attn_setup():
        import jax, jax.numpy as jnp
        import numpy as np
        B, N, C, H = (2, 256, 128, 16)
        D = C // H
        EPS = 1e-12

        def l2norm(t):
            n = jnp.linalg.norm(t, axis=-1, keepdims=True)
            return t / jnp.maximum(n, EPS)
        key = jax.random.key(seed)
        k1, k2, k3 = jax.random.split(key, 3)
        x = jax.random.normal(k1, (B, N, C), dtype=jnp.float32)
        qkv_w = jax.random.normal(k2, (3 * C, C), dtype=jnp.float32) * (1.0 / np.sqrt(C))
        temperature = jnp.ones((H, 1, 1), dtype=jnp.float32)
        proj_w = jax.random.normal(k3, (C, C), dtype=jnp.float32) * (1.0 / np.sqrt(C))
        proj_b = jnp.zeros((C,), dtype=jnp.float32)
        return {'x': x, 'qkv_w': qkv_w, 'temperature': temperature, 'proj_w': proj_w, 'proj_b': proj_b}
    _L1_attn_in = _L1_attn_setup()

    def _L1_ffn_setup():
        import jax, jax.numpy as jnp
        import numpy as np
        DIM = 128
        DEPTH = 2
        HEADS = 8
        DIM_HEAD = 64
        WINDOW = 64
        INNER = HEADS * DIM_HEAD
        HID = int(DIM * 4 * 2 / 3)
        B, N = (2, 1024)
        QK_SCALE = 8.0

        def shift_token(t):
            t1, t2 = jnp.split(t, 2, axis=-1)
            t2 = jnp.pad(t2, ((0, 0), (1, 0), (0, 0)))[:, :-1]
            return jnp.concatenate([t1, t2], axis=-1)

        def l2norm(t):
            return t / jnp.clip(jnp.linalg.norm(t, axis=-1, keepdims=True), 1e-12)

        def rotate_half(x):
            x1, x2 = jnp.split(x, 2, axis=-1)
            return jnp.concatenate([-x2, x1], axis=-1)

        def rotary_xpos(q, k):
            n = q.shape[-2]
            half_idx = jnp.arange(0, DIM_HEAD, 2, dtype=jnp.float32)
            inv_freq = 1.0 / 10000.0 ** (half_idx / DIM_HEAD)
            t = jnp.arange(n, dtype=jnp.float32)
            freqs = t[:, None] * inv_freq[None, :]
            freqs = jnp.concatenate([freqs, freqs], axis=-1)
            base = (half_idx + 0.4 * DIM_HEAD) / (1.4 * DIM_HEAD)
            power = (t - n // 2) / float(WINDOW // 2)
            scale = base[None, :] ** power[:, None]
            scale = jnp.concatenate([scale, scale], axis=-1)
            cos, sin = (jnp.cos(freqs), jnp.sin(freqs))
            q = q * cos * scale + rotate_half(q) * sin * scale
            k = k * cos / scale + rotate_half(k) * sin / scale
            return (q, k)

        def local_attention(q, k, v):
            b, h, n, d = q.shape
            w = n // WINDOW
            bq = q.reshape(b, h, w, WINDOW, d) * QK_SCALE
            bk = k.reshape(b, h, w, WINDOW, d)
            bv = v.reshape(b, h, w, WINDOW, d)

            def look_around(t):
                p = jnp.pad(t, ((0, 0), (0, 0), (1, 0), (0, 0), (0, 0)))
                return jnp.concatenate([p[:, :, :w], p[:, :, 1:]], axis=3)
            bk, bv = (look_around(bk), look_around(bv))
            bt = jnp.arange(n).reshape(w, WINDOW)
            btp = jnp.pad(bt, ((1, 0), (0, 0)), constant_values=-1)
            btk = jnp.concatenate([btp[:w], btp[1:]], axis=1)
            sim = jnp.einsum('bhwid,bhwjd->bhwij', bq, bk)
            i = bt[:, :, None]
            j = btk[:, None, :]
            mask = (i < j) | (i > j + WINDOW) | (j == -1)
            sim = jnp.where(mask, -jnp.finfo(sim.dtype).max, sim)
            attn = jax.nn.softmax(sim, axis=-1)
            out = jnp.einsum('bhwij,bhwjd->bhwid', attn, bv)
            return out.reshape(b, h, n, d)

        def _layer(x, wqkv, qs, ksc, wo, lg, lb, w1, b1, w2, b2):
            b, n, _ = x.shape
            h = shift_token(x)
            qkv = h @ wqkv
            q, k, v = jnp.split(qkv, 3, axis=-1)
            to_heads = lambda t: t.reshape(b, n, HEADS, DIM_HEAD).transpose(0, 2, 1, 3)
            q, k, v = (to_heads(q), to_heads(k), to_heads(v))
            q = l2norm(q) * qs
            k = l2norm(k) * ksc
            q, k = rotary_xpos(q, k)
            o = local_attention(q, k, v)
            o = o.transpose(0, 2, 1, 3).reshape(b, n, INNER)
            x = x + o @ wo
            h = shift_token(x)
            mu = h.mean(-1, keepdims=True)
            var = h.var(-1, keepdims=True)
            h = (h - mu) / jnp.sqrt(var + 1e-05) * lg + lb
            h = h @ w1 + b1
            a, g = jnp.split(h, 2, axis=-1)
            h = a * jax.nn.gelu(g, approximate=False)
            x = x + h @ w2 + b2
            return x
        key = jax.random.key(seed)
        ks = jax.random.split(key, 6)
        return {'x': jax.random.normal(ks[0], (B, N, DIM), jnp.float32), 'wqkv': jax.random.normal(ks[1], (DEPTH, DIM, 3 * INNER), jnp.float32) * 0.02, 'q_scale': jnp.ones((DEPTH, DIM_HEAD), jnp.float32), 'k_scale': jnp.ones((DEPTH, DIM_HEAD), jnp.float32), 'wo': jax.random.normal(ks[2], (DEPTH, INNER, DIM), jnp.float32) * 0.02, 'ln_g': jnp.ones((DEPTH, DIM), jnp.float32), 'ln_b': jnp.zeros((DEPTH, DIM), jnp.float32), 'w1': jax.random.normal(ks[3], (DEPTH, DIM, 2 * HID), jnp.float32) * 0.02, 'b1': jnp.zeros((DEPTH, 2 * HID), jnp.float32), 'w2': jax.random.normal(ks[4], (DEPTH, HID, DIM), jnp.float32) * 0.02, 'b2': jnp.zeros((DEPTH, DIM), jnp.float32)}
    _L1_ffn_in = _L1_ffn_setup()
    _L1_c = _w((lambda *s: np.random.randn(*s).astype(np.float32) * 0.05)(8, 128))
    _L1_wmod = _w((lambda *s: np.random.randn(*s).astype(np.float32) * 0.05)(128, 6 * 128) * 128 ** (-0.5))
    _d = {'L0_attn_x': _L0_attn_in['x'], 'L0_attn_Wq': _L0_attn_in['Wq'], 'L0_attn_bq': _L0_attn_in['bq'], 'L0_attn_Wk': _L0_attn_in['Wk'], 'L0_attn_bk': _L0_attn_in['bk'], 'L0_attn_Wv': _L0_attn_in['Wv'], 'L0_attn_bv': _L0_attn_in['bv'], 'L0_attn_Wo': _L0_attn_in['Wo'], 'L0_attn_bo': _L0_attn_in['bo'], 'L0_ffn_wg': _L0_ffn_in['wg'], 'L0_ffn_w1': _L0_ffn_in['w1'], 'L0_ffn_b1': _L0_ffn_in['b1'], 'L0_ffn_w2': _L0_ffn_in['w2'], 'L0_ffn_b2': _L0_ffn_in['b2'], 'L0_c': _L0_c, 'L0_wmod': _L0_wmod, 'L1_attn_qkv_w': _L1_attn_in['qkv_w'], 'L1_attn_temperature': _L1_attn_in['temperature'], 'L1_attn_proj_w': _L1_attn_in['proj_w'], 'L1_attn_proj_b': _L1_attn_in['proj_b'], 'L1_ffn_wqkv': _L1_ffn_in['wqkv'], 'L1_ffn_q_scale': _L1_ffn_in['q_scale'], 'L1_ffn_k_scale': _L1_ffn_in['k_scale'], 'L1_ffn_wo': _L1_ffn_in['wo'], 'L1_ffn_ln_g': _L1_ffn_in['ln_g'], 'L1_ffn_ln_b': _L1_ffn_in['ln_b'], 'L1_ffn_w1': _L1_ffn_in['w1'], 'L1_ffn_b1': _L1_ffn_in['b1'], 'L1_ffn_w2': _L1_ffn_in['w2'], 'L1_ffn_b2': _L1_ffn_in['b2'], 'L1_c': _L1_c, 'L1_wmod': _L1_wmod}
    _x0 = _d['L0_attn_x']
    _d['L0_attn_x'] = jax.random.normal(jax.random.fold_in(jax.random.key(seed), 1), (8, 512, 128), dtype=_x0.dtype)
    del _x0
    return _d

def reference(L0_attn_x, L0_attn_Wq, L0_attn_bq, L0_attn_Wk, L0_attn_bk, L0_attn_Wv, L0_attn_bv, L0_attn_Wo, L0_attn_bo, L0_ffn_wg, L0_ffn_w1, L0_ffn_b1, L0_ffn_w2, L0_ffn_b2, L0_c, L0_wmod, L1_attn_qkv_w, L1_attn_temperature, L1_attn_proj_w, L1_attn_proj_b, L1_ffn_wqkv, L1_ffn_q_scale, L1_ffn_k_scale, L1_ffn_wo, L1_ffn_ln_g, L1_ffn_ln_b, L1_ffn_w1, L1_ffn_b1, L1_ffn_w2, L1_ffn_b2, L1_c, L1_wmod):

    def _L0_attn_ref(x, Wq, bq, Wk, bk, Wv, bv, Wo, bo):
        import math
        import jax, jax.numpy as jnp
        import numpy as np
        B, T, C = (2, 256, 128)
        HEADS = 16
        HD = C // HEADS

        def _rope_tables(seq_len, dim):
            pos = jnp.arange(seq_len, dtype=jnp.float32)
            freqs = 1.0 / 10000.0 ** (jnp.arange(0, dim, 2, dtype=jnp.float32) / dim)
            ang = pos[:, None] * freqs[None, :]
            return (jnp.sin(ang)[None, :, None, :], jnp.cos(ang)[None, :, None, :])

        def _apply_rope(t, sin, cos, dim):
            t1, t2 = (t[..., :dim // 2], t[..., dim // 2:])
            return jnp.concatenate([t1 * cos + t2 * sin, t1 * sin - t2 * cos], axis=-1)
        Bx, Tx, Cx = x.shape
        q = (x @ Wq + bq).reshape(Bx, Tx, HEADS, HD)
        k = (x @ Wk + bk)[:, :, None, :]
        v = (x @ Wv + bv)[:, :, None, :]
        sin, cos = _rope_tables(Tx, HD)
        q = _apply_rope(q, sin, cos, HD)
        k = _apply_rope(k, sin, cos, HD)
        att = jnp.einsum('bthd,bThd->bhtT', q, k) / math.sqrt(HD)
        causal = jnp.triu(jnp.ones((Tx, Tx), bool), 1)
        att = jnp.where(causal, -jnp.inf, att)
        att = jax.nn.softmax(att, axis=-1)
        out = jnp.einsum('bhtT,bThd->bthd', att, v).reshape(Bx, Tx, Cx)
        return out @ Wo + bo

    def _L0_ffn_ref(x, wg, w1, b1, w2, b2):
        import jax, jax.numpy as jnp
        import numpy as np
        B, S, M, E, DFF = (4, 256, 128, 8, 512)
        CAPACITY_FACTOR = 1.25

        def _top1_gate(tokens, wg, capacity):
            gates = jax.nn.softmax(tokens @ wg)
            expert_idx = jnp.argmax(gates, axis=-1)
            mask1 = jax.nn.one_hot(expert_idx, gates.shape[-1], dtype=gates.dtype)
            pos = jnp.sum(jnp.cumsum(mask1, axis=0) * mask1, axis=-1).astype(jnp.int32) - 1
            keep = (pos < capacity).astype(gates.dtype)
            mask1c = mask1 * keep[:, None]
            gates1 = jnp.sum(gates * mask1c, axis=-1)
            loc_oh = jax.nn.one_hot(pos, capacity, dtype=gates.dtype)
            combine = gates1[:, None, None] * mask1c[:, :, None] * loc_oh[:, None, :]
            dispatch = (combine > 0).astype(tokens.dtype)
            return (combine, dispatch)
        d_model = x.shape[-1]
        tokens = x.reshape(-1, d_model)
        T = tokens.shape[0]
        num_experts = wg.shape[1]
        capacity = int(CAPACITY_FACTOR * T / num_experts)
        combine, dispatch = _top1_gate(tokens, wg, capacity)
        dispatched = jnp.einsum('sec,sm->ecm', dispatch, tokens)
        h = jax.nn.relu(jnp.einsum('ecm,emf->ecf', dispatched, w1) + b1[:, None, :])
        expert_out = jnp.einsum('ecf,efm->ecm', h, w2) + b2[:, None, :]
        combined = jnp.einsum('sec,ecm->sm', combine, expert_out)
        return combined.reshape(x.shape)

    def _L1_attn_ref(x, qkv_w, temperature, proj_w, proj_b):
        import jax, jax.numpy as jnp
        import numpy as np
        B, N, C, H = (2, 256, 128, 16)
        D = C // H
        EPS = 1e-12

        def l2norm(t):
            n = jnp.linalg.norm(t, axis=-1, keepdims=True)
            return t / jnp.maximum(n, EPS)
        b, n, c = x.shape
        qkv = jnp.einsum('bnc,fc->bnf', x, qkv_w)
        q, k, v = jnp.split(qkv, 3, axis=-1)
        q = l2norm(q)
        k = l2norm(k)
        q = q.reshape(b, n, H, D).transpose(0, 2, 1, 3)
        k = k.reshape(b, n, H, D).transpose(0, 2, 1, 3)
        v = v.reshape(b, n, H, D).transpose(0, 2, 1, 3)
        scale = 1.0 / np.sqrt(D)
        q = q * scale
        k = k * scale
        attn = jnp.einsum('bhnd,bhkd->bhnk', q, k)
        attn = attn / temperature
        attn = jax.nn.softmax(attn, axis=-1)
        out = jnp.einsum('bhnk,bhkd->bhnd', attn, v)
        out = out.transpose(0, 2, 1, 3).reshape(b, n, c)
        out = jnp.einsum('bnc,oc->bno', out, proj_w) + proj_b
        return out

    def _L1_ffn_ref(x, wqkv, q_scale, k_scale, wo, ln_g, ln_b, w1, b1, w2, b2):
        import jax, jax.numpy as jnp
        import numpy as np
        DIM = 128
        DEPTH = 2
        HEADS = 8
        DIM_HEAD = 64
        WINDOW = 64
        INNER = HEADS * DIM_HEAD
        HID = int(DIM * 4 * 2 / 3)
        B, N = (2, 1024)
        QK_SCALE = 8.0

        def shift_token(t):
            t1, t2 = jnp.split(t, 2, axis=-1)
            t2 = jnp.pad(t2, ((0, 0), (1, 0), (0, 0)))[:, :-1]
            return jnp.concatenate([t1, t2], axis=-1)

        def l2norm(t):
            return t / jnp.clip(jnp.linalg.norm(t, axis=-1, keepdims=True), 1e-12)

        def rotate_half(x):
            x1, x2 = jnp.split(x, 2, axis=-1)
            return jnp.concatenate([-x2, x1], axis=-1)

        def rotary_xpos(q, k):
            n = q.shape[-2]
            half_idx = jnp.arange(0, DIM_HEAD, 2, dtype=jnp.float32)
            inv_freq = 1.0 / 10000.0 ** (half_idx / DIM_HEAD)
            t = jnp.arange(n, dtype=jnp.float32)
            freqs = t[:, None] * inv_freq[None, :]
            freqs = jnp.concatenate([freqs, freqs], axis=-1)
            base = (half_idx + 0.4 * DIM_HEAD) / (1.4 * DIM_HEAD)
            power = (t - n // 2) / float(WINDOW // 2)
            scale = base[None, :] ** power[:, None]
            scale = jnp.concatenate([scale, scale], axis=-1)
            cos, sin = (jnp.cos(freqs), jnp.sin(freqs))
            q = q * cos * scale + rotate_half(q) * sin * scale
            k = k * cos / scale + rotate_half(k) * sin / scale
            return (q, k)

        def local_attention(q, k, v):
            b, h, n, d = q.shape
            w = n // WINDOW
            bq = q.reshape(b, h, w, WINDOW, d) * QK_SCALE
            bk = k.reshape(b, h, w, WINDOW, d)
            bv = v.reshape(b, h, w, WINDOW, d)

            def look_around(t):
                p = jnp.pad(t, ((0, 0), (0, 0), (1, 0), (0, 0), (0, 0)))
                return jnp.concatenate([p[:, :, :w], p[:, :, 1:]], axis=3)
            bk, bv = (look_around(bk), look_around(bv))
            bt = jnp.arange(n).reshape(w, WINDOW)
            btp = jnp.pad(bt, ((1, 0), (0, 0)), constant_values=-1)
            btk = jnp.concatenate([btp[:w], btp[1:]], axis=1)
            sim = jnp.einsum('bhwid,bhwjd->bhwij', bq, bk)
            i = bt[:, :, None]
            j = btk[:, None, :]
            mask = (i < j) | (i > j + WINDOW) | (j == -1)
            sim = jnp.where(mask, -jnp.finfo(sim.dtype).max, sim)
            attn = jax.nn.softmax(sim, axis=-1)
            out = jnp.einsum('bhwij,bhwjd->bhwid', attn, bv)
            return out.reshape(b, h, n, d)

        def _layer(x, wqkv, qs, ksc, wo, lg, lb, w1, b1, w2, b2):
            b, n, _ = x.shape
            h = shift_token(x)
            qkv = h @ wqkv
            q, k, v = jnp.split(qkv, 3, axis=-1)
            to_heads = lambda t: t.reshape(b, n, HEADS, DIM_HEAD).transpose(0, 2, 1, 3)
            q, k, v = (to_heads(q), to_heads(k), to_heads(v))
            q = l2norm(q) * qs
            k = l2norm(k) * ksc
            q, k = rotary_xpos(q, k)
            o = local_attention(q, k, v)
            o = o.transpose(0, 2, 1, 3).reshape(b, n, INNER)
            x = x + o @ wo
            h = shift_token(x)
            mu = h.mean(-1, keepdims=True)
            var = h.var(-1, keepdims=True)
            h = (h - mu) / jnp.sqrt(var + 1e-05) * lg + lb
            h = h @ w1 + b1
            a, g = jnp.split(h, 2, axis=-1)
            h = a * jax.nn.gelu(g, approximate=False)
            x = x + h @ w2 + b2
            return x
        for l in range(DEPTH):
            x = _layer(x, wqkv[l], q_scale[l], k_scale[l], wo[l], ln_g[l], ln_b[l], w1[l], b1[l], w2[l], b2[l])
        return x
    x = L0_attn_x
    mod = (_silu(L0_c) @ L0_wmod).reshape(L0_c.shape[0], 6, 1, -1)
    sa, ca, ga, sb, cb, gb = (mod[:, 0], mod[:, 1], mod[:, 2], mod[:, 3], mod[:, 4], mod[:, 5])
    ga = (2 * (ga >= 0) - 1) * jnp.maximum(jnp.abs(ga), 0.25)
    gb = (2 * (gb >= 0) - 1) * jnp.maximum(jnp.abs(gb), 0.25)
    h = _layernorm(x, axis=-1) * (1 + ca) + sa
    x = x + ga * _L0_attn_ref(h, L0_attn_Wq, L0_attn_bq, L0_attn_Wk, L0_attn_bk, L0_attn_Wv, L0_attn_bv, L0_attn_Wo, L0_attn_bo)
    h = _layernorm(x, axis=-1) * (1 + cb) + sb
    x = x + gb * _L0_ffn_ref(h, L0_ffn_wg, L0_ffn_w1, L0_ffn_b1, L0_ffn_w2, L0_ffn_b2)
    mod = (_silu(L1_c) @ L1_wmod).reshape(L1_c.shape[0], 6, 1, -1)
    sa, ca, ga, sb, cb, gb = (mod[:, 0], mod[:, 1], mod[:, 2], mod[:, 3], mod[:, 4], mod[:, 5])
    ga = (2 * (ga >= 0) - 1) * jnp.maximum(jnp.abs(ga), 0.25)
    gb = (2 * (gb >= 0) - 1) * jnp.maximum(jnp.abs(gb), 0.25)
    h = _layernorm(x, axis=-1) * (1 + ca) + sa
    x = x + ga * _L1_attn_ref(h, L1_attn_qkv_w, L1_attn_temperature, L1_attn_proj_w, L1_attn_proj_b)
    h = _layernorm(x, axis=-1) * (1 + cb) + sb
    x = x + gb * _L1_ffn_ref(h, L1_ffn_wqkv, L1_ffn_q_scale, L1_ffn_k_scale, L1_ffn_wo, L1_ffn_ln_g, L1_ffn_ln_b, L1_ffn_w1, L1_ffn_b1, L1_ffn_w2, L1_ffn_b2)
    return x

_drawn_inputs = setup_inputs


def setup_inputs(seed=0):
    import zlib

    import numpy as np

    out = dict(_drawn_inputs(seed))
    spreads = {'L0_attn_bq': (0.0, 0.8),
     'L0_attn_bk': (0.0, 0.8),
     'L0_attn_bv': (0.0, 0.8),
     'L0_attn_bo': (0.0, 0.307),
     'L0_ffn_b1': (0.0, 0.8),
     'L0_ffn_b2': (0.0, 0.8),
     'L1_attn_temperature': (1.0, 0.6),
     'L1_attn_proj_b': (0.0, 0.307),
     'L1_ffn_q_scale': (1.0, 0.6),
     'L1_ffn_k_scale': (1.0, 0.6),
     'L1_ffn_ln_g': (1.0, 0.6),
     'L1_ffn_ln_b': (0.0, 0.8),
     'L1_ffn_b1': (0.0, 0.8),
     'L1_ffn_b2': (0.0, 0.8)}
    factors = {'L0_attn_Wq': 8.0,
     'L0_attn_Wk': 8.0,
     'L0_attn_Wv': 8.0,
     'L0_attn_Wo': 8.0,
     'L0_ffn_wg': 8.0,
     'L0_ffn_w1': 8.0,
     'L0_ffn_w2': 8.0,
     'L1_attn_qkv_w': 4.703,
     'L1_attn_proj_w': 4.587,
     'L1_ffn_wqkv': 7.48,
     'L1_ffn_wo': 7.504,
     'L1_ffn_w1': 8.0,
     'L1_ffn_w2': 8.0}
    for name, (base, spread) in spreads.items():
        noise = np.random.default_rng([zlib.crc32(name.encode()), seed]).standard_normal(out[name].shape)
        drawn = base * np.exp(spread * noise) if base else spread * noise
        out[name] = jnp.asarray(drawn.astype(out[name].dtype))
    for name, factor in factors.items():
        out[name] = (out[name] * factor).astype(out[name].dtype)
    return out
```

```python
from contextlib import ExitStack, contextmanager

import numpy as np

import concourse.bass as bass
from concourse import mybir

F32 = mybir.dt.float32
BF16 = mybir.dt.bfloat16
I32 = mybir.dt.int32
ALU = mybir.AluOpType
ACT = mybir.ActivationFunctionType
AX = mybir.AxisListType

P = 128
B, N, C = 8, 512, 128
NT = B * N
H, D = 16, 8
UNITS = 4
UH = H // UNITS
CH = N // P
PARTS = 3
TERMS = PARTS * PARTS
RK = TERMS * D
RM = RK + PARTS
VW = 32
NEG = -1.0e30
E, F = 8, 512
CAP = NT * 5 // 4 // E
PAIRS, HD = 4, 64
INNER = 2 * PAIRS * HD
W = 64
WIN = W + P
HID = C * 4 * 2 // 3
HC = -(-HID // P)
QK_SCALE = 8.0
LN_EPS = 1e-5
L2_EPS = 1e-12


class Program:

    def __init__(self, nc, ctx, ins):
        self.nc, self.ctx, self.ins, self.sems = nc, ctx, ins, {}
        self.held = [ctx]
        self.attention_setups = 0
        self.count = 0

    def sb(self, name, shape, dt=F32):
        self.count += 1
        return self.held[-1].enter_context(self.nc.sbuf_tensor(f"{name}_sb{self.count}", shape, dt))

    @contextmanager
    def memory(self):
        with ExitStack() as held:
            self.held.append(held)
            yield
            self.held.pop()

    def sem(self, name):
        if name not in self.sems:
            self.sems[name] = self.ctx.enter_context(self.nc.semaphore(name))
        return self.sems[name]

    def dram(self, name, shape, dt=F32):
        return self.nc.dram_tensor(name, shape, dt, kind="Internal").ap()


def setup(g):
    nc, ins = g.nc, g.ins
    g.bank = [g.ctx.enter_context(nc.psum_tensor(f"bank{i}", [P, 512], F32)) for i in range(8)]
    g.ident = g.sb("ident", [P, P])
    g.identb = g.sb("identb", [P, P], BF16)
    g.mean_w = g.sb("mean_w", [P, P])
    g.sel_sum = g.sb("sel_sum", [P, P])
    g.maskf = g.sb("maskf", [P, 2, P])
    g.mask = g.sb("mask", [P, 2, P], BF16)
    g.mod = g.sb("mod", [P, 6, 2 * B])
    cT = g.sb("cT", [P, 2, B])
    sil = g.sb("sil", [P, 2, B])
    tmp = g.sb("mod_tmp", [P, 4, 2 * B])
    wmod = g.sb("wmod", [P, 2, 6 * C])
    ld, prod = g.sem("setup_loaded"), g.sem("mod_products")
    v, ex = g.sem("setup_vector"), g.sem("exp_of_c")
    with nc.Block() as block:
        @block.sync
        def _(sp):
            for dst, src in ((g.ident[:, :], ins["ident"]), (g.mean_w[:, :], ins["mean_w"]),
                             (g.sel_sum[:, :], ins["sel_sum"]), (g.maskf[:, :, :], ins["masks"]),
                             (cT[:, :, :], ins["cT"]), (wmod[:, :, :], ins["wmod"])):
                sp.dma_start(dst, src).then_inc(ld, 16)

        @block.scalar
        def _(act):
            act.wait_ge(ld, 96)
            act.activation(sil[:, :, :], cT[:, :, :], ACT.Exp, scale=-1.0).then_inc(ex, 1)

        @block.tensor
        def _(pe):
            pe.wait_ge(ld, 96)
            pe.wait_ge(v, 5)
            for layer in range(2):
                for j in range(6):
                    at = 16 * j + 8 * layer
                    mm = pe.matmul(g.bank[0][:, at:at + B], wmod[:, layer, j * C:(j + 1) * C],
                                   sil[:, layer, :], start=(layer + j == 0), stop=True, skip_group_check=True)
            mm.then_inc(prod, 1)

        @block.vector
        def _(dve):
            n = 0

            def step(ins_):
                nonlocal n
                n += 1
                ins_.then_inc(v, 1)
                dve.wait_ge(v, n)

            dve.wait_ge(ld, 96)
            step(dve.tensor_copy(g.identb[:, :], g.ident[:, :]))
            step(dve.tensor_copy(g.mask[:, :, :], g.maskf[:, :, :]))
            dve.wait_ge(ex, 1)
            step(dve.tensor_scalar(sil[:, :, :], sil[:, :, :], 1.0, None, ALU.add))
            step(dve.reciprocal(sil[:, :, :], sil[:, :, :]))
            step(dve.tensor_tensor(sil[:, :, :], sil[:, :, :], cT[:, :, :], ALU.mult))
            dve.wait_ge(prod, 1)
            step(dve.tensor_copy(g.mod[:, :, :], g.bank[0][:, 0:96].rearrange("p (j b) -> p j b", j=6)))
            for j in (1, 4):
                step(dve.tensor_scalar(g.mod[:, j, :], g.mod[:, j, :], 1.0, None, ALU.add))
            for j in (2, 5):
                step(dve.tensor_scalar(tmp[:, 0, :], g.mod[:, j, :], 0.0, 2.0, ALU.is_ge, ALU.mult))
                step(dve.tensor_scalar(tmp[:, 1, :], tmp[:, 0, :], -1.0, None, ALU.add))
                step(dve.scalar_tensor_tensor(out=tmp[:, 2, :], in0=g.mod[:, j, :], scalar=-1.0, in1=g.mod[:, j, :],
                                              op0=ALU.mult, op1=ALU.max))
                step(dve.scalar_tensor_tensor(out=g.mod[:, j, :], in0=tmp[:, 2, :], scalar=0.25, in1=tmp[:, 1, :],
                                              op0=ALU.max, op1=ALU.mult))


def setup_projection(g):
    nc = g.nc
    g.wq = g.sb("wq", [P, 2, 6, C])
    g.pcol = g.sb("pcol", [P, 6])
    g.rope = g.sb("rope", [P, 2, N])
    g.bv = g.sb("bv", [P, C])
    g.ones_w = g.sb("ones_w", [P, P])
    g.x_in = g.sb("x_in", [P, N])
    g.xc = g.sb("xc", [P, N])
    g.sq = g.sb("sq", [P, N])
    g.std = g.sb("std", [P, N])
    g.rstd = g.sb("rstd", [P, N])
    g.eps = g.sb("eps", [P, 1])
    g.xh = g.sb("xh", [P, N])
    g.h = g.sb("h", [P, N])
    g.ra = g.sb("ra", [P, 2, N])
    g.rb = g.sb("rb", [P, 2, N])
    g.qk = g.sb("qk", [P, 2, N])
    g.res = g.sb("res", [P, 2, N])
    g.res2 = g.sb("norms", [P, 2, N])
    g.parts = g.sb("parts", [P, 2, PARTS, N], BF16)
    g.vpad = g.sb("vpad", [P, CH, H, VW])
    g.ps = {n: g.sem("p_" + n) for n in (
        "setup", "setup_dve", "x_loaded", "mean", "xc", "sq", "var", "std", "rstd", "xh", "h", "qk_psum", "v_psum", "ra",
        "rb", "rot", "sumsq", "sumsq_psum", "norm", "part1", "res1", "part2", "part3", "parts_stored", "v_stored", "v_padded")}
    s = g.ps
    with nc.Block() as block:
        @block.sync
        def _(sp):
            for dst, src in ((g.wq[:, :, :, :], g.ins["wqkv"]), (g.pcol[:, 0:5], g.ins["pcol"]),
                             (g.rope[:, :, :], g.ins["rope"]), (g.bv[:, :], g.ins["bv"])):
                sp.dma_start(dst, src).then_inc(s["setup"], 16)

        @block.gpsimd
        def _(pool):
            pool.memset(g.ones_w[:, :], 1.0)
            pool.memset(g.eps[:, :], LN_EPS)
            pool.memset(g.vpad[:, :, :, :], 0.0).then_inc(s["v_padded"], 1)
            pool.wait_ge(s["v_padded"], 1)
            pool.memset(g.vpad[:, :, :, D:D + 1], 1.0)

        @block.vector
        def _(dve):
            dve.wait_ge(s["setup"], 64)
            dve.reciprocal(g.pcol[:, 5:6], g.pcol[:, 4:5]).then_inc(s["setup_dve"], 1)
            dve.wait_ge(s["setup_dve"], 1)
            dve.tensor_scalar(g.pcol[:, 5:6], g.pcol[:, 5:6], 1.0 / D, None, ALU.mult)


def project(g, layer, x):
    nc, s = g.nc, g.ps
    lo, hi = B * layer, B * (layer + 1)
    nmm = 4 if layer == 0 else 2

    with nc.Block() as block:
        @block.sync
        def _(sp):
            with sp.Fori(lo, hi) as it:
                sp.wait_ge(s["xc"], it)
                sp.dma_start(g.x_in[:, :], x[it - lo]).then_inc(s["x_loaded"], 16)
                for w in range(2):
                    sp.wait_ge(s["part3"], it * 2 + w + 1)
                    for part in range(PARTS):
                        sp.dma_start(g.qk_dram[it, w, :, part].rearrange("u d h n -> u (d h) n"),
                                     g.parts[:, w, part, :]).then_inc(s["parts_stored"], 16)
                sp.wait_ge(s["v_stored"], it * 17 + 1)
                sp.dma_start(g.v_dram[it].rearrange("c p m -> p c m"),
                             g.vpad[:, :, :, :].rearrange("p c h w -> p c (h w)")).then_inc(s["v_stored"], 16)
            sp.wait_ge(s["parts_stored"], hi * 2 * PARTS * 16)
            sp.wait_ge(s["v_stored"], hi * 17)

        @block.tensor
        def _(pe):
            with pe.Fori(lo, hi) as it:
                pe.wait_ge(s["x_loaded"], it * 16 + 16)
                pe.wait_ge(s["xc"], it)
                pe.matmul(g.bank[0][:, :], g.mean_w[:, :], g.x_in[:, :], start=True, stop=True).then_inc(s["mean"], 1)
                pe.wait_ge(s["sq"], it + 1)
                pe.wait_ge(s["std"], it)
                pe.matmul(g.bank[1][:, :], g.mean_w[:, :], g.sq[:, :], start=True, stop=True).then_inc(s["var"], 1)
                pe.wait_ge(s["h"], it + 1)
                if layer == 0:
                    for m in range(4):
                        w = m // 2
                        done = s["ra"] if m % 2 == 0 else s["rb"]
                        pe.wait_ge(done, it * 2)
                        pe.matmul(g.bank[2 + m][:, :], g.wq[:, 0, m, :], g.h[:, :],
                                  start=True, stop=True).then_inc(s["qk_psum"], 1)
                else:
                    for m in range(2):
                        pe.wait_ge(s["rot"], it * 2)
                        pe.matmul(g.bank[2 + m][:, :], g.wq[:, 1, m, :], g.h[:, :],
                                  start=True, stop=True).then_inc(s["qk_psum"], 2)
                pe.wait_ge(s["v_stored"], it * 17)
                for c in range(CH):
                    mm = pe.matmul(g.bank[6][:, c * C:(c + 1) * C], g.h[:, c * P:(c + 1) * P],
                                   g.wq[:, layer, 4 if layer == 0 else 2, :], start=(c == 0), stop=True,
                                   skip_group_check=True)
                mm.then_inc(s["v_psum"], 1)
                if layer == 1:
                    for w in range(2):
                        pe.wait_ge(s["sumsq"], (it - lo) * 2 + w + 1)
                        pe.wait_ge(s["ra"], it * 2)
                        pe.matmul(g.bank[4 + w][:, :], g.ones_w[:, :], g.ra[:, w, :],
                                  start=True, stop=True).then_inc(s["sumsq_psum"], 1)

        @block.scalar
        def _(act):
            with act.Fori(lo, hi) as it:
                act.wait_ge(s["xc"], it + 1)
                act.wait_ge(s["var"], it)
                act.activation(g.sq[:, :], g.xc[:, :], ACT.Square).then_inc(s["sq"], 1)
                act.wait_ge(s["var"], it + 1)
                act.wait_ge(s["xh"], it)
                act.activation(g.std[:, :], g.bank[1][:, :], ACT.Sqrt, bias=g.eps[:, 0:1]).then_inc(s["std"], 1)
                if layer == 1:
                    for w in range(2):
                        act.wait_ge(s["qk_psum"], it * 4 + 2 * w + 2)
                        act.wait_ge(s["sumsq_psum"], (it - lo) * 2 + w)
                        act.activation(g.ra[:, w, :], g.bank[2 + w][:, :], ACT.Square).then_inc(s["sumsq"], 1)
                    for w in range(2):
                        act.wait_ge(s["sumsq_psum"], (it - lo) * 2 + w + 1)
                        act.wait_ge(s["ra"], it * 2)
                        act.activation(g.rb[:, w, :], g.bank[4 + w][:, :], ACT.Sqrt).then_inc(s["norm"], 1)
                for w in range(2):
                    act.wait_ge(s["rot"], it * 2 + w + 1)
                    act.wait_ge(s["parts_stored"], it * 2 * PARTS * 16)
                    act.activation(g.parts[:, w, 0, :], g.qk[:, w, :], ACT.Copy).then_inc(s["part1"], 1)
                    act.wait_ge(s["res1"], it * 2 + w + 1)
                    act.activation(g.parts[:, w, 1, :], g.res[:, w, :], ACT.Copy).then_inc(s["part2"], 1)

        @block.gpsimd
        def _(pool):
            with pool.Fori(lo, hi) as it:
                for w in range(2):
                    pool.wait_ge(s["part1"], it * 2 + w + 1)
                    pool.wait_ge(s["part3"], it * 2 + w)
                    pool.tensor_tensor(g.res[:, w, :], g.qk[:, w, :], g.parts[:, w, 0, :],
                                       ALU.subtract).then_inc(s["res1"], 1)
                    pool.wait_ge(s["part2"], it * 2 + w + 1)
                    pool.tensor_tensor(g.parts[:, w, 2, :], g.res[:, w, :], g.parts[:, w, 1, :],
                                       ALU.subtract).then_inc(s["part3"], 1)

        @block.vector
        def _(dve):
            with dve.Fori(lo, hi) as it:
                dve.wait_ge(s["mean"], it + 1)
                dve.wait_ge(s["xh"], it)
                dve.wait_ge(s["sq"], it)
                dve.tensor_tensor(g.xc[:, :], g.x_in[:, :], g.bank[0][:, :], ALU.subtract).then_inc(s["xc"], 1)
                dve.wait_ge(s["std"], it + 1)
                dve.wait_ge(s["xc"], it + 1)
                dve.wait_ge(s["h"], it)
                dve.reciprocal(g.rstd[:, :], g.std[:, :]).then_inc(s["rstd"], 1)
                dve.wait_ge(s["rstd"], it + 1)
                dve.tensor_tensor(g.xh[:, :], g.xc[:, :], g.rstd[:, :], ALU.mult).then_inc(s["xh"], 1)
                dve.wait_ge(s["xh"], it + 1)
                dve.wait_ge(s["v_psum"], it)
                dve.tensor_scalar(g.h[:, :], g.xh[:, :], g.mod[:, 1, bass.ds(it, 1)], g.mod[:, 0, bass.ds(it, 1)],
                                  ALU.mult, ALU.add).then_inc(s["h"], 1)
                for w in range(2):
                    dve.wait_ge(s["part3"], it * 2 + w)
                    if layer == 0:
                        dve.wait_ge(s["qk_psum"], it * 4 + 2 * w + 1)
                        dve.wait_ge(s["rot"], it * 2 + w)
                        dve.scalar_tensor_tensor(out=g.ra[:, w, :], in0=g.bank[2 + 2 * w][:, :],
                                                 scalar=g.pcol[:, 2 * w:2 * w + 1], in1=g.rope[:, 0, :],
                                                 op0=ALU.add, op1=ALU.mult).then_inc(s["ra"], 1)
                        dve.wait_ge(s["qk_psum"], it * 4 + 2 * w + 2)
                        dve.scalar_tensor_tensor(out=g.rb[:, w, :], in0=g.bank[3 + 2 * w][:, :],
                                                 scalar=g.pcol[:, 2 * w + 1:2 * w + 2], in1=g.rope[:, 1, :],
                                                 op0=ALU.add, op1=ALU.mult).then_inc(s["rb"], 1)
                        dve.wait_ge(s["ra"], it * 2 + w + 1)
                        dve.wait_ge(s["rb"], it * 2 + w + 1)
                        dve.tensor_tensor(g.qk[:, w, :], g.ra[:, w, :], g.rb[:, w, :], ALU.add).then_inc(s["rot"], 1)
                    else:
                        dve.wait_ge(s["norm"], (it - lo) * 2 + w + 1)
                        dve.wait_ge(s["rot"], it * 2 + w)
                        dve.tensor_scalar(g.res2[:, w, :], g.rb[:, w, :], L2_EPS, None, ALU.max).then_inc(s["ra"], 1)
                        dve.wait_ge(s["ra"], it * 2 + w + 1)
                        dve.reciprocal(g.res2[:, w, :], g.res2[:, w, :]).then_inc(s["rb"], 1)
                        dve.wait_ge(s["rb"], it * 2 + w + 1)
                        dve.scalar_tensor_tensor(out=g.qk[:, w, :], in0=g.bank[2 + w][:, :],
                                                 scalar=g.pcol[:, 5:6] if w == 0 else 1.0, in1=g.res2[:, w, :],
                                                 op0=ALU.mult, op1=ALU.mult).then_inc(s["rot"], 1)
                dve.wait_ge(s["v_psum"], it + 1)
                dve.wait_ge(s["v_stored"], it * 17)
                psum = g.bank[6][:, :].rearrange("p (c h d) -> p c h d", c=CH, d=D)
                out = g.vpad[:, :, :, 0:D]
                if layer == 0:
                    bv = g.bv[:, :].rearrange("p (h d) -> p h d", d=D)
                    for c in range(CH):
                        last = dve.tensor_tensor(out[:, c], psum[:, c], bv, ALU.add)
                else:
                    last = dve.tensor_copy(out, psum)
                last.then_inc(s["v_stored"], 1)


def setup_attention(g):
    nc = g.nc
    g.Q = g.sb("Q", [RM, UNITS, UH, N], BF16)
    g.K = g.sb("K", [RM, UNITS, UH, N], BF16)
    g.V = g.sb("V", [P, UNITS, CH, UH * VW])
    g.wo = g.sb("wo", [P, 2, UNITS, C])
    g.bo = g.sb("bo", [P, 2])
    g.M = g.sb("M", [P, 2, CH, UH])
    g.mneg = g.sb("mneg", [UH, N])
    g.mres = g.sb("mres", [UH, N])
    g.mparts = g.sb("mparts", [UH, PARTS, N], BF16)
    g.probs = g.sb("probs", [P, 2, UH, N])
    g.osum = g.sb("osum", [P, N])
    g.rsum = g.sb("rsum", [P, N])
    g.onorm = g.sb("onorm", [P, N])
    g.xres = g.sb("xres", [P, N])
    g.ytmp = g.sb("ytmp", [P, N])
    g.xnew = g.sb("xnew", [P, N])
    g.as_ = {n: g.sem("a_" + n) for n in (
        "setup", "k_ones", "a_scores", "a_max", "max_turned", "mneg", "mpart1", "mres", "mpart2", "mpart3", "m_stored",
        "m_loaded", "b_scores", "exp", "pv", "o_copied", "sums", "rsum", "onorm", "yacc", "x_loaded", "ytmp", "xnew",
        "x_stored")}
    g.loaded = [g.sem(f"a_loaded{i}") for i in range(UNITS)]
    g.attention_setups += 1
    n_setup = g.attention_setups
    with nc.Block() as block:
        @block.sync
        def _(sp):
            sp.dma_start(g.wo[:, :, :, :], g.ins["wo"]).then_inc(g.as_["setup"], 16)
            sp.dma_start(g.bo[:, :], g.ins["bo"]).then_inc(g.as_["setup"], 16)
            sp.wait_ge(g.as_["setup"], 32 * n_setup)

        @block.gpsimd
        def _(pool):
            pool.memset(g.K[64:RM, :, :, :], 1.0)


def attend(g, layer, x, x_out):
    nc, s = g.nc, g.as_
    causal = layer == 0
    lo, hi = B * layer, B * (layer + 1)
    per = CH * UH
    nd = 3 + 3 + 1
    scale = float(D) ** -0.5 if layer == 0 else 1.0
    SA, SB, OB, MB, SUMB, YB = g.bank[0:2], g.bank[2:4], g.bank[4], g.bank[5], g.bank[6], g.bank[7]
    hk = (lambda h: 0) if causal else (lambda h: h)

    def first_query(k):
        return P * k if causal else 0

    def steps(i, last):
        return [(q, q + 2 if not (last and q >= 2) else None) for q in range(UNITS)]

    with nc.Block() as block:
        @block.sync
        def _(sp):
            def load(i, u):
                it, q = (i, u) if u < UNITS else (i + 1, u - UNITS)
                slot = q
                for part in range(PARTS):
                    src = g.qk_dram[it, 0, q, part].rearrange("d h n -> d (h n)")
                    for t in range(PARTS):
                        r = (PARTS * part + t) * D
                        sp.dma_start(g.Q[r:r + D, slot, :, :].rearrange("d h n -> d (h n)"), src)\
                          .then_inc(g.loaded[slot], 16)
                    src = g.qk_dram[it, 1, q].rearrange("s d h n -> (s d) h n")
                    r = PARTS * part * D
                    if causal:
                        sp.dma_start(g.K[r:r + PARTS * D, slot, 0, :], src[:, 0, :]).then_inc(g.loaded[slot], 16)
                    else:
                        sp.dma_start(g.K[r:r + PARTS * D, slot, :, :], src).then_inc(g.loaded[slot], 16)
                sp.dma_start(g.V[:, slot, :, :], g.v_dram[it].rearrange(
                    "c p (u m) -> p c u m", u=UNITS)[:, :, q, :]).then_inc(g.loaded[slot], 16)

            def move_max(i, u):
                at = i * 4 + u
                sp.wait_ge(s["mpart3"], at + 1)
                sp.dma_start(g.m_dram, g.mparts[:, :, :]).then_inc(s["m_stored"], 16)
                sp.wait_ge(s["m_stored"], at * 16 + 16)
                sp.dma_start(g.Q[RK:RM, u % UNITS, :, :], g.m_dram.rearrange("h s n -> s h n"))\
                    .then_inc(s["m_loaded"], 16)

            def batch(i, last):
                sp.wait_ge(s["ytmp"], i)
                sp.wait_ge(s["xnew"], i)
                sp.dma_start(g.xres[:, :], x[i - lo]).then_inc(s["x_loaded"], 16)
                for q in range(UNITS):
                    if not last or q == 0:
                        sp.wait_ge(s["pv"], i * 16 + 4 * q)
                        load(i, q + 3)
                    if q and (not last or q < 3):
                        move_max(i, q + 1)
                if not last:
                    move_max(i, UNITS + 1)
                sp.wait_ge(s["xnew"], i + 1)
                sp.dma_start(x_out[i - lo], g.xnew[:, :]).then_inc(s["x_stored"], 16)

            for u in range(3):
                load(lo, u)
            for u in range(2):
                move_max(lo, u)
            with sp.Fori(lo, hi - 1) as i:
                batch(i, False)
            batch(hi - 1, True)
            sp.wait_ge(s["x_stored"], hi * 16)

        LOADS = 13 * 16

        @block.tensor
        def _(pe):
            def a_tile(i, u, k, h):
                n = u * per + k * UH + h
                slot, t = u % UNITS, n % 2
                width = P * (k + 1) if causal else N
                if k + h == 0:
                    pe.wait_ge(g.loaded[slot], (i + u // UNITS) * LOADS + LOADS)
                if (u, k) != (0, 0) or h >= 2 or lo:
                    pe.wait_ge(s["a_max"], i * 64 + n - 1)
                mm = pe.matmul(SA[t][:, 0:width], g.Q[0:RK, slot, h, k * P:(k + 1) * P],
                               g.K[0:RK, slot, hk(h), 0:width], start=True, stop=not causal)
                if causal:
                    mm = pe.matmul(SA[t][:, width - P:width], g.identb[:, :], g.mask[:, 0, :], start=False, stop=True)
                mm.then_inc(s["a_scores"], 1)

            def turn_max(i, u):
                pe.wait_ge(s["a_max"], i * 64 + (u + 1) * per)
                pe.wait_ge(s["mneg"], 2 * (i * 4 + u))
                for k in range(CH):
                    mm = pe.transpose(MB[0:UH, k * P:(k + 1) * P], g.M[:, u % 2, k, :], g.ident[:, :])
                mm.then_inc(s["max_turned"], 1)

            def b_tile(i, q, k, h):
                n = q * per + k * UH + h
                t0 = first_query(k)
                if k + h == 0:
                    pe.wait_ge(s["m_loaded"], i * 64 + 16 * q + 16)
                if n >= 2:
                    pe.wait_ge(s["exp"], i * 64 + n - 1)
                mm = pe.matmul(SB[n % 2][:, t0:N], g.K[0:RM, q, hk(h), k * P:(k + 1) * P],
                               g.Q[0:RM, q, h, t0:N], start=True, stop=not causal)
                if causal:
                    mm = pe.matmul(SB[n % 2][:, t0:t0 + P], g.identb[:, :], g.mask[:, 1, :], start=False, stop=True)
                mm.then_inc(s["b_scores"], 1)

            def pv(i, q, k):
                t0 = first_query(k)
                pe.wait_ge(s["exp"], i * 64 + q * per + (k + 1) * UH)
                if k == 0:
                    pe.wait_ge(s["o_copied"], i * 4 + q)
                for h in range(UH):
                    mm = pe.matmul(OB[VW * h:VW * (h + 1), t0:N], g.V[:, q, k, VW * h:VW * (h + 1)],
                                   g.probs[:, k % 2, h, t0:N], start=(k == 0), stop=(k == CH - 1),
                                   skip_group_check=True)
                mm.then_inc(s["pv"], 1)

            def spread_sums(i, q):
                pe.wait_ge(s["o_copied"], i * 4 + q + 1)
                pe.wait_ge(s["rsum"], i * 4 + q)
                pe.matmul(SUMB[:, :], g.sel_sum[:, :], g.osum[:, :], start=True, stop=True).then_inc(s["sums"], 1)

            def out_project(i, q):
                pe.wait_ge(s["onorm"], i * 4 + q + 1)
                if q == 0:
                    pe.wait_ge(s["ytmp"], i)
                pe.matmul(YB[:, :], g.wo[:, layer, q, :], g.onorm[:, :], start=(q == 0), stop=(q == UNITS - 1),
                          skip_group_check=True).then_inc(s["yacc"], 1)

            def batch(i, last):
                for q, u in steps(i, last):
                    for k in range(CH):
                        for h in range(UH):
                            if u is not None:
                                a_tile(i, u, k, h)
                            b_tile(i, q, k, h)
                        if k == 0 and q:
                            pv(i, q - 1, CH - 1)
                        if k == 1 and q:
                            if u is not None or last and q == 2:
                                turn_max(i, q + 1)
                            spread_sums(i, q - 1)
                        if k > 0:
                            pv(i, q, k - 1)
                        if k == 3 and q:
                            out_project(i, q - 1)
                pv(i, UNITS - 1, CH - 1)
                if not last:
                    turn_max(i, UNITS + 1)
                spread_sums(i, UNITS - 1)
                out_project(i, UNITS - 1)

            for u in range(2):
                for k in range(CH):
                    for h in range(UH):
                        a_tile(lo, u, k, h)
                turn_max(lo, u)
            with pe.Fori(lo, hi - 1) as i:
                batch(i, False)
            batch(hi - 1, True)

        @block.scalar
        def _(act):
            def exp(i, q, k, h):
                n = q * per + k * UH + h
                t0 = first_query(k)
                if h == 0 and (q * CH + k >= 2 or lo):
                    act.wait_ge(s["pv"], i * 16 + q * CH + k - 1)
                elif h == 0:
                    act.wait_ge(s["pv"], i * 16)
                act.wait_ge(s["b_scores"], i * 64 + n + 1)
                act.activation(g.probs[:, k % 2, h, t0:N], SB[n % 2][:, t0:N], ACT.Exp, scale=scale)\
                   .then_inc(s["exp"], 1)

            def negate(i, u):
                act.wait_ge(s["max_turned"], i * 4 + u + 1)
                act.wait_ge(s["mpart3"], i * 4 + u)
                act.activation(g.mneg[:, :], MB[0:UH, :], ACT.Copy, scale=-1.0).then_inc(s["mneg"], 1)
                act.wait_ge(s["m_stored"], (i * 4 + u) * 16)
                act.activation(g.mparts[:, 0, :], MB[0:UH, :], ACT.Copy, scale=-1.0).then_inc(s["mneg"], 1)

            def copy_out(i, q):
                act.wait_ge(s["pv"], i * 16 + 4 * q + 4)
                act.wait_ge(s["onorm"], i * 4 + q)
                act.activation(g.osum[:, :], OB[:, :], ACT.Copy).then_inc(s["o_copied"], 1)

            def batch(i, last):
                for q, u in steps(i, last):
                    for k in range(CH):
                        for h in range(UH):
                            exp(i, q, k, h)
                        if k == 0 and q:
                            copy_out(i, q - 1)
                        if k == 2 and q and (u is not None or last and q == 2):
                            negate(i, q + 1)
                copy_out(i, UNITS - 1)
                if not last:
                    negate(i, UNITS + 1)

            for u in range(2):
                negate(lo, u)
            with act.Fori(lo, hi - 1) as i:
                batch(i, False)
            batch(hi - 1, True)

        @block.gpsimd
        def _(pool):
            def split_max(i, u):
                at = i * 4 + u
                pool.wait_ge(s["mneg"], 2 * at + 2)
                pool.wait_ge(s["mpart3"], at)
                pool.tensor_tensor(g.mres[:, :], g.mneg[:, :], g.mparts[:, 0, :], ALU.subtract).then_inc(s["mres"], 1)
                pool.wait_ge(s["m_stored"], at * 16)
                pool.tensor_tensor(g.mparts[:, 1, :], g.mneg[:, :], g.mparts[:, 0, :], ALU.subtract)\
                    .then_inc(s["mpart2"], 1)
                pool.wait_ge(s["mres"], at + 1)
                pool.wait_ge(s["mpart2"], at + 1)
                pool.wait_ge(s["m_loaded"], at * 16)
                pool.tensor_tensor(g.mparts[:, 2, :], g.mres[:, :], g.mparts[:, 1, :], ALU.subtract)\
                    .then_inc(s["mpart3"], 1)

            for u in range(2):
                split_max(lo, u)
            with pool.Fori(lo, hi - 1) as i:
                for q in range(UNITS):
                    split_max(i, q + 2)
            for q in range(2):
                split_max(hi - 1, q + 2)

        @block.vector
        def _(dve):
            def maxima(i, u, k, h):
                n = u * per + k * UH + h
                width = P * (k + 1) if causal else N
                if k + h == 0 and (u >= 2 or lo):
                    dve.wait_ge(s["max_turned"], i * 4 + u - 1)
                dve.wait_ge(s["a_scores"], i * 64 + n + 1)
                dve.reduce_max(g.M[:, u % 2, k, h:h + 1], SA[n % 2][:, 0:width], AX.X).then_inc(s["a_max"], 1)

            def normalise(i, q):
                dve.wait_ge(s["sums"], i * 4 + q + 1)
                dve.wait_ge(s["onorm"], i * 4 + q)
                dve.reciprocal(g.rsum[:, :], SUMB[:, :]).then_inc(s["rsum"], 1)
                dve.wait_ge(s["rsum"], i * 4 + q + 1)
                dve.wait_ge(s["yacc"], i * 4 + q)
                dve.tensor_tensor(g.onorm[:, :], g.osum[:, :], g.rsum[:, :], ALU.mult).then_inc(s["onorm"], 1)

            def batch(i, last):
                for q, u in steps(i, last):
                    for k in range(CH):
                        if u is not None:
                            for h in range(UH):
                                maxima(i, u, k, h)
                        if k == 2 and q:
                            normalise(i, q - 1)
                normalise(i, UNITS - 1)
                dve.wait_ge(s["yacc"], i * 4 + 4)
                dve.wait_ge(s["xnew"], i)
                dve.tensor_scalar(g.ytmp[:, :], YB[:, :], g.bo[:, layer:layer + 1], g.mod[:, 2, bass.ds(i, 1)]
                                  if not isinstance(i, int) else g.mod[:, 2, i:i + 1],
                                  ALU.add, ALU.mult).then_inc(s["ytmp"], 1)
                dve.wait_ge(s["ytmp"], i + 1)
                dve.wait_ge(s["x_loaded"], i * 16 + 16)
                dve.wait_ge(s["x_stored"], i * 16)
                dve.tensor_tensor(g.xnew[:, :], g.ytmp[:, :], g.xres[:, :], ALU.add).then_inc(s["xnew"], 1)

            for u in range(2):
                for k in range(CH):
                    for h in range(UH):
                        maxima(lo, u, k, h)
            with dve.Fori(lo, hi - 1) as i:
                batch(i, False)
            batch(hi - 1, True)


def setup_experts(g):
    nc = g.nc
    g.wg = g.sb("wg", [P, E])
    g.route_c = g.sb("route_c", [P, P + 3 * E])
    g.htok = g.sb("htok", [P, NT // P, C])
    g.logits = g.sb("logits", [P, NT // P, E])
    g.gate_w = g.sb("gate_w", [P, NT // P])
    g.slot_in = g.sb("slot_in", [P, NT // P], I32)
    g.slot_out = g.sb("slot_out", [P, NT // P], I32)
    g.gs = {n: g.sem("g_" + n) for n in (
        "setup", "x_loaded", "mean", "xc", "sq", "var", "std", "rstd", "xh", "h", "turned", "htok", "lpsum", "logits",
        "vec", "counts", "zeros", "zeroed", "scattered", "gathered", "picked", "pturned", "pscaled", "x2", "x2_stored")}


    s = g.gs
    with nc.Block() as block:
        @block.gpsimd
        def _(pool):
            pool.memset(g.htok[:, :, :], 0.0).then_inc(s["zeros"], 1)

        @block.sync
        def _(sp):
            sp.wait_ge(s["zeros"], 1)
            rows = g.slots.rearrange("(p r) c -> p r c", p=P)
            n = NT // P
            sp.dma_start(rows[:, 0:n, :], g.htok[:, :, :]).then_inc(s["zeroed"], 16)
            sp.dma_start(rows[:, n:, :], g.htok[:, 0:E * CAP // P - n, :]).then_inc(s["zeroed"], 16)
            sp.wait_ge(s["zeroed"], 32)


def gate(g, x):
    nc, s = g.nc, g.gs

    with nc.Block() as block:
        @block.sync
        def _(sp):
            sp.dma_start(g.wg[:, :], g.ins["wg"]).then_inc(s["setup"], 16)
            sp.dma_start(g.route_c[:, :], g.ins["route_c"]).then_inc(s["setup"], 16)
            with sp.Fori(0, B) as it:
                sp.wait_ge(s["xc"], it)
                sp.dma_start(g.x_in[:, :], x[it]).then_inc(s["x_loaded"], 16)

        @block.tensor
        def _(pe):
            pe.wait_ge(s["setup"], 32)
            with pe.Fori(0, B) as it:
                norm_tensor(g, s, pe, it)
                pe.wait_ge(s["h"], it + 1)
                pe.wait_ge(s["htok"], it)
                for c in range(CH):
                    mm = pe.transpose(g.bank[2][:, c * P:(c + 1) * P], g.h[:, c * P:(c + 1) * P], g.ident[:, :])
                mm.then_inc(s["turned"], 1)
                pe.wait_ge(s["logits"], it)
                for c in range(CH):
                    mm = pe.matmul(g.bank[3][:, c * E:(c + 1) * E], g.h[:, c * P:(c + 1) * P], g.wg[:, :],
                                   start=(c == 0), stop=True, skip_group_check=True)
                mm.then_inc(s["lpsum"], 1)

        @block.scalar
        def _(act):
            with act.Fori(0, B) as it:
                norm_scalar(g, s, act, it)

        @block.vector
        def _(dve):
            with dve.Fori(0, B) as it:
                norm_vector(g, s, dve, it, 4, 3, "lpsum", it)
                dve.wait_ge(s["turned"], it + 1)
                dve.tensor_scalar(g.htok[:, bass.ds(it * CH, CH), :],
                                  g.bank[2][:, :].rearrange("p (c n) -> p c n", c=CH), 1.0, None, ALU.mult)\
                   .then_inc(s["htok"], 1)
                dve.wait_ge(s["lpsum"], it + 1)
                dve.tensor_scalar(g.logits[:, bass.ds(it * CH, CH), :],
                                  g.bank[3][:, 0:CH * E].rearrange("p (c n) -> p c n", c=CH), 1.0, None, ALU.mult)\
                   .then_inc(s["logits"], 1)


def norm_tensor(g, s, pe, it):
    pe.wait_ge(s["x_loaded"], it * 16 + 16)
    pe.wait_ge(s["xc"], it)
    pe.matmul(g.bank[0][:, :], g.mean_w[:, :], g.x_in[:, :], start=True, stop=True).then_inc(s["mean"], 1)
    pe.wait_ge(s["sq"], it + 1)
    pe.wait_ge(s["std"], it)
    pe.matmul(g.bank[1][:, :], g.mean_w[:, :], g.sq[:, :], start=True, stop=True).then_inc(s["var"], 1)


def norm_scalar(g, s, act, it):
    act.wait_ge(s["xc"], it + 1)
    act.wait_ge(s["var"], it)
    act.activation(g.sq[:, :], g.xc[:, :], ACT.Square).then_inc(s["sq"], 1)
    act.wait_ge(s["var"], it + 1)
    act.wait_ge(s["rstd"], it)
    act.activation(g.std[:, :], g.bank[1][:, :], ACT.Sqrt, bias=g.eps[:, 0:1]).then_inc(s["std"], 1)


def norm_vector(g, s, dve, it, scale, shift, reader, read, col=None):
    col = it if col is None else col
    dve.wait_ge(s["mean"], it + 1)
    dve.wait_ge(s["xh"], it)
    dve.wait_ge(s["sq"], it)
    dve.tensor_tensor(g.xc[:, :], g.x_in[:, :], g.bank[0][:, :], ALU.subtract).then_inc(s["xc"], 1)
    dve.wait_ge(s["std"], it + 1)
    dve.wait_ge(s["xc"], it + 1)
    dve.reciprocal(g.rstd[:, :], g.std[:, :]).then_inc(s["rstd"], 1)
    dve.wait_ge(s["rstd"], it + 1)
    dve.wait_ge(s["h"], it)
    dve.tensor_tensor(g.xh[:, :], g.xc[:, :], g.rstd[:, :], ALU.mult).then_inc(s["xh"], 1)
    dve.wait_ge(s["xh"], it + 1)
    dve.wait_ge(s[reader], read)
    if reader == "lpsum":
        dve.wait_ge(s["turned"], it)
    dve.tensor_scalar(g.h[:, :], g.xh[:, :], g.mod[:, scale, bass.ds(col, 1)], g.mod[:, shift, bass.ds(col, 1)],
                      ALU.mult, ALU.add).then_inc(s["h"], 1)


def route(g):
    nc, s = g.nc, g.gs
    T = NT // P
    big = g.xc[:, 0:T * E].rearrange("p (t e) -> p t e", e=E)
    ex = g.sq[:, 0:T * E].rearrange("p (t e) -> p t e", e=E)
    hot = g.std[:, 0:T * E].rearrange("p (t e) -> p t e", e=E)
    cum = g.xh[:, 0:T * E].rearrange("p (t e) -> p t e", e=E)
    r = g.rstd[:, 0:10 * T].rearrange("p (n t) -> p n t", n=10)
    top, den, pick, pos, keep, slot = (r[:, n, :] for n in range(6))
    tri, rev = g.route_c[:, 0:P], g.route_c[:, P:P + E]
    base, ones = g.route_c[:, P + E:P + 2 * E], g.ones_w[:, 0:T]

    def wide(col):
        return col.unsqueeze(2).broadcast_to([P, T, E])

    def rows(c):
        return c.unsqueeze(1).broadcast_to([P, T, E])

    with nc.Block() as block:
        @block.vector
        def _(dve):
            n = 0

            def step(i):
                nonlocal n
                n += 1
                i.then_inc(s["vec"], 1)
                dve.wait_ge(s["vec"], n)

            step(dve.reduce_max(top, g.logits[:, :, :], AX.X))
            step(dve.tensor_tensor(big, g.logits[:, :, :], wide(top), ALU.subtract))
            dve.wait_ge(s["sq"], B + 1)
            step(dve.reduce_sum(den, ex, AX.X))
            step(dve.reduce_max(top, ex, AX.X))
            step(dve.reciprocal(den, den))
            step(dve.tensor_tensor(g.gate_w[:, :], top, den, ALU.mult))
            step(dve.tensor_tensor(big, ex, wide(top), ALU.is_equal))
            step(dve.tensor_tensor(big, big, rows(rev), ALU.mult))
            step(dve.reduce_max(pick, big, AX.X))
            step(dve.tensor_tensor(hot, big, wide(pick), ALU.is_equal))
            dve.wait_ge(s["counts"], 1)
            step(dve.tensor_copy(big, g.bank[5][:, 0:T * E].rearrange("p (t e) -> p t e", e=E)))
            for e in range(E):
                scan = dve.tensor_tensor_scan(ex[:, :, e], ones, big[:, :, e], 0.0, ALU.mult, ALU.add)
                step(scan)
            step(dve.tensor_tensor(ex, ex, big, ALU.subtract))
            step(dve.tensor_tensor(cum, ex, g.bank[4][:, 0:T * E].rearrange("p (t e) -> p t e", e=E), ALU.add))
            step(dve.tensor_tensor(big, cum, hot, ALU.mult))
            step(dve.reduce_sum(pos, big, AX.X))
            step(dve.tensor_scalar(keep, pos, float(CAP), None, ALU.is_le))
            step(dve.tensor_tensor(g.gate_w[:, :], g.gate_w[:, :], keep, ALU.mult))
            step(dve.tensor_tensor(big, hot, rows(base), ALU.mult))
            step(dve.reduce_sum(slot, big, AX.X))
            step(dve.scalar_tensor_tensor(out=slot, in0=slot, scalar=-1.0, in1=pos, op0=ALU.add, op1=ALU.add))
            step(dve.tensor_tensor(slot, slot, keep, ALU.mult))
            step(dve.tensor_copy(g.slot_out[:, :], slot))
            step(dve.tensor_scalar(keep, keep, -float(E * CAP), float(E * CAP), ALU.mult, ALU.add))
            step(dve.tensor_tensor(slot, slot, keep, ALU.add))
            step(dve.tensor_copy(g.slot_in[:, :], slot))
            g.route_steps = n

        @block.scalar
        def _(act):
            act.wait_ge(s["vec"], 2)
            act.activation(ex, big, ACT.Exp).then_inc(s["sq"], 1)

        @block.tensor
        def _(pe):
            pe.wait_ge(s["vec"], 10)
            flat = g.std[:, 0:T * E]
            pe.matmul(g.bank[4][:, 0:T * E], tri, flat, start=True, stop=True)
            pe.matmul(g.bank[5][:, 0:T * E], g.ones_w[:, :], flat, start=True, stop=True).then_inc(s["counts"], 1)

    with nc.Block() as block:
        @block.gpsimd
        def _(pool):
            for t in range(T):
                pool.indirect_dma_start(g.slots, bass.IndirectOffsetOnAxis(ap=g.slot_in[:, t:t + 1], axis=0),
                                        g.htok[:, t, :], None, bounds_check=E * CAP - 1, oob_is_err=False)\
                    .then_inc(s["scattered"], 16)
            pool.wait_ge(s["scattered"], 16 * T)


def setup_expert_loop(g):
    g.ew1 = g.sb("ew1", [P, 2, F])
    g.ew2 = g.sb("ew2", [P, 2, F])
    g.eb1 = g.sb("eb1", [P, 2, F // P])
    g.eb2 = g.sb("eb2", [P, 2, C])
    g.eh = g.sb("eh", [P, F // P, CAP])
    g.exT = g.sb("exT", [P, CAP])
    g.es = {n: g.sem("e_" + n) for n in ("turned", "xT", "hidden", "relu", "answer", "biased", "stored")}
    g.eload = [g.sem(f"e_loaded{i}") for i in range(2)]


def experts(g):
    nc, s = g.nc, g.es
    ST = CAP // P
    HALF = CAP // 2
    xs = [g.qk[:, :, :], g.ra[:, :, :]]
    ys = [g.rb[:, :, :], g.res[:, :, :]]

    def tile(t):
        return t.rearrange("p a n -> p (a n)")[:, 0:CAP].rearrange("p (s c) -> p s c", c=C)

    with nc.Block() as block:
        @block.sync
        def _(sp):
            def load(e, par):
                sp.dma_start(g.ew1[:, par, :], g.ins["ew1"][e]).then_inc(g.eload[par], 16)
                sp.dma_start(g.ew2[:, par, :].rearrange("p (f c) -> p f c", c=C), g.ins["ew2"][e])\
                  .then_inc(g.eload[par], 16)
                sp.dma_start(g.eb1[:, par, :], g.ins["eb1"][e]).then_inc(g.eload[par], 16)
                sp.dma_start(g.eb2[:, par, :], g.ins["eb2"][e]).then_inc(g.eload[par], 16)
                sp.dma_start(tile(xs[par]), g.slots_by_expert[e]).then_inc(g.eload[par], 16)

            def two(i, last):
                for par in range(2):
                    if par == 0:
                        sp.wait_ge(s["answer"], i * 2 * ST)
                        load(i * 2 + 1, 1)
                    sp.wait_ge(s["biased"], (i * 2 + par + 1) * ST)
                    sp.dma_start(g.answers_by_expert[i * 2 + par], tile(ys[par])).then_inc(s["stored"], 16)
                    if par == 0 and not last:
                        load(i * 2 + 2, 0)

            load(0, 0)
            with sp.Fori(0, E // 2 - 1) as i:
                two(i, False)
            two(E // 2 - 1, True)
            sp.wait_ge(s["stored"], 16 * E)

        @block.tensor
        def _(pe):
            with pe.Fori(0, E // 2) as i:
                for par in range(2):
                    pe.wait_ge(g.eload[par], i * 80 + 80)
                    pe.wait_ge(s["xT"], (i * 2 + par) * 2)
                    for t in range(ST):
                        bank, col = (g.bank[0], t * P) if t < 4 else (g.bank[1], 0)
                        mm = pe.transpose(bank[:, col:col + P], tile(xs[par])[:, t, :], g.ident[:, :])
                    mm.then_inc(s["turned"], 1)
                    pe.wait_ge(s["xT"], (i * 2 + par) * 2 + 2)
                    for f in range(F // P):
                        for half in range(2):
                            n = f * 2 + half
                            pe.wait_ge(s["relu"], (i * 2 + par) * 8 + n - 3) if n >= 4 else None
                            pe.matmul(g.bank[2 + n % 4][:, 0:HALF], g.ew1[:, par, f * P:(f + 1) * P],
                                      g.exT[:, half * HALF:(half + 1) * HALF], start=True, stop=True)\
                              .then_inc(s["hidden"], 1)
                    pe.wait_ge(s["relu"], (i * 2 + par) * 8 + 8)
                    for t in range(ST):
                        if t >= 2:
                            pe.wait_ge(s["biased"], (i * 2 + par) * ST + t - 1)
                        for f in range(F // P):
                            mm = pe.matmul(g.bank[6 + t % 2][:, 0:C], g.eh[:, f, t * P:(t + 1) * P],
                                           g.ew2[:, par, f * C:(f + 1) * C], start=(f == 0), stop=(f == F // P - 1))
                        mm.then_inc(s["answer"], 1)
                    pe.wait_ge(s["biased"], (i * 2 + par + 1) * ST)

        @block.scalar
        def _(act):
            with act.Fori(0, E // 2) as i:
                for par in range(2):
                    act.wait_ge(s["answer"], (i * 2 + par) * ST)
                    for f in range(F // P):
                        for half in range(2):
                            n = f * 2 + half
                            act.wait_ge(s["hidden"], (i * 2 + par) * 8 + n + 1)
                            act.activation(g.eh[:, f, half * HALF:(half + 1) * HALF], g.bank[2 + n % 4][:, 0:HALF],
                                           ACT.Relu, bias=g.eb1[:, par, f:f + 1]).then_inc(s["relu"], 1)

        @block.vector
        def _(dve):
            with dve.Fori(0, E // 2) as i:
                for par in range(2):
                    dve.wait_ge(s["turned"], i * 2 + par + 1)
                    dve.wait_ge(s["hidden"], (i * 2 + par) * 8)
                    dve.tensor_copy(g.exT[:, 0:512], g.bank[0][:, :]).then_inc(s["xT"], 1)
                    dve.tensor_copy(g.exT[:, 512:CAP], g.bank[1][:, 0:CAP - 512]).then_inc(s["xT"], 1)
                    dve.wait_ge(s["stored"], (i * 2 + par) * 16)
                    for t in range(ST):
                        dve.wait_ge(s["answer"], (i * 2 + par) * ST + t + 1)
                        dve.tensor_tensor(tile(ys[par])[:, t, :], g.bank[6 + t % 2][:, 0:C], g.eb2[:, par, :],
                                          ALU.add).then_inc(s["biased"], 1)


def combine(g, x1, x2):
    nc, s = g.nc, g.gs
    T = NT // P
    with nc.Block() as block:
        @block.gpsimd
        def _(pool):
            for t in range(T):
                pool.indirect_dma_start(g.htok[:, t, :], None, g.answers,
                                        bass.IndirectOffsetOnAxis(ap=g.slot_out[:, t:t + 1], axis=0))\
                    .then_inc(s["gathered"], 16)
            pool.wait_ge(s["gathered"], 16 * T)
    with nc.Block() as block:
        @block.sync
        def _(sp):
            with sp.Fori(0, B) as it:
                sp.wait_ge(s["x2"], it)
                sp.dma_start(g.x_in[:, :], x1[it]).then_inc(s["x_loaded"], 16)
                sp.wait_ge(s["x2"], it + 1)
                sp.dma_start(x2[it], g.xh[:, :]).then_inc(s["x2_stored"], 16)
            sp.wait_ge(s["x2_stored"], B * 16)

        @block.vector
        def _(dve):
            with dve.Fori(0, B) as it:
                dve.wait_ge(s["pturned"], it)
                gate_w = g.gate_w[:, bass.ds(it * CH, CH)].unsqueeze(2).broadcast_to([P, CH, C])
                dve.tensor_tensor(g.xc[:, :].rearrange("p (c n) -> p c n", c=CH),
                                  g.htok[:, bass.ds(it * CH, CH), :], gate_w, ALU.mult).then_inc(s["picked"], 1)
                dve.wait_ge(s["pturned"], it + 1)
                dve.wait_ge(s["x2"], it)
                dve.tensor_scalar(g.sq[:, :], g.bank[2][:, :], g.mod[:, 5, bass.ds(it, 1)], None, ALU.mult)\
                   .then_inc(s["pscaled"], 1)
                dve.wait_ge(s["pscaled"], it + 1)
                dve.wait_ge(s["x_loaded"], (it + B) * 16 + 16)
                dve.wait_ge(s["x2_stored"], it * 16)
                dve.tensor_tensor(g.xh[:, :], g.sq[:, :], g.x_in[:, :], ALU.add).then_inc(s["x2"], 1)

        @block.tensor
        def _(pe):
            with pe.Fori(0, B) as it:
                pe.wait_ge(s["picked"], it + 1)
                pe.wait_ge(s["pscaled"], it)
                for c in range(CH):
                    mm = pe.transpose(g.bank[2][:, c * P:(c + 1) * P], g.xc[:, c * P:(c + 1) * P], g.ident[:, :])
                mm.then_inc(s["pturned"], 1)


def setup_local(g):
    nc = g.nc
    g.lw = g.sb("lw", [P, 2, 5 * INNER])
    g.lwo = g.sb("lwo", [P, 2, PAIRS, C])
    g.lw1 = g.sb("lw1", [P, 2, 2 * HID])
    g.lw2 = g.sb("lw2", [P, 2, HC, C])
    g.lcol = g.sb("lcol", [P, 2, 7 + 2 * HC])
    g.xpos = g.sb("xpos", [P, 4, N])
    g.head_ones = g.sb("head_ones", [P, P])
    g.bandf = g.sb("bandf", [P, 2, WIN])
    g.band = g.sb("band", [P, 2, WIN], BF16)
    g.xr = g.sb("l_x", [P, N])
    g.xs = g.sb("l_xs", [P, N])
    g.lsq = g.sb("l_sq", [P, 2, N])
    g.lnrm = g.sb("l_nrm", [P, 2, N])
    g.linv = g.sb("l_inv", [P, 2, N])
    g.lt1 = g.sb("l_t1", [P, 2, N])
    g.lt2 = g.sb("l_t2", [P, 2, N])
    g.lts = g.sb("l_ts", [P, 2, N])
    g.qr = g.sb("l_qr", [P, PAIRS, N])
    g.kr = g.sb("l_kr", [P, PAIRS, W + N])
    g.vt = g.sb("l_vt", [P, CH, INNER])
    g.lmx = g.sb("l_mx", [P, 4, 2])
    g.lnb = g.sb("l_nb", [P, 4, 2])
    g.lsm = g.sb("l_sm", [P, 4, 2])
    g.lrs = g.sb("l_rs", [P, 4, 2])
    g.pe_ = g.sb("l_p", [P, 2, 2, WIN])
    g.pn = g.sb("l_pn", [P, 2, 2, 2 * P])
    g.pt = g.sb("l_pt", [P, 2, 4, P])
    g.ot = g.sb("l_ot", [P, PAIRS, N])
    g.x1l = g.sb("l_x1", [P, N])
    g.s2 = g.sb("l_s2", [P, N])
    g.lxc = g.sb("l_xc", [P, N])
    g.lh = g.sb("l_h", [P, N])
    g.gl = g.sb("l_gl", [P, HC, N])
    g.hm = g.sb("l_hm", [P, HC, N])
    g.xo = g.sb("l_xo", [P, N])
    g.xf = g.sb("l_xf", [P, N])
    g.leps = g.sb("l_eps", [P, 1])
    g.ls = {n: g.sem("l_" + n) for n in (
        "setup", "vec", "x_loaded", "proj", "sq", "ssq", "nrm", "clip", "inv", "t1", "t2", "tsum", "qk", "v_psum", "v",
        "scores", "max", "nbias", "exp", "rsum", "pnorm", "turned", "pt", "pv", "o", "wo", "x1", "s2", "mean", "xc",
        "sq2", "var", "std", "rstd", "xh", "h", "mlp1", "gelu", "hidden", "y2", "x2", "final", "stored", "zero")}
    s = g.ls
    with nc.Block() as block:
        @block.sync
        def _(sp):
            for dst, src in ((g.lw[:, :, :], g.ins["lw"]), (g.lwo[:, :, :, :], g.ins["lwo"]),
                             (g.lw1[:, :, :], g.ins["lw1"]), (g.lw2[:, :, :, :], g.ins["lw2"]),
                             (g.lcol[:, :, :], g.ins["lcol"]), (g.xpos[:, :, :], g.ins["xpos"]),
                             (g.head_ones[:, :], g.ins["head_ones"]), (g.bandf[:, :, :], g.ins["band"])):
                sp.dma_start(dst, src).then_inc(s["setup"], 16)
            sp.wait_ge(s["setup"], 8 * 16)

        @block.vector
        def _(dve):
            dve.wait_ge(s["setup"], 8 * 16)
            dve.tensor_copy(g.band[:, :, :], g.bandf[:, :, :]).then_inc(s["vec"], 1)
            dve.memset(g.leps[:, :], LN_EPS)

        @block.gpsimd
        def _(pool):
            pool.memset(g.pn[:, :, :, :], 0.0)
            pool.memset(g.kr[:, :, 0:W], 0.0)
            pool.memset(g.xs[:, :], 0.0)
            pool.memset(g.s2[:, :], 0.0)


def local_input(g, x, h_out):
    nc = g.nc
    s = {n: g.sem("n_" + n) for n in ("x_loaded", "mean", "xc", "sq", "var", "std", "rstd", "xh", "h", "stored")}
    with nc.Block() as block:
        @block.sync
        def _(sp):
            with sp.Fori(0, B) as it:
                sp.wait_ge(s["xc"], it)
                sp.dma_start(g.x_in[:, :], x[it]).then_inc(s["x_loaded"], 16)
                sp.wait_ge(s["h"], it + 1)
                sp.dma_start(h_out[it], g.h[:, :]).then_inc(s["stored"], 16)
            sp.wait_ge(s["stored"], B * 16)

        @block.tensor
        def _(pe):
            with pe.Fori(0, B) as it:
                norm_tensor(g, s, pe, it)

        @block.scalar
        def _(act):
            with act.Fori(0, B) as it:
                norm_scalar(g, s, act, it)

        @block.vector
        def _(dve):
            with dve.Fori(0, B) as it:
                norm_vector(g, s, dve, it, 4, 3, "stored", it * 16, it + B)


def local_layer(g, layer, x_in, x_out, x3):
    nc, s = g.nc, g.ls
    lo, hi = B * layer, B * (layer + 1)
    NU = PAIRS * 2 * 2
    LAG_T, LAG_V = 2, 3
    bank = g.bank
    col = lambda n: g.lcol[:, layer, n:n + 1]

    def after(it, per, n):
        return it * per + max(n, 0)

    def unit(n):
        return n // 4, n // 2 % 2, n % 2

    with nc.Block() as block:
        @block.sync
        def _(sp):
            with sp.Fori(lo, hi) as it:
                sp.wait_ge(s["x1"], it)
                sp.dma_start(g.xr[:, :], x_in[it - lo]).then_inc(s["x_loaded"], 16)
                sp.wait_ge(s["v_psum"], it * CH)
                sp.dma_start(g.xs[0:C // 2, :], x_in[it - lo, 0:C // 2, :]).then_inc(s["x_loaded"], 16)
                sp.dma_start(g.xs[C // 2:C, 1:N], x_in[it - lo, C // 2:C, 0:N - 1]).then_inc(s["x_loaded"], 16)
                if layer == 1:
                    sp.wait_ge(s["final"], it - lo)
                    sp.dma_start(g.xf[:, :], x3[it - lo]).then_inc(s["x_loaded"], 16)
                    sp.wait_ge(s["final"], it - lo + 1)
                else:
                    sp.wait_ge(s["x2"], it + 1)
                sp.dma_start(x_out[it - lo], g.xo[:, :]).then_inc(s["stored"], 16)
            sp.wait_ge(s["stored"], hi * 16)

        loads = 48 if layer == 0 else 64
        base = 0 if layer == 0 else B * 48

        @block.tensor
        def _(pe):
            def project(it, n):
                w, p = n // PAIRS, n % PAIRS
                pe.wait_ge(s["t1"], after(it, 8, n - 1))
                pe.wait_ge(s["sq"], after(it, 8, n - 1))
                at = 2 * w * INNER + p * P
                pe.matmul(bank[n % 2][:, :], g.lw[:, layer, at:at + P], g.xs[:, :], start=True, stop=True)\
                  .then_inc(s["proj"], 1)
                at += INNER
                pe.wait_ge(s["t2"], after(it, 8, n - 1))
                pe.matmul(bank[2 + n % 2][:, :], g.lw[:, layer, at:at + P], g.xs[:, :], start=True, stop=True)\
                  .then_inc(s["proj"], 1)

            def sum_squares(it, n):
                pe.wait_ge(s["sq"], it * 8 + n + 1)
                pe.wait_ge(s["nrm"], after(it, 8, n - 1))
                pe.matmul(bank[4 + n % 2][:, :], g.head_ones[:, :], g.lsq[:, n % 2, :], start=True, stop=True)\
                  .then_inc(s["ssq"], 1)

            def values(it, c):
                pe.wait_ge(s["v"], after(it, CH, c - 1))
                pe.matmul(bank[6 + c % 2][:, :], g.xs[:, c * P:(c + 1) * P], g.lw[:, layer, 4 * INNER:5 * INNER],
                          start=True, stop=True).then_inc(s["v_psum"], 1)

            def scores(it, n):
                p, e, half = unit(n)
                r = slice(HD * e, HD * (e + 1))
                if n < 2:
                    pe.wait_ge(s["qk"], it * 8 + 8)
                else:
                    pe.wait_ge(s["exp"], it * NU + n - 1)
                for j in range(2):
                    t = 2 * half + j
                    out = bank[n % 2][:, WIN * j:WIN * (j + 1)]
                    pe.matmul(out, g.qr[r, p, t * P:(t + 1) * P], g.kr[r, p, t * P:t * P + WIN],
                              start=True, stop=False, skip_group_check=True)
                    mm = pe.matmul(out, g.identb[:, :], g.band[:, min(t, 1), :], start=False, stop=True,
                                   skip_group_check=True)
                mm.then_inc(s["scores"], 1)

            def turn(it, n):
                pe.wait_ge(s["pnorm"], it * NU + n + 1)
                if n < 2:
                    pe.wait_ge(s["qk"], it * 8 + 8)
                pe.wait_ge(s["pt"], after(it, NU, n - 1))
                for j in range(4):
                    mm = pe.transpose(bank[2 + n % 2][:, j * P:(j + 1) * P],
                                      g.pn[:, n % 2, j // 2, (j % 2) * P:(j % 2 + 1) * P], g.ident[:, :])
                mm.then_inc(s["turned"], 1)

            def pv(it, n):
                p, e, half = unit(n)
                pe.wait_ge(s["pt"], it * NU + n + 1)
                if n % 4 == 0:
                    pe.wait_ge(s["o"], after(it, PAIRS, p - 1))
                if n == 0:
                    pe.wait_ge(s["v"], it * CH + CH)
                ch = slice((2 * p + e) * HD, (2 * p + e + 1) * HD)
                for j in range(2):
                    t = 2 * half + j
                    out = bank[4 + p % 2][HD * e:HD * (e + 1), t * P:(t + 1) * P]
                    mm = pe.matmul(out, g.vt[:, t, ch], g.pt[:, n % 2, 2 * j + 1, :], start=True, stop=(t == 0),
                                   skip_group_check=True)
                    if t:
                        mm = pe.matmul(out, g.vt[:, t - 1, ch], g.pt[:, n % 2, 2 * j, :], start=False, stop=True,
                                       skip_group_check=True)
                mm.then_inc(s["pv"], 1)

            def out_project(it, p):
                pe.wait_ge(s["o"], it * PAIRS + p + 1)
                mm = pe.matmul(bank[7][:, :], g.lwo[:, layer, p, :], g.ot[:, p, :], start=(p == 0),
                               stop=(p == PAIRS - 1), skip_group_check=True)
                if p == PAIRS - 1:
                    mm.then_inc(s["wo"], 1)

            with pe.Fori(lo, hi) as it:
                pe.wait_ge(s["x_loaded"], (it - lo) * loads + (base + loads))
                pe.wait_ge(s["x2"], it)
                for n in range(8):
                    project(it, n)
                    if n:
                        sum_squares(it, n - 1)
                    if n % 2:
                        values(it, n // 2)
                sum_squares(it, 7)
                for n in range(NU + LAG_V):
                    if n < NU:
                        scores(it, n)
                    if 0 <= n - LAG_T < NU:
                        turn(it, n - LAG_T)
                    if n >= LAG_V:
                        pv(it, n - LAG_V)
                    if n >= LAG_V + 5 and (n - LAG_V - 5) % 4 == 0:
                        out_project(it, (n - LAG_V - 5) // 4)
                out_project(it, PAIRS - 1)
                pe.wait_ge(s["s2"], it * 2 + 2)
                pe.matmul(bank[0][:, :], g.mean_w[:, :], g.s2[:, :], start=True, stop=True).then_inc(s["mean"], 1)
                pe.wait_ge(s["sq2"], it + 1)
                pe.matmul(bank[1][:, :], g.mean_w[:, :], g.lsq[:, 0, :], start=True, stop=True).then_inc(s["var"], 1)
                pe.wait_ge(s["h"], it + 1)
                for j in range(HC):
                    w = min(P, HID - j * P)
                    for half in range(2):
                        at = half * HID + j * P
                        pe.matmul(bank[2 * j + half][0:w, :], g.lw1[:, layer, at:at + w], g.lh[:, :],
                                  start=True, stop=True).then_inc(s["mlp1"], 1)
                for j in range(HC):
                    w = min(P, HID - j * P)
                    pe.wait_ge(s["hidden"], it * HC + j + 1)
                    mm = pe.matmul(bank[7][:, :], g.lw2[0:w, layer, j, :], g.hm[0:w, j, :], start=(j == 0),
                                   stop=(j == HC - 1), skip_group_check=True)
                mm.then_inc(s["y2"], 1)

        @block.scalar
        def _(act):
            with act.Fori(lo, hi) as it:
                for n in range(9):
                    if n < 8:
                        act.wait_ge(s["proj"], it * 16 + 2 * n + 1)
                        act.wait_ge(s["ssq"], after(it, 8, n - 1))
                        act.activation(g.lsq[:, n % 2, :], bank[n % 2][:, :], ACT.Square).then_inc(s["sq"], 1)
                    if n:
                        act.wait_ge(s["ssq"], it * 8 + n)
                        act.wait_ge(s["clip"], after(it, 8, n - 2))
                        act.activation(g.lnrm[:, (n - 1) % 2, :], bank[4 + (n - 1) % 2][:, :], ACT.Sqrt)\
                           .then_inc(s["nrm"], 1)

                def exps(n):
                    act.wait_ge(s["nbias"], it * NU + n + 1)
                    act.wait_ge(s["pnorm"], after(it, NU, n - 1))
                    for j in range(2):
                        last = act.activation(g.pe_[:, n % 2, j, :], bank[n % 2][:, WIN * j:WIN * (j + 1)], ACT.Exp,
                                              bias=g.lnb[:, n % 4, j:j + 1], scale=QK_SCALE,
                                              accum_out=g.lsm[:, n % 4, j:j + 1])
                    last.then_inc(s["exp"], 1)

                def copy_pt(n):
                    act.wait_ge(s["turned"], it * NU + n + 1)
                    act.wait_ge(s["pv"], after(it, NU, n - 1))
                    act.activation(g.pt[:, n % 2, :, :], bank[2 + n % 2][:, :].rearrange("p (j n) -> p j n", j=4),
                                   ACT.Copy).then_inc(s["pt"], 1)

                def copy_o(p):
                    act.wait_ge(s["pv"], it * NU + 4 * p + 4)
                    act.wait_ge(s["wo"], it)
                    act.activation(g.ot[:, p, :], bank[4 + p % 2][:, :], ACT.Copy).then_inc(s["o"], 1)

                for n in range(NU + LAG_V):
                    if n < NU:
                        exps(n)
                    if 0 <= n - LAG_T < NU:
                        copy_pt(n - LAG_T)
                    if n >= LAG_V + 4 and (n - LAG_V - 4) % 4 == 0:
                        copy_o((n - LAG_V - 4) // 4)
                copy_o(PAIRS - 1)
                act.wait_ge(s["x1"], it + 1)
                act.wait_ge(s["mean"], it)
                act.activation(g.s2[0:C // 2, :], g.x1l[0:C // 2, :], ACT.Copy).then_inc(s["s2"], 1)
                act.activation(g.s2[C // 2:C, 1:N], g.x1l[C // 2:C, 0:N - 1], ACT.Copy).then_inc(s["s2"], 1)
                act.wait_ge(s["xc"], it + 1)
                act.activation(g.lsq[:, 0, :], g.lxc[:, :], ACT.Square).then_inc(s["sq2"], 1)
                act.wait_ge(s["var"], it + 1)
                act.activation(g.lnrm[:, 0, :], bank[1][:, :], ACT.Sqrt, bias=g.leps[:, 0:1]).then_inc(s["std"], 1)
                for j in range(HC):
                    w = min(P, HID - j * P)
                    act.wait_ge(s["mlp1"], it * 2 * HC + 2 * j + 2)
                    act.activation(g.gl[0:w, j, :], bank[2 * j + 1][0:w, :], ACT.Gelu,
                                   bias=g.lcol[0:w, layer, 7 + HC + j:8 + HC + j]).then_inc(s["gelu"], 1)

        @block.gpsimd
        def _(pool):
            with pool.Fori(lo, hi) as it:
                for n in range(8):
                    pool.wait_ge(s["t1"], it * 8 + n + 1)
                    pool.wait_ge(s["t2"], it * 8 + n + 1)
                    pool.wait_ge(s["qk"], after(it, 8, n - 1))
                    pool.tensor_tensor(g.lts[:, n % 2, :], g.lt1[:, n % 2, :], g.lt2[:, n % 2, :], ALU.add)\
                        .then_inc(s["tsum"], 1)
                for n in range(NU):
                    pool.wait_ge(s["exp"], it * NU + n + 1)
                    pool.wait_ge(s["turned"], after(it, NU, n - 1))
                    pool.wait_ge(s["rsum"], it * NU + n + 1)
                    pool.tensor_tensor(g.pn[:, n % 2, :, W:2 * P], g.pe_[:, n % 2, :, :],
                                       g.lrs[:, n % 4, :].unsqueeze(2).broadcast_to([P, 2, WIN]), ALU.mult)\
                        .then_inc(s["pnorm"], 1)

        @block.vector
        def _(dve):
            with dve.Fori(lo, hi) as it:
                def rotate(n):
                    w = n // PAIRS
                    dve.wait_ge(s["tsum"], after(it, 8, n - 1))
                    dve.wait_ge(s["sq"], it * 8 + n + 1)
                    dve.scalar_tensor_tensor(out=g.lt1[:, n % 2, :], in0=bank[n % 2][:, :], scalar=col(2 * w),
                                             in1=g.xpos[:, 2 * w, :], op0=ALU.mult, op1=ALU.mult)\
                       .then_inc(s["t1"], 1)
                    dve.wait_ge(s["proj"], it * 16 + 2 * n + 2)
                    dve.scalar_tensor_tensor(out=g.lt2[:, n % 2, :], in0=bank[2 + n % 2][:, :], scalar=col(2 * w + 1),
                                             in1=g.xpos[:, 2 * w + 1, :], op0=ALU.mult, op1=ALU.mult)\
                       .then_inc(s["t2"], 1)

                def invert(n):
                    dve.wait_ge(s["nrm"], it * 8 + n + 1)
                    dve.tensor_scalar(g.linv[:, n % 2, :], g.lnrm[:, n % 2, :], L2_EPS, None, ALU.max)\
                       .then_inc(s["clip"], 1)
                    dve.wait_ge(s["clip"], it * 8 + n + 1)
                    dve.reciprocal(g.linv[:, n % 2, :], g.linv[:, n % 2, :]).then_inc(s["inv"], 1)
                    dve.wait_ge(s["inv"], it * 8 + n + 1)
                    dve.wait_ge(s["tsum"], it * 8 + n + 1)
                    w, p = n // PAIRS, n % PAIRS
                    out = g.qr[:, p, :] if w == 0 else g.kr[:, p, W:W + N]
                    dve.tensor_tensor(out, g.lts[:, n % 2, :], g.linv[:, n % 2, :], ALU.mult).then_inc(s["qk"], 1)

                def copy_v(c):
                    dve.wait_ge(s["v_psum"], it * CH + c + 1)
                    dve.tensor_copy(g.vt[:, c, :], bank[6 + c % 2][:, :]).then_inc(s["v"], 1)

                for n in range(8):
                    rotate(n)
                    if n:
                        invert(n - 1)
                    if n % 2:
                        copy_v(n // 2)
                invert(7)

                def maxima(n):
                    dve.wait_ge(s["scores"], it * NU + n + 1)
                    dve.reduce_max(g.lmx[:, n % 4, :], bank[n % 2][:, 0:2 * WIN].rearrange("p (j n) -> p j n", j=2),
                                   AX.X).then_inc(s["max"], 1)
                    dve.wait_ge(s["max"], it * NU + n + 1)
                    dve.tensor_scalar(g.lnb[:, n % 4, :], g.lmx[:, n % 4, :], -QK_SCALE, None, ALU.mult)\
                       .then_inc(s["nbias"], 1)

                def inverse_sum(n):
                    dve.wait_ge(s["exp"], it * NU + n + 1)
                    dve.reciprocal(g.lrs[:, n % 4, :], g.lsm[:, n % 4, :]).then_inc(s["rsum"], 1)

                for n in range(NU + 1):
                    if n < NU:
                        maxima(n)
                    if n:
                        inverse_sum(n - 1)
                dve.wait_ge(s["wo"], it + 1)
                dve.tensor_tensor(g.x1l[:, :], g.xr[:, :], bank[7][:, :], ALU.add).then_inc(s["x1"], 1)
                dve.wait_ge(s["mean"], it + 1)
                dve.tensor_tensor(g.lxc[:, :], g.s2[:, :], bank[0][:, :], ALU.subtract).then_inc(s["xc"], 1)
                dve.wait_ge(s["std"], it + 1)
                dve.reciprocal(g.linv[:, 0, :], g.lnrm[:, 0, :]).then_inc(s["rstd"], 1)
                dve.wait_ge(s["rstd"], it + 1)
                dve.wait_ge(s["xc"], it + 1)
                dve.tensor_tensor(g.lt1[:, 0, :], g.lxc[:, :], g.linv[:, 0, :], ALU.mult).then_inc(s["xh"], 1)
                dve.wait_ge(s["xh"], it + 1)
                dve.tensor_scalar(g.lh[:, :], g.lt1[:, 0, :], col(4), col(5), ALU.mult, ALU.add).then_inc(s["h"], 1)
                for j in range(HC):
                    w = min(P, HID - j * P)
                    dve.wait_ge(s["gelu"], it * HC + j + 1)
                    dve.scalar_tensor_tensor(out=g.hm[0:w, j, :], in0=bank[2 * j][0:w, :],
                                             scalar=g.lcol[0:w, layer, 7 + j:8 + j], in1=g.gl[0:w, j, :],
                                             op0=ALU.add, op1=ALU.mult).then_inc(s["hidden"], 1)
                dve.wait_ge(s["y2"], it + 1)
                dve.wait_ge(s["stored"], it * 16)
                x2 = g.xo if layer == 0 else g.lxc
                dve.scalar_tensor_tensor(out=x2[:, :], in0=bank[7][:, :], scalar=col(6), in1=g.x1l[:, :],
                                         op0=ALU.add, op1=ALU.add).then_inc(s["x2"], 1)
                if layer == 1:
                    dve.wait_ge(s["x2"], it + 1)
                    dve.scalar_tensor_tensor(out=g.xo[:, :], in0=x2[:, :], scalar=g.mod[:, 5, bass.ds(it, 1)],
                                             in1=g.xf[:, :], op0=ALU.mult, op1=ALU.add).then_inc(s["final"], 1)


def build(nc, ins, out, stop=None):
    with ExitStack() as ctx:
        g = Program(nc, ctx, ins)
        g.qk_dram = g.dram("qk_dram", [2 * B, 2, UNITS, PARTS, D, UH, N], BF16)
        g.v_dram = g.dram("v_dram", [2 * B, CH, P, H * VW])
        g.m_dram = g.dram("m_dram", [UH, PARTS, N], BF16)
        x1, x2, x3, hx, hy = (g.dram(n, [B, P, N]) for n in ("x1", "x2", "x3", "hx", "hy"))
        g.slots = g.dram("slots", [E * CAP, C])
        g.answers = g.dram("answers", [E * CAP, C])
        g.slots_by_expert = g.slots.rearrange("(e s p) c -> e p s c", e=E, p=P)
        g.answers_by_expert = g.answers.rearrange("(e s p) c -> e p s c", e=E, p=P)
        setup(g)
        with g.memory():
            setup_projection(g)
            with g.memory():
                setup_attention(g)
                project(g, 0, ins["xT"])
                attend(g, 0, ins["xT"], out if stop == "att0" else x1)
            if stop == "att0":
                return
            with g.memory():
                setup_experts(g)
                gate(g, x1)
                route(g)
                setup_expert_loop(g)
                experts(g)
                combine(g, x1, out if stop == "moe" else x2)
            if stop == "moe":
                return
            with g.memory():
                setup_attention(g)
                project(g, 1, x2)
                attend(g, 1, x2, out if stop == "att1" else x3)
            if stop == "att1":
                return
            local_input(g, x3, out if stop == "h7" else hx)
            if stop == "h7":
                return
        with g.memory():
            setup_local(g)
            local_layer(g, 0, hx, hy, x3)
            local_layer(g, 1, hy, out, x3)


def heads_to_partitions(w):
    lead = w.shape[:-1]
    return np.ascontiguousarray(
        np.moveaxis(w.reshape(*lead, UNITS, UH, D), -1, -2).reshape(*lead, C))


def constants():
    i = np.arange(P)
    sel = np.zeros((P, P), np.float32)
    for h in range(UH):
        sel[VW * h + D, VW * h:VW * (h + 1)] = 1.0
    later = (i[None, :] > i[:, None])
    masks = np.stack([np.where(later, NEG, 0.0), np.where(later.T, NEG, 0.0)], 1).astype(np.float32)
    pos = np.arange(N, dtype=np.float32)
    freqs = (1.0 / np.float32(10000.0) ** (np.arange(0, D, 2, dtype=np.float32) / np.float32(D))).astype(np.float32)
    ang = (pos[:, None] * freqs[None, :]).astype(np.float32)
    cos, sin = np.cos(ang).T, np.sin(ang).T
    c8, s8 = np.concatenate([cos, -cos]), np.concatenate([sin, sin])
    rope = np.stack([heads_to_partitions(np.tile(t, (H, 1)).T).T for t in (c8, s8)], 1).astype(np.float32)
    tri = (i[:, None] <= i[None, :]).astype(np.float32)
    e = np.arange(E, dtype=np.float32)
    route_c = np.concatenate([tri, np.tile(np.concatenate([E - e, e * CAP, np.ones(E)]), (P, 1))], 1)
    half = np.arange(0, HD, 2, dtype=np.float32)
    f = 1.0 / np.float32(10000.0) ** (half / np.float32(HD))
    ang = (pos[:, None] * f[None, :]).astype(np.float32)
    ang = np.concatenate([ang, ang], -1)
    power = (pos - N // 2) / np.float32(W // 2)
    xs = ((half + np.float32(0.4 * HD)) / np.float32(1.4 * HD))[None, :] ** power[:, None]
    xs = np.concatenate([xs, xs], -1)
    sign = np.concatenate([-np.ones(HD // 2), np.ones(HD // 2)])
    tables = [np.cos(ang) * xs, np.sin(ang) * sign * xs, np.cos(ang) / xs, np.sin(ang) * sign / xs]
    xpos = np.stack([np.tile(t.T, (2, 1)) for t in tables], 1).astype(np.float32)
    j = np.arange(WIN)
    seen = (j[None, :] >= i[:, None]) & (j[None, :] <= i[:, None] + W)
    band = np.stack([np.where(seen & (j >= W)[None, :], 0.0, NEG), np.where(seen, 0.0, NEG)], 1)
    return {"route_c": route_c.astype(np.float32), "xpos": np.ascontiguousarray(xpos),
            "band": band.astype(np.float32), "head_ones": np.kron(np.eye(2), np.ones((HD, HD))).astype(np.float32),
            "ident": np.eye(P, dtype=np.float32), "mean_w": np.full((P, P), 1.0 / C, np.float32), "sel_sum": sel,
            "masks": masks, "rope": np.ascontiguousarray(rope)}


def layouts(a):
    h2p = heads_to_partitions
    turn = np.r_[D // 2:D, 0:D // 2]

    def turned(w):
        return w.reshape(*w.shape[:-1], H, D)[..., turn].reshape(w.shape)

    def heads(w):
        return np.tile(w, (1,) * (w.ndim - 1) + (H,))

    wq, wk, wv = a["L0_attn_Wq"], heads(a["L0_attn_Wk"]), heads(a["L0_attn_Wv"])
    bq, bk = a["L0_attn_bq"], heads(a["L0_attn_bk"])
    zero = np.zeros((C, C), np.float32)
    w1 = a["L1_attn_qkv_w"].T
    wqkv = np.stack([
        np.stack([h2p(wq), h2p(turned(wq)), h2p(wk), h2p(turned(wk)), wv, zero], 1),
        np.stack([h2p(w1[:, 0:C]), h2p(w1[:, C:2 * C]), w1[:, 2 * C:3 * C], zero, zero, zero], 1)], 1)
    temp = np.repeat(a["L1_attn_temperature"].reshape(H), D)
    pcol = np.stack([h2p(bq), h2p(turned(bq)), h2p(bk), h2p(turned(bk)), h2p(temp)], 1)

    def padded(w):
        out = np.zeros((UH, VW, UNITS, C), np.float32)
        out[:, 0:D] = w.reshape(UNITS, UH, D, C).transpose(1, 2, 0, 3)
        return out.reshape(P, UNITS, C)

    turn_l = np.r_[HD // 2:HD, 0:HD // 2]

    def turned_l(w):
        return w.reshape(*w.shape[:-1], 2 * PAIRS, HD)[..., turn_l].reshape(w.shape)

    def columns(w, n, width=P):
        out = np.zeros((P, 2, n), np.float32)
        for c in range(n):
            part = w[:, c * width:(c + 1) * width]
            out[:part.shape[1], :, c] = part.T
        return out

    lq = a["L1_ffn_wqkv"].transpose(1, 0, 2)
    q, k, v = lq[..., 0:INNER], lq[..., INNER:2 * INNER], lq[..., 2 * INNER:]
    qs, ks = a["L1_ffn_q_scale"], a["L1_ffn_k_scale"]
    two = lambda w: np.tile(w, (1, 2))
    b1 = a["L1_ffn_b1"]
    lcol = np.concatenate(
        [columns(two(w), 1) for w in (qs, qs[:, turn_l], ks, ks[:, turn_l])]
        + [columns(a["L1_ffn_ln_g"], 1), columns(a["L1_ffn_ln_b"], 1), columns(a["L1_ffn_b2"], 1),
           columns(b1[:, 0:HID], HC), columns(b1[:, HID:], HC)], 2)
    lw2 = np.zeros((P, 2, HC, C), np.float32)
    for c in range(HC):
        part = a["L1_ffn_w2"][:, c * P:(c + 1) * P]
        lw2[:part.shape[1], :, c] = part.transpose(1, 0, 2)
    return {
        "wg": a["L0_ffn_wg"], "ew1": a["L0_ffn_w1"],
        "ew2": a["L0_ffn_w2"].reshape(E, F // P, P, C).transpose(0, 2, 1, 3),
        "eb1": a["L0_ffn_b1"].reshape(E, F // P, P).transpose(0, 2, 1),
        "eb2": np.repeat(a["L0_ffn_b2"][:, None, :], P, 1),
        "lw": np.concatenate([q, turned_l(q), k, turned_l(k), v], 2),
        "lwo": a["L1_ffn_wo"].reshape(2, PAIRS, P, C).transpose(2, 0, 1, 3),
        "lw1": a["L1_ffn_w1"].transpose(1, 0, 2), "lw2": lw2, "lcol": lcol,
        "xT": a["L0_attn_x"].transpose(0, 2, 1),
        "cT": np.stack([a["L0_c"].T, a["L1_c"].T], 1),
        "wmod": np.stack([a["L0_wmod"], a["L1_wmod"]], 1),
        "wqkv": wqkv, "pcol": pcol, "bv": np.tile(heads(a["L0_attn_bv"]), (P, 1)),
        "wo": np.stack([padded(a["L0_attn_Wo"]), padded(a["L1_attn_proj_w"].T)], 1),
        "bo": np.stack([a["L0_attn_bo"], a["L1_attn_proj_b"]], 1),
    }


def kernel(**inputs):
    import concourse.bacc as bacc
    from concourse.bass_utils import run_bass_kernel_spmd

    nc = bacc.Bacc("TRN2", target_bir_lowering=False, num_devices=1)
    data = {k: np.asarray(v) for k, v in inputs.items()}
    arrays = {f"in_{k}": np.ascontiguousarray(v) for k, v in {**constants(), **layouts(data)}.items()}
    ins = {k[3:]: nc.dram_tensor(k, v.shape, mybir.dt.from_np(v.dtype), kind="ExternalInput").ap()
           for k, v in arrays.items()}
    out = nc.dram_tensor("out_0", (B, C, N), F32, kind="ExternalOutput").ap()
    build(nc, ins, out)
    r = run_bass_kernel_spmd(nc, [arrays], core_ids=[0])
    return np.ascontiguousarray(r.results[0]["out_0"].transpose(0, 2, 1))
```

```python
import math
from contextlib import ExitStack, contextmanager

import numpy as np

import concourse.bass as bass
from concourse import mybir

F32 = mybir.dt.float32
BF16 = mybir.dt.bfloat16
I32 = mybir.dt.int32
ALU = mybir.AluOpType
ACT = mybir.ActivationFunctionType
AX = mybir.AxisListType

P = 128
B, N, C = 8, 512, 128
NT = B * N
H, D = 16, 8
UNITS = 4
UH = H // UNITS
CH = N // P
PARTS = 3
TERMS = PARTS * PARTS
RK = TERMS * D
RM = RK + PARTS
VW = 32
NEG = -1.0e30
E, F = 8, 512
CAP = NT * 5 // 4 // E
PAIRS, HD = 4, 64
INNER = 2 * PAIRS * HD
W = 64
WIN = W + P
HID = C * 4 * 2 // 3
HC = -(-HID // P)
QK_SCALE = 8.0
LN_EPS = 1e-5
L2_EPS = 1e-12
L2_RANGE = 2.0 ** 17


class Program:

    def __init__(self, nc, ctx, ins):
        self.nc, self.ctx, self.ins, self.sems = nc, ctx, ins, {}
        self.held = [ctx]
        self.attention_setups = 0
        self.count = 0

    def sb(self, name, shape, dt=F32):
        self.count += 1
        return self.held[-1].enter_context(self.nc.sbuf_tensor(f"{name}_sb{self.count}", shape, dt))

    @contextmanager
    def memory(self):
        with ExitStack() as held:
            self.held.append(held)
            yield
            self.held.pop()

    def sem(self, name):
        if name not in self.sems:
            self.sems[name] = self.ctx.enter_context(self.nc.semaphore(name))
        return self.sems[name]

    def dram(self, name, shape, dt=F32):
        return self.nc.dram_tensor(name, shape, dt, kind="Internal").ap()


def setup(g):
    nc, ins = g.nc, g.ins
    g.bank = [g.ctx.enter_context(nc.psum_tensor(f"bank{i}", [P, 512], F32)) for i in range(8)]
    g.ident = g.sb("ident", [P, P])
    g.identb = g.sb("identb", [P, P], BF16)
    g.mean_w = g.sb("mean_w", [P, P])
    g.sel_sum = g.sb("sel_sum", [P, P])
    g.maskf = g.sb("maskf", [P, 2, P])
    g.mask = g.sb("mask", [P, 2, P], BF16)
    g.mod = g.sb("mod", [P, 6, 2 * B])
    cT = g.sb("cT", [P, 2, B])
    sil = g.sb("sil", [P, 2, B])
    tmp = g.sb("mod_tmp", [P, 4, 2 * B])
    wmod = g.sb("wmod", [P, 2, 6 * C])
    ld, prod = g.sem("setup_loaded"), g.sem("mod_products")
    v, ex = g.sem("setup_vector"), g.sem("exp_of_c")
    with nc.Block() as block:
        @block.sync
        def _(sp):
            for dst, src in ((g.ident[:, :], ins["ident"]), (g.mean_w[:, :], ins["mean_w"]),
                             (g.sel_sum[:, :], ins["sel_sum"]), (g.maskf[:, :, :], ins["masks"]),
                             (cT[:, :, :], ins["cT"]), (wmod[:, :, :], ins["wmod"])):
                sp.dma_start(dst, src).then_inc(ld, 16)

        @block.scalar
        def _(act):
            act.wait_ge(ld, 96)
            act.activation(sil[:, :, :], cT[:, :, :], ACT.Exp, scale=-1.0).then_inc(ex, 1)

        @block.tensor
        def _(pe):
            pe.wait_ge(ld, 96)
            pe.wait_ge(v, 5)
            for layer in range(2):
                for j in range(6):
                    at = 16 * j + 8 * layer
                    mm = pe.matmul(g.bank[0][:, at:at + B], wmod[:, layer, j * C:(j + 1) * C],
                                   sil[:, layer, :], start=(layer + j == 0), stop=True, skip_group_check=True)
            mm.then_inc(prod, 1)

        @block.vector
        def _(dve):
            n = 0

            def step(ins_):
                nonlocal n
                n += 1
                ins_.then_inc(v, 1)
                dve.wait_ge(v, n)

            dve.wait_ge(ld, 96)
            step(dve.tensor_copy(g.identb[:, :], g.ident[:, :]))
            step(dve.tensor_copy(g.mask[:, :, :], g.maskf[:, :, :]))
            dve.wait_ge(ex, 1)
            step(dve.tensor_scalar(sil[:, :, :], sil[:, :, :], 1.0, None, ALU.add))
            step(dve.reciprocal(sil[:, :, :], sil[:, :, :]))
            step(dve.tensor_tensor(sil[:, :, :], sil[:, :, :], cT[:, :, :], ALU.mult))
            dve.wait_ge(prod, 1)
            step(dve.tensor_copy(g.mod[:, :, :], g.bank[0][:, 0:96].rearrange("p (j b) -> p j b", j=6)))
            for j in (1, 4):
                step(dve.tensor_scalar(g.mod[:, j, :], g.mod[:, j, :], 1.0, None, ALU.add))
            for j in (2, 5):
                step(dve.tensor_scalar(tmp[:, 0, :], g.mod[:, j, :], 0.0, 2.0, ALU.is_ge, ALU.mult))
                step(dve.tensor_scalar(tmp[:, 1, :], tmp[:, 0, :], -1.0, None, ALU.add))
                step(dve.scalar_tensor_tensor(out=tmp[:, 2, :], in0=g.mod[:, j, :], scalar=-1.0, in1=g.mod[:, j, :],
                                              op0=ALU.mult, op1=ALU.max))
                step(dve.scalar_tensor_tensor(out=g.mod[:, j, :], in0=tmp[:, 2, :], scalar=0.25, in1=tmp[:, 1, :],
                                              op0=ALU.max, op1=ALU.mult))


def setup_projection(g):
    nc = g.nc
    g.wq = g.sb("wq", [P, 2, 6, C])
    g.pcol = g.sb("pcol", [P, 6])
    g.rope = g.sb("rope", [P, 2, N])
    g.bv = g.sb("bv", [P, C])
    g.ones_w = g.sb("ones_w", [P, P])
    g.x_in = g.sb("x_in", [P, N])
    g.xc = g.sb("xc", [P, N])
    g.sq = g.sb("sq", [P, N])
    g.std = g.sb("std", [P, N])
    g.rstd = g.sb("rstd", [P, N])
    g.eps = g.sb("eps", [P, 2])
    g.xh = g.sb("xh", [P, N])
    g.h = g.sb("h", [P, N])
    g.ra = g.sb("ra", [P, 2, N])
    g.rb = g.sb("rb", [P, 2, N])
    g.qk = g.sb("qk", [P, 2, N])
    g.res = g.sb("res", [P, 2, N])
    g.res2 = g.sb("norms", [P, 2, N])
    g.inv = g.sb("inv", [P, 2, N])
    g.parts = g.sb("parts", [P, 2, PARTS, N], BF16)
    g.vpad = g.sb("vpad", [P, CH, H, VW])
    g.ps = {n: g.sem("p_" + n) for n in (
        "setup", "setup_dve", "x_loaded", "mean", "xc", "sq", "var", "std", "rstd", "xh", "h", "qk_psum", "v_psum", "ra",
        "rb", "rot", "sumsq", "sumsq_psum", "norm", "part1", "res1", "part2", "part3", "parts_stored", "v_stored", "v_padded")}
    s = g.ps
    with nc.Block() as block:
        @block.sync
        def _(sp):
            for dst, src in ((g.wq[:, :, :, :], g.ins["wqkv"]), (g.pcol[:, 0:5], g.ins["pcol"]),
                             (g.rope[:, :, :], g.ins["rope"]), (g.bv[:, :], g.ins["bv"])):
                sp.dma_start(dst, src).then_inc(s["setup"], 16)

        @block.gpsimd
        def _(pool):
            pool.memset(g.ones_w[:, :], 1.0)
            pool.memset(g.eps[:, 0:1], LN_EPS)
            pool.memset(g.eps[:, 1:2], 0.5 * math.log(L2_RANGE))
            pool.memset(g.vpad[:, :, :, :], 0.0).then_inc(s["v_padded"], 1)
            pool.wait_ge(s["v_padded"], 1)
            pool.memset(g.vpad[:, :, :, D:D + 1], 1.0)

        @block.vector
        def _(dve):
            dve.wait_ge(s["setup"], 64)
            dve.reciprocal(g.pcol[:, 5:6], g.pcol[:, 4:5]).then_inc(s["setup_dve"], 1)
            dve.wait_ge(s["setup_dve"], 1)
            dve.tensor_scalar(g.pcol[:, 5:6], g.pcol[:, 5:6], 1.0 / D, None, ALU.mult)


def project(g, layer, x):
    nc, s = g.nc, g.ps
    lo, hi = B * layer, B * (layer + 1)
    nmm = 4 if layer == 0 else 2

    with nc.Block() as block:
        @block.sync
        def _(sp):
            def batch(it, last):
                if not last:
                    sp.wait_ge(s["xc"], it + 1)
                    sp.dma_start(g.x_in[:, :], x[it + 1 - lo]).then_inc(s["x_loaded"], 16)
                for w in range(2):
                    sp.wait_ge(s["part3"], it * 2 + w + 1)
                    for part in range(PARTS):
                        sp.dma_start(g.qk_dram[it, w, :, part].rearrange("u d h n -> u (d h) n"),
                                     g.parts[:, w, part, :]).then_inc(s["parts_stored"], 16)
                sp.wait_ge(s["v_stored"], it * 17 + 1)
                sp.dma_start(g.v_dram[it].rearrange("c p m -> p c m"),
                             g.vpad[:, :, :, :].rearrange("p c h w -> p c (h w)")).then_inc(s["v_stored"], 16)

            sp.dma_start(g.x_in[:, :], x[0]).then_inc(s["x_loaded"], 16)
            with sp.Fori(lo, hi - 1) as it:
                batch(it, False)
            batch(hi - 1, True)
            sp.wait_ge(s["parts_stored"], hi * 2 * PARTS * 16)
            sp.wait_ge(s["v_stored"], hi * 17)

        @block.tensor
        def _(pe):
            with pe.Fori(lo, hi) as it:
                pe.wait_ge(s["x_loaded"], it * 16 + 16)
                pe.wait_ge(s["xc"], it)
                pe.matmul(g.bank[0][:, :], g.mean_w[:, :], g.x_in[:, :], start=True, stop=True).then_inc(s["mean"], 1)
                pe.wait_ge(s["sq"], it + 1)
                pe.wait_ge(s["std"], it)
                pe.matmul(g.bank[1][:, :], g.mean_w[:, :], g.sq[:, :], start=True, stop=True).then_inc(s["var"], 1)
                pe.wait_ge(s["h"], it + 1)
                if layer == 0:
                    for m in range(4):
                        w = m // 2
                        done = s["ra"] if m % 2 == 0 else s["rb"]
                        pe.wait_ge(done, it * 2)
                        pe.matmul(g.bank[2 + m][:, :], g.wq[:, 0, m, :], g.h[:, :],
                                  start=True, stop=True).then_inc(s["qk_psum"], 1)
                else:
                    for m in range(2):
                        pe.wait_ge(s["rot"], it * 2)
                        pe.matmul(g.bank[2 + m][:, :], g.wq[:, 1, m, :], g.h[:, :],
                                  start=True, stop=True).then_inc(s["qk_psum"], 2)
                pe.wait_ge(s["v_stored"], it * 17)
                for c in range(CH):
                    mm = pe.matmul(g.bank[6][:, c * C:(c + 1) * C], g.h[:, c * P:(c + 1) * P],
                                   g.wq[:, layer, 4 if layer == 0 else 2, :], start=(c == 0), stop=True,
                                   skip_group_check=True)
                mm.then_inc(s["v_psum"], 1)
                if layer == 1:
                    for w in range(2):
                        pe.wait_ge(s["sumsq"], (it - lo) * 2 + w + 1)
                        pe.wait_ge(s["rb"], it * 2)
                        pe.matmul(g.bank[4 + w][:, :], g.ones_w[:, :], g.ra[:, w, :],
                                  start=True, stop=True).then_inc(s["sumsq_psum"], 1)

        @block.scalar
        def _(act):
            with act.Fori(lo, hi) as it:
                act.wait_ge(s["xc"], it + 1)
                act.wait_ge(s["var"], it)
                act.activation(g.sq[:, :], g.xc[:, :], ACT.Square).then_inc(s["sq"], 1)
                act.wait_ge(s["var"], it + 1)
                act.activation(g.std[:, :], g.bank[1][:, :], ACT.Ln, bias=g.eps[:, 0:1]).then_inc(s["std"], 1)
                act.wait_ge(s["std"], it + 1)
                act.wait_ge(s["xh"], it)
                act.activation(g.rstd[:, :], g.std[:, :], ACT.Exp, scale=-0.5).then_inc(s["rstd"], 1)
                if layer == 1:
                    for w in range(2):
                        act.wait_ge(s["qk_psum"], it * 4 + 2 * w + 2)
                        act.wait_ge(s["sumsq_psum"], (it - lo) * 2 + w)
                        act.activation(g.ra[:, w, :], g.bank[2 + w][:, :], ACT.Square).then_inc(s["sumsq"], 1)
                    for w in range(2):
                        act.wait_ge(s["rb"], it * 2 + w + 1)
                        act.activation(g.rb[:, w, :], g.res2[:, w, :], ACT.Ln, scale=L2_RANGE).then_inc(s["norm"], 1)
                        act.wait_ge(s["norm"], ((it - lo) * 2 + w) * 2 + 1)
                        act.wait_ge(s["rot"], it * 2 + w)
                        act.activation(g.inv[:, w, :], g.rb[:, w, :], ACT.Exp, scale=-0.5, bias=g.eps[:, 1:2])\
                           .then_inc(s["norm"], 1)
                for w in range(2):
                    act.wait_ge(s["rot"], it * 2 + w + 1)
                    act.wait_ge(s["parts_stored"], it * 2 * PARTS * 16)
                    act.activation(g.parts[:, w, 0, :], g.qk[:, w, :], ACT.Copy).then_inc(s["part1"], 1)

        @block.gpsimd
        def _(pool):
            with pool.Fori(lo, hi) as it:
                for w in range(2):
                    pool.wait_ge(s["part1"], it * 2 + w + 1)
                    pool.wait_ge(s["part3"], it * 2 + w)
                    pool.tensor_tensor(g.res[:, w, :], g.qk[:, w, :], g.parts[:, w, 0, :],
                                       ALU.subtract).then_inc(s["res1"], 1)
                    pool.tensor_tensor(g.parts[:, w, 1, :], g.qk[:, w, :], g.parts[:, w, 0, :],
                                       ALU.subtract).then_inc(s["part2"], 1)
                    pool.wait_ge(s["res1"], it * 2 + w + 1)
                    pool.wait_ge(s["part2"], it * 2 + w + 1)
                    pool.tensor_tensor(g.parts[:, w, 2, :], g.res[:, w, :], g.parts[:, w, 1, :],
                                       ALU.subtract).then_inc(s["part3"], 1)

        @block.vector
        def _(dve):
            with dve.Fori(lo, hi) as it:
                dve.wait_ge(s["mean"], it + 1)
                dve.wait_ge(s["xh"], it)
                dve.wait_ge(s["sq"], it)
                dve.tensor_tensor(g.xc[:, :], g.x_in[:, :], g.bank[0][:, :], ALU.subtract).then_inc(s["xc"], 1)
                dve.wait_ge(s["rstd"], it + 1)
                dve.wait_ge(s["xc"], it + 1)
                dve.wait_ge(s["h"], it)
                dve.tensor_tensor(g.xh[:, :], g.xc[:, :], g.rstd[:, :], ALU.mult).then_inc(s["xh"], 1)
                dve.wait_ge(s["xh"], it + 1)
                dve.wait_ge(s["v_psum"], it)
                dve.tensor_scalar(g.h[:, :], g.xh[:, :], g.mod[:, 1, bass.ds(it, 1)], g.mod[:, 0, bass.ds(it, 1)],
                                  ALU.mult, ALU.add).then_inc(s["h"], 1)
                for w in range(2):
                    if layer == 0:
                        dve.wait_ge(s["part3"], it * 2 + w)
                        dve.wait_ge(s["qk_psum"], it * 4 + 2 * w + 1)
                        dve.wait_ge(s["rot"], it * 2 + w)
                        dve.scalar_tensor_tensor(out=g.ra[:, w, :], in0=g.bank[2 + 2 * w][:, :],
                                                 scalar=g.pcol[:, 2 * w:2 * w + 1], in1=g.rope[:, 0, :],
                                                 op0=ALU.add, op1=ALU.mult).then_inc(s["ra"], 1)
                        dve.wait_ge(s["qk_psum"], it * 4 + 2 * w + 2)
                        dve.scalar_tensor_tensor(out=g.rb[:, w, :], in0=g.bank[3 + 2 * w][:, :],
                                                 scalar=g.pcol[:, 2 * w + 1:2 * w + 2], in1=g.rope[:, 1, :],
                                                 op0=ALU.add, op1=ALU.mult).then_inc(s["rb"], 1)
                        dve.wait_ge(s["ra"], it * 2 + w + 1)
                        dve.wait_ge(s["rb"], it * 2 + w + 1)
                        dve.tensor_tensor(g.qk[:, w, :], g.ra[:, w, :], g.rb[:, w, :], ALU.add).then_inc(s["rot"], 1)
                    else:
                        dve.wait_ge(s["sumsq_psum"], (it - lo) * 2 + w + 1)
                        dve.wait_ge(s["norm"], (it - lo) * 4)
                        dve.tensor_scalar(g.res2[:, w, :], g.bank[4 + w][:, :], L2_EPS * L2_EPS, None, ALU.max)\
                           .then_inc(s["rb"], 1)
                if layer == 1:
                    for w in range(2):
                        dve.wait_ge(s["norm"], ((it - lo) * 2 + w) * 2 + 2)
                        dve.wait_ge(s["part3"], it * 2 + w)
                        dve.scalar_tensor_tensor(out=g.qk[:, w, :], in0=g.bank[2 + w][:, :],
                                                 scalar=g.pcol[:, 5:6] if w == 0 else 1.0, in1=g.inv[:, w, :],
                                                 op0=ALU.mult, op1=ALU.mult).then_inc(s["rot"], 1)
                dve.wait_ge(s["v_psum"], it + 1)
                dve.wait_ge(s["v_stored"], it * 17)
                psum = g.bank[6][:, :].rearrange("p (c h d) -> p c h d", c=CH, d=D)
                out = g.vpad[:, :, :, 0:D]
                if layer == 0:
                    bv = g.bv[:, :].rearrange("p (h d) -> p h d", d=D)
                    for c in range(CH):
                        last = dve.tensor_tensor(out[:, c], psum[:, c], bv, ALU.add)
                else:
                    last = dve.tensor_copy(out, psum)
                last.then_inc(s["v_stored"], 1)


def setup_attention(g):
    nc = g.nc
    g.Q = g.sb("Q", [RM, UNITS, UH, N], BF16)
    g.K = g.sb("K", [RM, UNITS, UH, N], BF16)
    g.V = g.sb("V", [P, UNITS, CH, UH * VW])
    g.wo = g.sb("wo", [P, 2, UNITS, C])
    g.bo = g.sb("bo", [P, 2])
    g.M = g.sb("M", [P, 2, CH, UH])
    g.mneg = g.sb("mneg", [UH, N])
    g.mres = g.sb("mres", [UH, N])
    g.mparts = g.sb("mparts", [UH, PARTS, N], BF16)
    g.probs = g.sb("probs", [P, 2, UH, N])
    g.osum = g.sb("osum", [P, N])
    g.lsum = g.sb("lsum", [P, N])
    g.rsum = g.sb("rsum", [P, N])
    g.scheck = g.sb("scheck", [P, N])
    g.oscaled = g.sb("oscaled", [P, N])
    g.onorm = g.sb("onorm", [P, N])
    g.xres = g.sb("xres", [P, N])
    g.ytmp = g.sb("ytmp", [P, N])
    g.xnew = g.sb("xnew", [P, N])
    g.as_ = {n: g.sem("a_" + n) for n in (
        "setup", "k_ones", "a_scores", "a_max", "max_turned", "mneg", "mpart1", "mres", "mpart2", "mpart3", "m_stored",
        "m_loaded", "b_scores", "exp", "pv", "o_copied", "sums", "ln_sum", "rsum", "check", "scaled", "onorm", "yacc", "x_loaded", "ytmp", "xnew",
        "x_stored")}
    g.loaded = [g.sem(f"a_loaded{i}") for i in range(UNITS)]
    g.attention_setups += 1
    n_setup = g.attention_setups
    with nc.Block() as block:
        @block.sync
        def _(sp):
            sp.dma_start(g.wo[:, :, :, :], g.ins["wo"]).then_inc(g.as_["setup"], 16)
            sp.dma_start(g.bo[:, :], g.ins["bo"]).then_inc(g.as_["setup"], 16)
            sp.wait_ge(g.as_["setup"], 32 * n_setup)

        @block.gpsimd
        def _(pool):
            pool.memset(g.K[64:RM, :, :, :], 1.0)


def attend(g, layer, x, x_out):
    nc, s = g.nc, g.as_
    causal = layer == 0
    lo, hi = B * layer, B * (layer + 1)
    per = CH * UH
    scale = float(D) ** -0.5 if causal else 1.0
    SA, SB, OB, MB, YB = g.bank[0:3], g.bank[3:5], g.bank[5], g.bank[6], g.bank[7]
    SUMB = MB
    hk = (lambda h: 0) if causal else (lambda h: h)
    LOADS = 13 * 16

    def first_query(k):
        return P * k if causal else 0

    def batches(engine, batch):
        batch(lo, True, False)
        with engine.Fori(lo + 1, hi - 1) as i:
            batch(i, False, False)
        batch(hi - 1, False, True)

    def a_unit(q, last):
        return q + 2 if not (last and q >= 2) else None

    def m_unit(q, first, last):
        return q + 1 if not (first and q == 0) and not (last and q == UNITS - 1) else None

    with nc.Block() as block:
        @block.sync
        def _(sp):
            def load(i, u):
                it, q = (i, u) if u < UNITS else (i + 1, u - UNITS)
                slot = q
                for part in range(PARTS):
                    src = g.qk_dram[it, 0, q, part].rearrange("d h n -> d (h n)")
                    for t in range(PARTS):
                        r = (PARTS * part + t) * D
                        sp.dma_start(g.Q[r:r + D, slot, :, :].rearrange("d h n -> d (h n)"), src)\
                          .then_inc(g.loaded[slot], 16)
                    src = g.qk_dram[it, 1, q].rearrange("s d h n -> (s d) h n")
                    r = PARTS * part * D
                    if causal:
                        sp.dma_start(g.K[r:r + PARTS * D, slot, 0, :], src[:, 0, :]).then_inc(g.loaded[slot], 16)
                    else:
                        sp.dma_start(g.K[r:r + PARTS * D, slot, :, :], src).then_inc(g.loaded[slot], 16)
                sp.dma_start(g.V[:, slot, :, :], g.v_dram[it].rearrange(
                    "c p (u m) -> p c u m", u=UNITS)[:, :, q, :]).then_inc(g.loaded[slot], 16)

            def move_max(i, u):
                at = i * 4 + u
                sp.wait_ge(s["mpart3"], at + 1)
                sp.dma_start(g.m_dram, g.mparts[:, :, :]).then_inc(s["m_stored"], 16)
                sp.wait_ge(s["m_stored"], at * 16 + 16)
                sp.dma_start(g.Q[RK:RM, u % UNITS, :, :], g.m_dram.rearrange("h s n -> s h n"))\
                    .then_inc(s["m_loaded"], 16)

            def store(i):
                sp.wait_ge(s["xnew"], i)
                sp.dma_start(x_out[i - lo - 1], g.xnew[:, :]).then_inc(s["x_stored"], 16)

            def batch(i, first, last):
                for q in range(UNITS):
                    if not last or q == 0:
                        if not (first and q == 0):
                            sp.wait_ge(s["pv"], i * 16 + 4 * q)
                        load(i, q + 3)
                    u = m_unit(q, first, last)
                    if u is not None:
                        move_max(i, u)
                    if q == 2:
                        if not first:
                            store(i)
                        sp.dma_start(g.xres[:, :], x[i - lo]).then_inc(s["x_loaded"], 16)

            for u in range(3):
                load(lo, u)
            for u in range(2):
                move_max(lo, u)
            batches(sp, batch)
            store(hi)
            sp.wait_ge(s["x_stored"], hi * 16)

        @block.tensor
        def _(pe):
            def a_tile(i, u, k, h):
                n = u * per + k * UH + h
                slot, ring = u % UNITS, n % (UNITS * per)
                out = SA[ring % 3]
                width = P * (k + 1) if causal else N
                if k + h == 0:
                    pe.wait_ge(g.loaded[slot], (i + u // UNITS) * LOADS + LOADS)
                if ring >= 3:
                    pe.wait_ge(s["a_max"], i * 64 + n - 2)
                elif ring == 0 and (u or lo):
                    pe.wait_ge(s["a_max"], i * 64 + n)
                mm = pe.matmul(out[:, 0:width], g.Q[0:RK, slot, h, k * P:(k + 1) * P],
                               g.K[0:RK, slot, hk(h), 0:width], start=True, stop=not causal)
                if causal:
                    mm = pe.matmul(out[:, width - P:width], g.identb[:, :], g.mask[:, 0, :], start=False, stop=True)
                mm.then_inc(s["a_scores"], 1)

            def turn_max(i, u):
                pe.wait_ge(s["a_max"], i * 64 + (u + 1) * per)
                pe.wait_ge(s["mneg"], 2 * (i * 4 + u))
                if u >= 2:
                    pe.wait_ge(s["check"], i * 4 + u - 2)
                for k in range(CH):
                    mm = pe.transpose(MB[0:UH, k * P:(k + 1) * P], g.M[:, u % 2, k, :], g.ident[:, :])
                mm.then_inc(s["max_turned"], 1)

            def b_tile(i, q, k, h):
                n = q * per + k * UH + h
                t0 = first_query(k)
                if k + h == 0:
                    pe.wait_ge(s["m_loaded"], i * 64 + 16 * q + 16)
                if n >= 2 or not isinstance(i, int) or i:
                    pe.wait_ge(s["exp"], i * 64 + n - 1)
                mm = pe.matmul(SB[n % 2][:, t0:N], g.K[0:RM, q, hk(h), k * P:(k + 1) * P],
                               g.Q[0:RM, q, h, t0:N], start=True, stop=not causal)
                if causal:
                    mm = pe.matmul(SB[n % 2][:, t0:t0 + P], g.identb[:, :], g.mask[:, 1, :], start=False, stop=True)
                mm.then_inc(s["b_scores"], 1)

            def pv(i, q, k):
                t0 = first_query(k)
                slot = q % UNITS
                pe.wait_ge(s["exp"], i * 64 + q * per + (k + 1) * UH)
                if k == 0:
                    pe.wait_ge(s["o_copied"], i * 4 + q)
                for h in range(UH):
                    mm = pe.matmul(OB[VW * h:VW * (h + 1), t0:N], g.V[:, slot, k, VW * h:VW * (h + 1)],
                                   g.probs[:, k % 2, h, t0:N], start=(k == 0), stop=(k == CH - 1),
                                   skip_group_check=True)
                mm.then_inc(s["pv"], 1)

            def spread_sums(i, q, m):
                pe.wait_ge(s["o_copied"], i * 4 + q + 1)
                pe.wait_ge(s["check"], i * 4 + q)
                if m is not None:
                    pe.wait_ge(s["mneg"], 2 * (i * 4 + m + 1))
                pe.matmul(SUMB[:, :], g.sel_sum[:, :], g.osum[:, :], start=True, stop=True).then_inc(s["sums"], 1)

            def out_project(i, q):
                w = q % UNITS
                pe.wait_ge(s["onorm"], i * 4 + q + 1)
                if w == 0:
                    pe.wait_ge(s["ytmp"], i)
                pe.matmul(YB[:, :], g.wo[:, layer, w, :], g.onorm[:, :], start=(w == 0), stop=(w == UNITS - 1),
                          skip_group_check=True).then_inc(s["yacc"], 1)

            def batch(i, first, last):
                for q in range(UNITS):
                    u, m = a_unit(q, last), m_unit(q, first, last)
                    for k in range(CH):
                        for h in range(UH):
                            if u is not None:
                                a_tile(i, u, k, h)
                            b_tile(i, q, k, h)
                            if h == 1 and k:
                                pv(i, q, k - 1)
                            elif h == 1 and not (first and q == 0):
                                pv(i, q - 1, CH - 1)
                            if (k, h) == (0, 2) and m is not None:
                                turn_max(i, m)
                            if (k, h) == (0, 3) and not (first and q < 2):
                                out_project(i, q - 2)
                            if (k, h) == (2, 0) and not (first and q == 0):
                                spread_sums(i, q - 1, m)

            for u in range(2):
                for k in range(CH):
                    for h in range(UH):
                        a_tile(lo, u, k, h)
                turn_max(lo, u)
            batches(pe, batch)
            pv(hi, -1, CH - 1)
            out_project(hi, -2)
            spread_sums(hi, -1, None)
            out_project(hi, -1)

        @block.scalar
        def _(act):
            def exp(i, q, k, h):
                n = q * per + k * UH + h
                t0 = first_query(k)
                if h == 0 and (q * CH + k >= 2 or not isinstance(i, int) or i):
                    act.wait_ge(s["pv"], i * 16 + q * CH + k - 1)
                act.wait_ge(s["b_scores"], i * 64 + n + 1)
                act.activation(g.probs[:, k % 2, h, t0:N], SB[n % 2][:, t0:N], ACT.Exp, scale=scale)\
                   .then_inc(s["exp"], 1)

            def negate(i, u):
                act.wait_ge(s["max_turned"], i * 4 + u + 1)
                act.wait_ge(s["mpart3"], i * 4 + u)
                act.activation(g.mneg[:, :], MB[0:UH, :], ACT.Copy, scale=-1.0).then_inc(s["mneg"], 1)

            def first_part(i, u):
                act.wait_ge(s["max_turned"], i * 4 + u + 1)
                act.wait_ge(s["m_stored"], (i * 4 + u) * 16)
                act.activation(g.mparts[:, 0, :], MB[0:UH, :], ACT.Copy, scale=-1.0).then_inc(s["mneg"], 1)

            def copy_out(i, q):
                act.wait_ge(s["pv"], i * 16 + 4 * q + 4)
                act.wait_ge(s["scaled"], i * 4 + q)
                act.wait_ge(s["sums"], i * 4 + q)
                act.activation(g.osum[:, :], OB[:, :], ACT.Copy).then_inc(s["o_copied"], 1)

            def ln_sums(i, q):
                act.wait_ge(s["sums"], i * 4 + q + 1)
                act.wait_ge(s["rsum"], i * 4 + q)
                act.activation(g.lsum[:, :], SUMB[:, :], ACT.Ln, scale=-1.0).then_inc(s["ln_sum"], 1)

            def exp_sums(i, q):
                act.wait_ge(s["ln_sum"], i * 4 + q + 1)
                act.wait_ge(s["check"], i * 4 + q)
                act.wait_ge(s["scaled"], i * 4 + q)
                act.activation(g.rsum[:, :], g.lsum[:, :], ACT.Exp, scale=-1.0).then_inc(s["rsum"], 1)

            def batch(i, first, last):
                for q in range(UNITS):
                    m = m_unit(q, first, last)
                    for k in range(CH):
                        for h in range(UH):
                            exp(i, q, k, h)
                            if not (first and q == 0):
                                if (k, h) == (0, 3):
                                    copy_out(i, q - 1)
                                if (k, h) == (2, 2):
                                    ln_sums(i, q - 1)
                                if (k, h) == (3, 0):
                                    exp_sums(i, q - 1)
                            if m is not None:
                                if (k, h) == (1, 0):
                                    negate(i, m)
                                if (k, h) == (1, 1):
                                    first_part(i, m)

            for u in range(2):
                negate(lo, u)
                first_part(lo, u)
            batches(act, batch)
            copy_out(hi, -1)
            ln_sums(hi, -1)
            exp_sums(hi, -1)

        @block.gpsimd
        def _(pool):
            def split_max(i, u):
                at = i * 4 + u
                pool.wait_ge(s["mneg"], 2 * at + 2)
                pool.wait_ge(s["mpart3"], at)
                pool.tensor_tensor(g.mres[:, :], g.mneg[:, :], g.mparts[:, 0, :], ALU.subtract).then_inc(s["mres"], 1)
                pool.wait_ge(s["m_stored"], at * 16)
                pool.tensor_tensor(g.mparts[:, 1, :], g.mneg[:, :], g.mparts[:, 0, :], ALU.subtract)\
                    .then_inc(s["mpart2"], 1)
                pool.wait_ge(s["mres"], at + 1)
                pool.wait_ge(s["mpart2"], at + 1)
                pool.wait_ge(s["m_loaded"], at * 16)
                pool.tensor_tensor(g.mparts[:, 2, :], g.mres[:, :], g.mparts[:, 1, :], ALU.subtract)\
                    .then_inc(s["mpart3"], 1)

            def scale_out(i, q):
                pool.wait_ge(s["rsum"], i * 4 + q + 1)
                pool.wait_ge(s["onorm"], i * 4 + q)
                pool.tensor_tensor(g.oscaled[:, :], g.osum[:, :], g.rsum[:, :], ALU.mult).then_inc(s["scaled"], 1)

            def residual(i):
                pool.wait_ge(s["ytmp"], i)
                pool.wait_ge(s["x_loaded"], i * 16)
                pool.wait_ge(s["x_stored"], (i - 1) * 16)
                pool.tensor_tensor(g.xnew[:, :], g.ytmp[:, :], g.xres[:, :], ALU.add).then_inc(s["xnew"], 1)

            def batch(i, first, last):
                for q in range(UNITS):
                    m = m_unit(q, first, last)
                    if m is not None:
                        split_max(i, m)
                    if q == 1 and not first:
                        residual(i)
                    if not (first and q == 0):
                        scale_out(i, q - 1)

            for u in range(2):
                split_max(lo, u)
            batches(pool, batch)
            scale_out(hi, -1)
            residual(hi)

        @block.vector
        def _(dve):
            def maxima(i, u, k, h):
                n = u * per + k * UH + h
                ring = n % (UNITS * per)
                width = P * (k + 1) if causal else N
                if k + h == 0 and (u >= 2 or lo):
                    dve.wait_ge(s["max_turned"], i * 4 + u - 1)
                dve.wait_ge(s["a_scores"], i * 64 + n + 1)
                dve.reduce_max(g.M[:, u % 2, k, h:h + 1], SA[ring % 3][:, 0:width], AX.X).then_inc(s["a_max"], 1)

            def check(i, q):
                dve.wait_ge(s["rsum"], i * 4 + q + 1)
                dve.wait_ge(s["onorm"], i * 4 + q)
                dve.tensor_tensor(g.scheck[:, :], SUMB[:, :], g.rsum[:, :], ALU.mult).then_inc(s["check"], 1)

            def normalise(i, q):
                dve.wait_ge(s["check"], i * 4 + q + 1)
                dve.wait_ge(s["scaled"], i * 4 + q + 1)
                dve.wait_ge(s["yacc"], i * 4 + q)
                dve.scalar_tensor_tensor(out=g.onorm[:, :], in0=g.scheck[:, :], scalar=2.0, in1=g.oscaled[:, :],
                                         op0=ALU.add, op1=ALU.mult).then_inc(s["onorm"], 1)

            def output(i):
                gate = g.mod[:, 2, bass.ds(i - 1, 1)] if not isinstance(i, int) else g.mod[:, 2, i - 1:i]
                dve.wait_ge(s["yacc"], i * 4)
                dve.wait_ge(s["xnew"], i - 1)
                dve.tensor_scalar(g.ytmp[:, :], YB[:, :], g.bo[:, layer:layer + 1], gate, ALU.add, ALU.mult)\
                   .then_inc(s["ytmp"], 1)

            def batch(i, first, last):
                for q in range(UNITS):
                    u = a_unit(q, last)
                    for k in range(CH):
                        for h in range(UH):
                            if u is not None:
                                maxima(i, u, k, h)
                            if (k, h) == (1, 1) and q == 1 and not first:
                                output(i)
                            if (k, h) == (3, 1) and not (first and q == 0):
                                check(i, q - 1)
                            if (k, h) == (3, 3) and not (first and q == 0):
                                normalise(i, q - 1)

            for u in range(2):
                for k in range(CH):
                    for h in range(UH):
                        maxima(lo, u, k, h)
            batches(dve, batch)
            check(hi, -1)
            normalise(hi, -1)
            output(hi)


def setup_experts(g):
    nc = g.nc
    g.wg = g.sb("wg", [P, E])
    g.route_c = g.sb("route_c", [P, P + 3 * E])
    g.htok = g.sb("htok", [P, NT // P, C])
    g.logits = g.sb("logits", [P, NT // P, E])
    g.gate_w = g.sb("gate_w", [P, NT // P])
    g.slot_in = g.sb("slot_in", [P, NT // P], I32)
    g.slot_out = g.sb("slot_out", [P, NT // P], I32)
    g.gs = {n: g.sem("g_" + n) for n in (
        "setup", "x_loaded", "mean", "xc", "sq", "var", "std", "rstd", "xh", "h", "turned", "htok", "lpsum", "logits",
        "vec", "counts", "zeros", "zeroed", "scattered", "gathered", "picked", "pturned", "pscaled", "x2", "x2_stored")}


    s = g.gs
    with nc.Block() as block:
        @block.gpsimd
        def _(pool):
            pool.memset(g.htok[:, :, :], 0.0).then_inc(s["zeros"], 1)

        @block.sync
        def _(sp):
            sp.wait_ge(s["zeros"], 1)
            rows = g.slots.rearrange("(p r) c -> p r c", p=P)
            n = NT // P
            sp.dma_start(rows[:, 0:n, :], g.htok[:, :, :]).then_inc(s["zeroed"], 16)
            sp.dma_start(rows[:, n:, :], g.htok[:, 0:E * CAP // P - n, :]).then_inc(s["zeroed"], 16)
            sp.wait_ge(s["zeroed"], 32)


def gate(g, x):
    nc, s = g.nc, g.gs

    with nc.Block() as block:
        @block.sync
        def _(sp):
            sp.dma_start(g.wg[:, :], g.ins["wg"]).then_inc(s["setup"], 16)
            sp.dma_start(g.route_c[:, :], g.ins["route_c"]).then_inc(s["setup"], 16)
            with sp.Fori(0, B) as it:
                sp.wait_ge(s["xc"], it)
                sp.dma_start(g.x_in[:, :], x[it]).then_inc(s["x_loaded"], 16)

        @block.tensor
        def _(pe):
            pe.wait_ge(s["setup"], 32)
            with pe.Fori(0, B) as it:
                norm_tensor(g, s, pe, it)
                pe.wait_ge(s["h"], it + 1)
                pe.wait_ge(s["htok"], it)
                for c in range(CH):
                    mm = pe.transpose(g.bank[2][:, c * P:(c + 1) * P], g.h[:, c * P:(c + 1) * P], g.ident[:, :])
                mm.then_inc(s["turned"], 1)
                pe.wait_ge(s["logits"], it)
                for c in range(CH):
                    mm = pe.matmul(g.bank[3][:, c * E:(c + 1) * E], g.h[:, c * P:(c + 1) * P], g.wg[:, :],
                                   start=(c == 0), stop=True, skip_group_check=True)
                mm.then_inc(s["lpsum"], 1)

        @block.scalar
        def _(act):
            with act.Fori(0, B) as it:
                norm_scalar(g, s, act, it)

        @block.vector
        def _(dve):
            with dve.Fori(0, B) as it:
                norm_vector(g, s, dve, it, 4, 3, "lpsum", it)
                dve.wait_ge(s["turned"], it + 1)
                dve.tensor_scalar(g.htok[:, bass.ds(it * CH, CH), :],
                                  g.bank[2][:, :].rearrange("p (c n) -> p c n", c=CH), 1.0, None, ALU.mult)\
                   .then_inc(s["htok"], 1)
                dve.wait_ge(s["lpsum"], it + 1)
                dve.tensor_scalar(g.logits[:, bass.ds(it * CH, CH), :],
                                  g.bank[3][:, 0:CH * E].rearrange("p (c n) -> p c n", c=CH), 1.0, None, ALU.mult)\
                   .then_inc(s["logits"], 1)


def norm_tensor(g, s, pe, it):
    pe.wait_ge(s["x_loaded"], it * 16 + 16)
    pe.wait_ge(s["xc"], it)
    pe.matmul(g.bank[0][:, :], g.mean_w[:, :], g.x_in[:, :], start=True, stop=True).then_inc(s["mean"], 1)
    pe.wait_ge(s["sq"], it + 1)
    pe.wait_ge(s["std"], it)
    pe.matmul(g.bank[1][:, :], g.mean_w[:, :], g.sq[:, :], start=True, stop=True).then_inc(s["var"], 1)


def norm_scalar(g, s, act, it):
    act.wait_ge(s["xc"], it + 1)
    act.wait_ge(s["var"], it)
    act.activation(g.sq[:, :], g.xc[:, :], ACT.Square).then_inc(s["sq"], 1)
    act.wait_ge(s["var"], it + 1)
    act.activation(g.std[:, :], g.bank[1][:, :], ACT.Ln, bias=g.eps[:, 0:1]).then_inc(s["std"], 1)
    act.wait_ge(s["std"], it + 1)
    act.wait_ge(s["xh"], it)
    act.activation(g.rstd[:, :], g.std[:, :], ACT.Exp, scale=-0.5).then_inc(s["rstd"], 1)


def norm_vector(g, s, dve, it, scale, shift, reader, read, col=None):
    col = it if col is None else col
    dve.wait_ge(s["mean"], it + 1)
    dve.wait_ge(s["xh"], it)
    dve.wait_ge(s["sq"], it)
    dve.tensor_tensor(g.xc[:, :], g.x_in[:, :], g.bank[0][:, :], ALU.subtract).then_inc(s["xc"], 1)
    dve.wait_ge(s["rstd"], it + 1)
    dve.wait_ge(s["xc"], it + 1)
    dve.wait_ge(s["h"], it)
    dve.tensor_tensor(g.xh[:, :], g.xc[:, :], g.rstd[:, :], ALU.mult).then_inc(s["xh"], 1)
    dve.wait_ge(s["xh"], it + 1)
    dve.wait_ge(s[reader], read)
    if reader == "lpsum":
        dve.wait_ge(s["turned"], it)
    dve.tensor_scalar(g.h[:, :], g.xh[:, :], g.mod[:, scale, bass.ds(col, 1)], g.mod[:, shift, bass.ds(col, 1)],
                      ALU.mult, ALU.add).then_inc(s["h"], 1)


def route(g):
    nc, s = g.nc, g.gs
    T = NT // P
    big = g.xc[:, 0:T * E].rearrange("p (t e) -> p t e", e=E)
    ex = g.sq[:, 0:T * E].rearrange("p (t e) -> p t e", e=E)
    hot = g.std[:, 0:T * E].rearrange("p (t e) -> p t e", e=E)
    cum = g.xh[:, 0:T * E].rearrange("p (t e) -> p t e", e=E)
    r = g.rstd[:, 0:10 * T].rearrange("p (n t) -> p n t", n=10)
    top, den, pick, pos, keep, slot = (r[:, n, :] for n in range(6))
    tri, rev = g.route_c[:, 0:P], g.route_c[:, P:P + E]
    base, ones = g.route_c[:, P + E:P + 2 * E], g.ones_w[:, 0:T]

    def wide(col):
        return col.unsqueeze(2).broadcast_to([P, T, E])

    def rows(c):
        return c.unsqueeze(1).broadcast_to([P, T, E])

    with nc.Block() as block:
        @block.vector
        def _(dve):
            n = 0

            def step(i):
                nonlocal n
                n += 1
                i.then_inc(s["vec"], 1)
                dve.wait_ge(s["vec"], n)

            step(dve.reduce_max(top, g.logits[:, :, :], AX.X))
            step(dve.tensor_tensor(big, g.logits[:, :, :], wide(top), ALU.subtract))
            dve.wait_ge(s["sq"], B + 1)
            step(dve.reduce_sum(den, ex, AX.X))
            step(dve.reduce_max(top, ex, AX.X))
            step(dve.reciprocal(den, den))
            step(dve.tensor_tensor(g.gate_w[:, :], top, den, ALU.mult))
            step(dve.tensor_tensor(big, ex, wide(top), ALU.is_equal))
            step(dve.tensor_tensor(big, big, rows(rev), ALU.mult))
            step(dve.reduce_max(pick, big, AX.X))
            step(dve.tensor_tensor(hot, big, wide(pick), ALU.is_equal))
            dve.wait_ge(s["counts"], 1)
            step(dve.tensor_copy(big, g.bank[5][:, 0:T * E].rearrange("p (t e) -> p t e", e=E)))
            for e in range(E):
                scan = dve.tensor_tensor_scan(ex[:, :, e], ones, big[:, :, e], 0.0, ALU.mult, ALU.add)
                step(scan)
            step(dve.tensor_tensor(ex, ex, big, ALU.subtract))
            step(dve.tensor_tensor(cum, ex, g.bank[4][:, 0:T * E].rearrange("p (t e) -> p t e", e=E), ALU.add))
            step(dve.tensor_tensor(big, cum, hot, ALU.mult))
            step(dve.reduce_sum(pos, big, AX.X))
            step(dve.tensor_scalar(keep, pos, float(CAP), None, ALU.is_le))
            step(dve.tensor_tensor(g.gate_w[:, :], g.gate_w[:, :], keep, ALU.mult))
            step(dve.tensor_tensor(big, hot, rows(base), ALU.mult))
            step(dve.reduce_sum(slot, big, AX.X))
            step(dve.scalar_tensor_tensor(out=slot, in0=slot, scalar=-1.0, in1=pos, op0=ALU.add, op1=ALU.add))
            step(dve.tensor_tensor(slot, slot, keep, ALU.mult))
            step(dve.tensor_copy(g.slot_out[:, :], slot))
            step(dve.tensor_scalar(keep, keep, -float(E * CAP), float(E * CAP), ALU.mult, ALU.add))
            step(dve.tensor_tensor(slot, slot, keep, ALU.add))
            step(dve.tensor_copy(g.slot_in[:, :], slot))
            g.route_steps = n

        @block.scalar
        def _(act):
            act.wait_ge(s["vec"], 2)
            act.activation(ex, big, ACT.Exp).then_inc(s["sq"], 1)

        @block.tensor
        def _(pe):
            pe.wait_ge(s["vec"], 10)
            flat = g.std[:, 0:T * E]
            pe.matmul(g.bank[4][:, 0:T * E], tri, flat, start=True, stop=True)
            pe.matmul(g.bank[5][:, 0:T * E], g.ones_w[:, :], flat, start=True, stop=True).then_inc(s["counts"], 1)

    with nc.Block() as block:
        @block.gpsimd
        def _(pool):
            for t in range(T):
                pool.indirect_dma_start(g.slots, bass.IndirectOffsetOnAxis(ap=g.slot_in[:, t:t + 1], axis=0),
                                        g.htok[:, t, :], None, bounds_check=E * CAP - 1, oob_is_err=False)\
                    .then_inc(s["scattered"], 16)
            pool.wait_ge(s["scattered"], 16 * T)


def setup_expert_loop(g):
    g.ew1 = g.sb("ew1", [P, 2, F])
    g.ew2 = g.sb("ew2", [P, 2, F])
    g.eb1 = g.sb("eb1", [P, 2, F // P])
    g.eb2 = g.sb("eb2", [P, 2, C])
    g.eh = g.sb("eh", [P, F // P, CAP])
    g.exT = g.sb("exT", [P, CAP])
    g.es = {n: g.sem("e_" + n) for n in ("turned", "xT", "hidden", "relu", "answer", "biased", "stored")}
    g.eload = [g.sem(f"e_loaded{i}") for i in range(2)]


def experts(g):
    nc, s = g.nc, g.es
    ST = CAP // P
    HALF = CAP // 2
    xs = [g.qk[:, :, :], g.ra[:, :, :]]
    ys = [g.rb[:, :, :], g.res[:, :, :]]

    def tile(t):
        return t.rearrange("p a n -> p (a n)")[:, 0:CAP].rearrange("p (s c) -> p s c", c=C)

    with nc.Block() as block:
        @block.sync
        def _(sp):
            def load(e, par):
                sp.dma_start(g.ew1[:, par, :], g.ins["ew1"][e]).then_inc(g.eload[par], 16)
                sp.dma_start(g.ew2[:, par, :].rearrange("p (f c) -> p f c", c=C), g.ins["ew2"][e])\
                  .then_inc(g.eload[par], 16)
                sp.dma_start(g.eb1[:, par, :], g.ins["eb1"][e]).then_inc(g.eload[par], 16)
                sp.dma_start(g.eb2[:, par, :], g.ins["eb2"][e]).then_inc(g.eload[par], 16)
                sp.dma_start(tile(xs[par]), g.slots_by_expert[e]).then_inc(g.eload[par], 16)

            def two(i, last):
                for par in range(2):
                    if par == 0:
                        sp.wait_ge(s["answer"], i * 2 * ST)
                        load(i * 2 + 1, 1)
                    sp.wait_ge(s["biased"], (i * 2 + par + 1) * ST)
                    sp.dma_start(g.answers_by_expert[i * 2 + par], tile(ys[par])).then_inc(s["stored"], 16)
                    if par == 0 and not last:
                        load(i * 2 + 2, 0)

            load(0, 0)
            with sp.Fori(0, E // 2 - 1) as i:
                two(i, False)
            two(E // 2 - 1, True)
            sp.wait_ge(s["stored"], 16 * E)

        @block.tensor
        def _(pe):
            with pe.Fori(0, E // 2) as i:
                for par in range(2):
                    pe.wait_ge(g.eload[par], i * 80 + 80)
                    pe.wait_ge(s["xT"], (i * 2 + par) * 2)
                    for t in range(ST):
                        bank, col = (g.bank[0], t * P) if t < 4 else (g.bank[1], 0)
                        mm = pe.transpose(bank[:, col:col + P], tile(xs[par])[:, t, :], g.ident[:, :])
                    mm.then_inc(s["turned"], 1)
                    pe.wait_ge(s["xT"], (i * 2 + par) * 2 + 2)
                    for f in range(F // P):
                        for half in range(2):
                            n = f * 2 + half
                            pe.wait_ge(s["relu"], (i * 2 + par) * 8 + n - 3) if n >= 4 else None
                            pe.matmul(g.bank[2 + n % 4][:, 0:HALF], g.ew1[:, par, f * P:(f + 1) * P],
                                      g.exT[:, half * HALF:(half + 1) * HALF], start=True, stop=True)\
                              .then_inc(s["hidden"], 1)
                    pe.wait_ge(s["relu"], (i * 2 + par) * 8 + 8)
                    for t in range(ST):
                        if t >= 2:
                            pe.wait_ge(s["biased"], (i * 2 + par) * ST + t - 1)
                        for f in range(F // P):
                            mm = pe.matmul(g.bank[6 + t % 2][:, 0:C], g.eh[:, f, t * P:(t + 1) * P],
                                           g.ew2[:, par, f * C:(f + 1) * C], start=(f == 0), stop=(f == F // P - 1))
                        mm.then_inc(s["answer"], 1)
                    pe.wait_ge(s["biased"], (i * 2 + par + 1) * ST)

        @block.scalar
        def _(act):
            with act.Fori(0, E // 2) as i:
                for par in range(2):
                    act.wait_ge(s["answer"], (i * 2 + par) * ST)
                    for f in range(F // P):
                        for half in range(2):
                            n = f * 2 + half
                            act.wait_ge(s["hidden"], (i * 2 + par) * 8 + n + 1)
                            act.activation(g.eh[:, f, half * HALF:(half + 1) * HALF], g.bank[2 + n % 4][:, 0:HALF],
                                           ACT.Relu, bias=g.eb1[:, par, f:f + 1]).then_inc(s["relu"], 1)

        @block.vector
        def _(dve):
            with dve.Fori(0, E // 2) as i:
                for par in range(2):
                    dve.wait_ge(s["turned"], i * 2 + par + 1)
                    dve.wait_ge(s["hidden"], (i * 2 + par) * 8)
                    dve.tensor_copy(g.exT[:, 0:512], g.bank[0][:, :]).then_inc(s["xT"], 1)
                    dve.tensor_copy(g.exT[:, 512:CAP], g.bank[1][:, 0:CAP - 512]).then_inc(s["xT"], 1)
                    dve.wait_ge(s["stored"], (i * 2 + par) * 16)
                    for t in range(ST):
                        dve.wait_ge(s["answer"], (i * 2 + par) * ST + t + 1)
                        dve.tensor_tensor(tile(ys[par])[:, t, :], g.bank[6 + t % 2][:, 0:C], g.eb2[:, par, :],
                                          ALU.add).then_inc(s["biased"], 1)


def combine(g, x1, x2):
    nc, s = g.nc, g.gs
    T = NT // P
    with nc.Block() as block:
        @block.gpsimd
        def _(pool):
            for t in range(T):
                pool.indirect_dma_start(g.htok[:, t, :], None, g.answers,
                                        bass.IndirectOffsetOnAxis(ap=g.slot_out[:, t:t + 1], axis=0))\
                    .then_inc(s["gathered"], 16)
            pool.wait_ge(s["gathered"], 16 * T)
    with nc.Block() as block:
        @block.sync
        def _(sp):
            with sp.Fori(0, B) as it:
                sp.wait_ge(s["x2"], it)
                sp.dma_start(g.x_in[:, :], x1[it]).then_inc(s["x_loaded"], 16)
                sp.wait_ge(s["x2"], it + 1)
                sp.dma_start(x2[it], g.xh[:, :]).then_inc(s["x2_stored"], 16)
            sp.wait_ge(s["x2_stored"], B * 16)

        @block.vector
        def _(dve):
            with dve.Fori(0, B) as it:
                dve.wait_ge(s["pturned"], it)
                gate_w = g.gate_w[:, bass.ds(it * CH, CH)].unsqueeze(2).broadcast_to([P, CH, C])
                dve.tensor_tensor(g.xc[:, :].rearrange("p (c n) -> p c n", c=CH),
                                  g.htok[:, bass.ds(it * CH, CH), :], gate_w, ALU.mult).then_inc(s["picked"], 1)
                dve.wait_ge(s["pturned"], it + 1)
                dve.wait_ge(s["x2"], it)
                dve.tensor_scalar(g.sq[:, :], g.bank[2][:, :], g.mod[:, 5, bass.ds(it, 1)], None, ALU.mult)\
                   .then_inc(s["pscaled"], 1)
                dve.wait_ge(s["pscaled"], it + 1)
                dve.wait_ge(s["x_loaded"], (it + B) * 16 + 16)
                dve.wait_ge(s["x2_stored"], it * 16)
                dve.tensor_tensor(g.xh[:, :], g.sq[:, :], g.x_in[:, :], ALU.add).then_inc(s["x2"], 1)

        @block.tensor
        def _(pe):
            with pe.Fori(0, B) as it:
                pe.wait_ge(s["picked"], it + 1)
                pe.wait_ge(s["pscaled"], it)
                for c in range(CH):
                    mm = pe.transpose(g.bank[2][:, c * P:(c + 1) * P], g.xc[:, c * P:(c + 1) * P], g.ident[:, :])
                mm.then_inc(s["pturned"], 1)


def setup_local(g):
    nc = g.nc
    g.lw = g.sb("lw", [P, 2, 3 * INNER])
    g.lwo = g.sb("lwo", [P, 2, PAIRS, C])
    g.lw1 = g.sb("lw1", [P, 2, 2 * HID])
    g.lw2 = g.sb("lw2", [P, 2, HC, C])
    g.lcol = g.sb("lcol", [P, 2, 3 + 2 * HC])
    g.lqk = g.sb("lqk", [P, 2, 4, HD])
    g.xpos = g.sb("xpos", [P, 4, CH, HD])
    g.turn = g.sb("l_turn", [P, 2, 4, CH, HD])
    g.minus_half = g.sb("l_minus_half", [P, 2 * PAIRS])
    g.bandf = g.sb("bandf", [P, 2, WIN])
    g.band = g.sb("band", [P, 2, WIN], BF16)
    g.xs = g.sb("l_xs", [P, N])
    g.lsq = g.sb("l_sq", [P, 2, 2 * PAIRS, HD])
    g.lt1 = g.sb("l_t1", [P, 2 * PAIRS, HD])
    g.lt2 = g.sb("l_t2", [P, 2 * PAIRS, HD])
    g.lts = g.sb("l_ts", [P, 2, 2 * PAIRS, HD])
    g.lss = g.sb("l_ss", [P, 2, 2 * PAIRS])
    g.lclip = g.sb("l_clip", [P, 2, 2 * PAIRS])
    g.linv = g.sb("l_inv", [P, 2, 2 * PAIRS])
    g.lqn = g.sb("l_qn", [P, 2, 2 * PAIRS, HD])
    g.qr = g.sb("l_qr", [P, PAIRS, N])
    g.kr = g.sb("l_kr", [P, PAIRS, W + N])
    g.vt = g.sb("l_vt", [P, CH, INNER])
    g.lmx = g.sb("l_mx", [P, 4, 2])
    g.lnb = g.sb("l_nb", [P, 4, 2])
    g.lsm = g.sb("l_sm", [P, 4, 2])
    g.lrs = g.sb("l_rs", [P, 4, 2])
    g.pe_ = g.sb("l_p", [P, 2, 2, WIN])
    g.pn = g.sb("l_pn", [P, 2, 2, 2 * P])
    g.pt = g.sb("l_pt", [P, 2, 4, P])
    g.ot = g.sb("l_ot", [P, PAIRS, N])
    g.xr = g.sb("l_x", [P, N])
    g.x1l = g.sb("l_x1", [P, N])
    g.s2 = g.sb("l_s2", [P, N])
    g.cxc = g.sb("c_xc", [P, N])
    g.csq = g.sb("c_sq", [P, N])
    g.cvar = g.sb("c_var", [P, CH])
    g.crs = g.sb("c_rs", [P, CH])
    g.cspread = g.sb("c_spread", [P, CH, P])
    g.cxh = g.sb("c_xh", [P, N])
    g.lh = g.sb("l_h", [P, N])
    g.graw = g.sb("l_graw", [P, HC, N])
    g.gl = g.sb("l_gl", [P, HC, N])
    g.hm = g.sb("l_hm", [P, HC, N])
    g.x2l = g.sb("l_x2", [P, N])
    g.xo = g.sb("l_xo", [P, N])
    g.xf = g.sb("l_xf", [P, N])
    g.ls = {n: g.sem("l_" + n) for n in (
        "setup", "xs_loaded", "xr_loaded", "xf_loaded", "proj", "sq", "ss", "clip", "inv", "t1", "t2", "tsum", "qn",
        "qk_turned", "qk", "one_head", "v_psum", "v", "scores", "max", "nbias", "exp", "rsum", "pnorm",
        "turned", "pt", "pv", "o", "wo", "x1", "s2", "mean", "xc", "sq2", "var", "veps", "rstd", "spread", "rstd_psum",
        "xh", "h", "gate_psum", "gate", "gelu", "value_psum", "hidden", "y2", "x2", "final", "stored")}
    s = g.ls
    with nc.Block() as block:
        @block.sync
        def _(sp):
            for dst, src in ((g.lw[:, :, :], g.ins["lw"]), (g.lwo[:, :, :, :], g.ins["lwo"]),
                             (g.lw1[:, :, :], g.ins["lw1"]), (g.lw2[:, :, :, :], g.ins["lw2"]),
                             (g.lcol[:, :, :], g.ins["lcol"]), (g.xpos[:, :, :, :], g.ins["xpos"]),
                             (g.lqk[:, :, :, :], g.ins["lqk"]), (g.bandf[:, :, :], g.ins["band"])):
                sp.dma_start(dst, src).then_inc(s["setup"], 16)
            sp.wait_ge(s["setup"], 8 * 16)

        @block.vector
        def _(dve):
            dve.memset(g.minus_half[:, :], -0.5)
            dve.memset(g.graw[:, :, :], 0.0)
            dve.wait_ge(s["setup"], 8 * 16)
            dve.tensor_copy(g.band[:, :, :], g.bandf[:, :, :])
            for layer in range(2):
                dve.tensor_tensor(g.turn[:, layer, :, :, :], g.xpos[:, :, :, :],
                                  g.lqk[:, layer, :, :].unsqueeze(2).broadcast_to([P, 4, CH, HD]), ALU.mult)

        @block.gpsimd
        def _(pool):
            pool.memset(g.pn[:, :, :, :], 0.0)
            pool.memset(g.kr[:, :, 0:W], 0.0)
            pool.memset(g.xs[:, :], 0.0)
            pool.memset(g.s2[:, :], 0.0)


def local_input(g, x, h_out):
    nc = g.nc
    s = {n: g.sem("n_" + n) for n in ("x_loaded", "mean", "xc", "sq", "var", "std", "rstd", "xh", "h", "stored")}
    with nc.Block() as block:
        @block.sync
        def _(sp):
            with sp.Fori(0, B) as it:
                sp.wait_ge(s["xc"], it)
                sp.dma_start(g.x_in[:, :], x[it]).then_inc(s["x_loaded"], 16)
                sp.wait_ge(s["h"], it + 1)
                sp.dma_start(h_out[it], g.h[:, :]).then_inc(s["stored"], 16)
            sp.wait_ge(s["stored"], B * 16)

        @block.tensor
        def _(pe):
            with pe.Fori(0, B) as it:
                norm_tensor(g, s, pe, it)

        @block.scalar
        def _(act):
            with act.Fori(0, B) as it:
                norm_scalar(g, s, act, it)

        @block.vector
        def _(dve):
            with dve.Fori(0, B) as it:
                norm_vector(g, s, dve, it, 4, 3, "stored", it * 16, it + B)


def local_layer(g, layer, x_in, x_out, x3):
    nc, s = g.nc, g.ls
    lo, hi = B * layer, B * (layer + 1)
    NU, NH, HH = CH * PAIRS, 2 * PAIRS, HD // 2
    S, TB, OB, PB, KB, XB, YB = g.bank[0:2], g.bank[2], g.bank[3], g.bank[4], g.bank[5], g.bank[6], g.bank[7]
    MB = (PB, KB)
    col = lambda n: g.lcol[:, layer, n:n + 1]

    def heads(ap):
        return ap.rearrange("p (h d) -> p h d", d=HD)

    def after(it, per, n):
        return it * per + n if not isinstance(it, int) else max(it * per + n, 0)

    def kept(t, last):
        return t < 2 or not last

    def passes(engine, batch, drain):
        batch(lo, True, False)
        with engine.Fori(lo + 1, hi - 1) as it:
            batch(it, False, False)
        batch(hi - 1, False, True)
        drain(hi)

    with nc.Block() as block:
        @block.sync
        def _(sp):
            def load_xs(b):
                sp.dma_start(g.xs[0:C // 2, :], x_in[b - lo, 0:C // 2, :]).then_inc(s["xs_loaded"], 16)
                sp.dma_start(g.xs[C // 2:C, 1:N], x_in[b - lo, C // 2:C, 0:N - 1]).then_inc(s["xs_loaded"], 16)

            def load_xf(it):
                if layer == 1:
                    sp.wait_ge(s["final"], it - 1 - lo)
                    sp.dma_start(g.xf[:, :], x3[it - 1 - lo]).then_inc(s["xf_loaded"], 16)

            def store(it):
                if layer == 1:
                    sp.wait_ge(s["final"], it - lo)
                else:
                    sp.wait_ge(s["x2"], it)
                sp.dma_start(x_out[it - 1 - lo], g.xo[:, :]).then_inc(s["stored"], 16)

            def batch(it, first, last):
                if not first:
                    load_xf(it)
                if not last:
                    sp.wait_ge(s["v_psum"], it * CH + CH)
                    load_xs(it + 1)
                if not first:
                    sp.wait_ge(s["x1"], it)
                sp.dma_start(g.xr[:, :], x_in[it - lo]).then_inc(s["xr_loaded"], 16)
                if not first:
                    store(it)

            def drain(it):
                load_xf(it)
                store(it)

            load_xs(lo)
            passes(sp, batch, drain)
            sp.wait_ge(s["stored"], hi * 16)

        @block.tensor
        def _(pe):
            def project(it, a, w):
                c = a % CH
                if c == 0 and w == 0:
                    pe.wait_ge(s["xs_loaded"], (it + a // CH) * 32 + 32)
                pe.wait_ge(s["t2"], after(it, 4 * CH, 4 * a + 2 * w - 2))
                if w == 0:
                    pe.wait_ge(s["v"], it * CH + a)
                pe.matmul(MB[w][:, :], g.xs[:, c * P:(c + 1) * P], g.lw[:, layer, w * INNER:(w + 1) * INNER],
                          start=True, stop=True).then_inc(s["proj"], 1)

            def values(it, a):
                c = a % CH
                pe.wait_ge(s["t2"], it * 4 * CH + 4 * a + 2)
                pe.matmul(PB[:, :], g.xs[:, c * P:(c + 1) * P], g.lw[:, layer, 2 * INNER:3 * INNER],
                          start=True, stop=True).then_inc(s["v_psum"], 1)

            def turn_item(it, a, w):
                m = it * 2 * CH + 2 * a + w
                pe.wait_ge(s["qn"], m + 1)
                pe.wait_ge(s["qk"], m)
                for p in range(PAIRS):
                    mm = pe.transpose(XB[:, p * P:(p + 1) * P],
                                      g.lqn[:, w, 2 * p:2 * p + 2, :].rearrange("p h d -> p (h d)"), g.ident[:, :])
                mm.then_inc(s["qk_turned"], 1)

            def projections(it, a, j):
                if j == 0:
                    project(it, a, 0)
                if j == 1:
                    project(it, a, 1)
                if j == 2:
                    values(it, a)
                    turn_item(it, a, 0)
                if j == 3:
                    turn_item(it, a, 1)

            def scores(it, n, first):
                t, p = divmod(n, PAIRS)
                if p == 0:
                    pe.wait_ge(s["qk"], it * 2 * CH + 2 * t + 2)
                if n > 1 or not first:
                    pe.wait_ge(s["exp"], it * NU + n - 1)
                for e in range(2):
                    r = slice(HD * e, HD * (e + 1))
                    out = S[n % 2][:, WIN * e:WIN * (e + 1)]
                    if e == 1:
                        pe.wait_ge(s["one_head"], it * NU + n + 1)
                    mm = pe.matmul(out, g.qr[r, p, t * P:(t + 1) * P], g.kr[r, p, t * P:t * P + WIN],
                                   start=True, stop=False, skip_group_check=True)
                    if e == 0:
                        mm.then_inc(s["one_head"], 1)
                    mm = pe.matmul(out, g.identb[:, :], g.band[:, min(t, 1), :], start=False, stop=True,
                                   skip_group_check=True)
                mm.then_inc(s["scores"], 1)

            def turn(it, n):
                pe.wait_ge(s["pnorm"], it * NU + n + 1)
                pe.wait_ge(s["pt"], it * NU + n)
                for j in range(4):
                    mm = pe.transpose(TB[:, j * P:(j + 1) * P],
                                      g.pn[:, n % 2, j // 2, (j % 2) * P:(j % 2 + 1) * P], g.ident[:, :])
                mm.then_inc(s["turned"], 1)

            def pv(it, n):
                t, p = n // PAIRS % CH, n % PAIRS
                pe.wait_ge(s["pt"], it * NU + n + 1)
                if p == 0:
                    pe.wait_ge(s["o"], it * CH + n // PAIRS)
                    pe.wait_ge(s["v"], it * CH + n // PAIRS + 1)
                for j in (1, 0) if t else (1,):
                    for e in range(2):
                        at = (2 * p + e) * HD
                        mm = pe.matmul(OB[HD * e:HD * (e + 1), p * P:(p + 1) * P], g.vt[:, t - 1 + j, at:at + HD],
                                       g.pt[:, n % 2, 2 * e + j, :], start=(j == 1), stop=(j == 0 or t == 0),
                                       skip_group_check=True)
                mm.then_inc(s["pv"], 1)

            def chain(it, n):
                if n == 4:
                    pe.wait_ge(s["o"], it * CH)
                    pe.wait_ge(s["x2"], it - 1)
                    for p in range(PAIRS):
                        mm = pe.matmul(YB[:, :], g.lwo[:, layer, p, :], g.ot[:, p, :], start=(p == 0),
                                       stop=(p == PAIRS - 1), skip_group_check=True)
                    mm.then_inc(s["wo"], 1)
                if n == 5:
                    pe.wait_ge(s["s2"], it * 2)
                    pe.matmul(YB[:, :], g.mean_w[:, :], g.s2[:, :], start=True, stop=True).then_inc(s["mean"], 1)
                if n == 6:
                    pe.wait_ge(s["sq2"], it)
                    for c in range(CH):
                        mm = pe.matmul(YB[:, c:c + 1], g.csq[:, c * P:(c + 1) * P], g.mean_w[:, 0:1],
                                       start=True, stop=True, skip_group_check=True)
                    mm.then_inc(s["var"], 1)
                if n == 8:
                    pe.wait_ge(s["spread"], it)
                    for c in range(CH):
                        mm = pe.matmul(YB[:, c * P:(c + 1) * P], g.cspread[:, c, :], g.ident[:, :],
                                       start=True, stop=True, skip_group_check=True)
                    mm.then_inc(s["rstd_psum"], 1)
                if 9 <= n < 9 + HC:
                    j = n - 9
                    w, at = min(P, HID - j * P), HID + j * P
                    pe.wait_ge(s["h"], it)
                    pe.wait_ge(s["gate"], (it - 1) * HC + j)
                    pe.matmul(YB[0:w, :], g.lw1[:, layer, at:at + w], g.lh[:, :], start=True, stop=True)\
                      .then_inc(s["gate_psum"], 1)
                if 12 <= n < 12 + HC:
                    j = n - 12
                    w, at = min(P, HID - j * P), j * P
                    pe.wait_ge(s["gate"], it * HC)
                    pe.wait_ge(s["hidden"], (it - 1) * HC + j)
                    pe.matmul(YB[0:w, :], g.lw1[:, layer, at:at + w], g.lh[:, :], start=True, stop=True)\
                      .then_inc(s["value_psum"], 1)
                if n == 15:
                    pe.wait_ge(s["hidden"], it * HC)
                    for j in range(HC):
                        w = min(P, HID - j * P)
                        mm = pe.matmul(YB[:, :], g.lw2[0:w, layer, j, :], g.hm[0:w, j, :], start=(j == 0),
                                       stop=(j == HC - 1), skip_group_check=True)
                    mm.then_inc(s["y2"], 1)

            def batch(it, first, last):
                for n in range(NU):
                    t, j = divmod(n, 4)
                    scores(it, n, first)
                    if kept(t, last):
                        projections(it, t + 2, j)
                    if not first or n >= 2:
                        turn(it, n - 2)
                    if not first:
                        chain(it, n)
                    if not first or n >= 3:
                        pv(it, n - 3)

            def drain(it):
                for n in range(NU):
                    if n < 2:
                        turn(it, n - 2)
                    if n < 3:
                        pv(it, n - 3)
                    chain(it, n)

            for a in range(2):
                for j in range(4):
                    projections(lo, a, j)
            passes(pe, batch, drain)

        @block.scalar
        def _(act):
            def square(it, a, w):
                m = it * 2 * CH + 2 * a + w
                act.wait_ge(s["proj"], m + 1)
                act.wait_ge(s["ss"], after(it, 2 * CH, 2 * a + w - 1))
                act.activation(g.lsq[:, w, :, :], heads(MB[w][:, :]), ACT.Square).then_inc(s["sq"], 1)

            def copy_item(it, a, w):
                m, c = it * 2 * CH + 2 * a + w, a % CH
                act.wait_ge(s["qk_turned"], m + 1)
                out = g.qr[:, :, c * P:(c + 1) * P] if w == 0 else g.kr[:, :, W + c * P:W + (c + 1) * P]
                act.activation(out, XB[:, :].rearrange("p (h n) -> p h n", h=PAIRS), ACT.Copy).then_inc(s["qk"], 1)

            def projections(it, a, j):
                if j < 2:
                    square(it, a, j)
                else:
                    copy_item(it, a, j - 2)

            def exps(it, n, first):
                act.wait_ge(s["nbias"], it * NU + n + 1)
                if n > 1 or not first:
                    act.wait_ge(s["pnorm"], it * NU + n - 1)
                for e in range(2):
                    last = act.activation(g.pe_[:, n % 2, e, :], S[n % 2][:, WIN * e:WIN * (e + 1)], ACT.Exp,
                                          bias=g.lnb[:, n % 4, e:e + 1], scale=QK_SCALE,
                                          accum_out=g.lsm[:, n % 4, e:e + 1])
                last.then_inc(s["exp"], 1)

            def copy_pt(it, n):
                act.wait_ge(s["turned"], it * NU + n + 1)
                act.wait_ge(s["pv"], after(it, NU, n - 1))
                act.activation(g.pt[:, n % 2, :, :], TB[:, :].rearrange("p (j n) -> p j n", j=4),
                               ACT.Copy).then_inc(s["pt"], 1)

            def copy_o(it, t):
                act.wait_ge(s["pv"], it * NU + 4 * t + 4)
                act.wait_ge(s["wo"], it if t >= 0 else it - 1)
                c = t % CH
                act.activation(g.ot[:, :, c * P:(c + 1) * P], OB[:, :].rearrange("p (h n) -> p h n", h=PAIRS),
                               ACT.Copy).then_inc(s["o"], 1)

            def chain(it, n):
                if n == 5:
                    act.wait_ge(s["x1"], it)
                    act.wait_ge(s["xc"], it - 1)
                    act.activation(g.s2[0:C // 2, :], g.x1l[0:C // 2, :], ACT.Copy).then_inc(s["s2"], 1)
                    act.activation(g.s2[C // 2:C, 1:N], g.x1l[C // 2:C, 0:N - 1], ACT.Copy).then_inc(s["s2"], 1)
                if n == 6:
                    act.wait_ge(s["xc"], it)
                    act.wait_ge(s["var"], it - 1)
                    act.activation(g.csq[:, :], g.cxc[:, :], ACT.Square).then_inc(s["sq2"], 1)
                if n == 12:
                    act.wait_ge(s["gate"], it * HC)
                    act.wait_ge(s["hidden"], (it - 1) * HC)
                    act.activation(g.gl[:, :, :], g.graw[:, :, :], ACT.Gelu).then_inc(s["gelu"], 1)

            def batch(it, first, last):
                for n in range(NU):
                    t, j = divmod(n, 4)
                    if j == 3 and not (first and t == 0):
                        copy_o(it, t - 1)
                    exps(it, n, first)
                    if not first:
                        chain(it, n)
                    if not first or n >= 2:
                        copy_pt(it, n - 2)
                    if kept(t, last):
                        projections(it, t + 2, j)

            def drain(it):
                for n in range(NU):
                    if n < 2:
                        copy_pt(it, n - 2)
                    if n == 2:
                        copy_o(it, -1)
                    chain(it, n)

            for a in range(2):
                for j in range(4):
                    projections(lo, a, j)
            passes(act, batch, drain)

        @block.gpsimd
        def _(pool):
            def add_turned(it, a, w):
                m = it * 2 * CH + 2 * a + w
                pool.wait_ge(s["t1"], m + 1)
                pool.wait_ge(s["t2"], 2 * m + 2)
                pool.wait_ge(s["qn"], after(it, 2 * CH, 2 * a + w - 1))
                pool.tensor_tensor(g.lts[:, w, :, :], g.lt1[:, :, :], g.lt2[:, :, :], ALU.add).then_inc(s["tsum"], 1)

            def over_norm(it, a, w):
                m = it * 2 * CH + 2 * a + w
                pool.wait_ge(s["clip"], m + 1)
                pool.wait_ge(s["qn"], after(it, 2 * CH, 2 * a + w - 1))
                pool.tensor_tensor(g.linv[:, w, :], g.lclip[:, w, :], g.minus_half[:, :], ALU.pow)\
                    .then_inc(s["inv"], 1)
                pool.wait_ge(s["inv"], m + 1)
                pool.wait_ge(s["tsum"], m + 1)
                pool.wait_ge(s["qk_turned"], after(it, 2 * CH, 2 * a + w - 1))
                pool.tensor_tensor(g.lqn[:, w, :, :], g.lts[:, w, :, :],
                                   g.linv[:, w, :].unsqueeze(2).broadcast_to([P, NH, HD]), ALU.mult)\
                    .then_inc(s["qn"], 1)

            def projections(it, a, j):
                if j < 2:
                    add_turned(it, a, j)
                    over_norm(it, a, j)

            def normalise(it, n):
                pool.wait_ge(s["exp"], it * NU + n + 1)
                pool.wait_ge(s["turned"], after(it, NU, n - 1))
                pool.wait_ge(s["rsum"], it * NU + n + 1)
                pool.tensor_tensor(g.pn[:, n % 2, :, W:2 * P], g.pe_[:, n % 2, :, :],
                                   g.lrs[:, n % 4, :].unsqueeze(2).broadcast_to([P, 2, WIN]), ALU.mult)\
                    .then_inc(s["pnorm"], 1)

            def chain(it, n):
                if n == 7:
                    pool.wait_ge(s["veps"], it)
                    pool.wait_ge(s["spread"], it - 1)
                    pool.tensor_tensor(g.crs[:, :], g.cvar[:, :], g.minus_half[:, 0:CH], ALU.pow)\
                        .then_inc(s["rstd"], 1)

            def batch(it, first, last):
                for n in range(NU):
                    t, j = divmod(n, 4)
                    if not first or n:
                        normalise(it, n - 1)
                    if not first:
                        chain(it, n)
                    if kept(t, last):
                        projections(it, t + 2, j)

            def drain(it):
                normalise(it, -1)
                chain(it, 7)

            for a in range(2):
                for j in range(2):
                    projections(lo, a, j)
            passes(pool, batch, drain)

        @block.vector
        def _(dve):
            def rotate(it, a, w):
                m, c = it * 2 * CH + 2 * a + w, a % CH
                table = lambda k, d: g.turn[:, layer, 2 * w + k, c, d].unsqueeze(1)
                psum = heads(MB[w][:, :])
                dve.wait_ge(s["tsum"], m)
                dve.wait_ge(s["sq"], m + 1)
                dve.tensor_tensor(g.lt1[:, :, :], psum, table(0, slice(0, HD)).broadcast_to([P, NH, HD]),
                                  ALU.mult).then_inc(s["t1"], 1)
                for lower, upper in ((slice(0, HH), slice(HH, HD)), (slice(HH, HD), slice(0, HH))):
                    dve.tensor_tensor(g.lt2[:, :, lower], psum[:, :, upper],
                                      table(1, lower).broadcast_to([P, NH, HH]), ALU.mult).then_inc(s["t2"], 1)

            def sum_squares(it, a, w):
                m = it * 2 * CH + 2 * a + w
                dve.wait_ge(s["sq"], m + 1)
                dve.wait_ge(s["clip"], after(it, 2 * CH, 2 * a + w - 1))
                dve.reduce_sum(g.lss[:, w, :], g.lsq[:, w, :, :], AX.X).then_inc(s["ss"], 1)
                dve.wait_ge(s["ss"], m + 1)
                dve.wait_ge(s["inv"], after(it, 2 * CH, 2 * a + w - 1))
                dve.tensor_scalar(g.lclip[:, w, :], g.lss[:, w, :], L2_EPS * L2_EPS, None, ALU.max)\
                   .then_inc(s["clip"], 1)

            def copy_v(it, a):
                dve.wait_ge(s["v_psum"], it * CH + a + 1)
                dve.wait_ge(s["pv"], after(it, NU, 4 * (a - 2)))
                dve.tensor_copy(g.vt[:, a % CH, :], PB[:, :]).then_inc(s["v"], 1)

            def projections(it, a, j):
                if j < 2:
                    sum_squares(it, a, j)
                    rotate(it, a, j)
                if j == 3:
                    copy_v(it, a)

            def maxima(it, n):
                at = it * NU + n
                dve.wait_ge(s["scores"], at + 1)
                dve.reduce_max(g.lmx[:, n % 4, :], S[n % 2][:, 0:2 * WIN].rearrange("p (e n) -> p e n", e=2),
                               AX.X).then_inc(s["max"], 1)
                dve.wait_ge(s["max"], at + 1)
                dve.tensor_scalar(g.lnb[:, n % 4, :], g.lmx[:, n % 4, :], -QK_SCALE, None, ALU.mult)\
                   .then_inc(s["nbias"], 1)

            def inverse_sum(it, n):
                dve.wait_ge(s["exp"], it * NU + n + 1)
                dve.reciprocal(g.lrs[:, n % 4, :], g.lsm[:, n % 4, :]).then_inc(s["rsum"], 1)

            def chain(it, n):
                if n == 4:
                    dve.wait_ge(s["wo"], it)
                    dve.wait_ge(s["xr_loaded"], it * 16)
                    dve.wait_ge(s["x2"], it - 1)
                    dve.tensor_tensor(g.x1l[:, :], g.xr[:, :], YB[:, :], ALU.add).then_inc(s["x1"], 1)
                if n == 5:
                    dve.wait_ge(s["mean"], it)
                    dve.wait_ge(s["xh"], it - 1)
                    dve.tensor_tensor(g.cxc[:, :], g.s2[:, :], YB[:, :], ALU.subtract).then_inc(s["xc"], 1)
                if n == 6:
                    dve.wait_ge(s["var"], it)
                    dve.wait_ge(s["rstd"], it - 1)
                    dve.tensor_scalar(g.cvar[:, :], YB[:, 0:CH], LN_EPS, None, ALU.add).then_inc(s["veps"], 1)
                if n == 7:
                    dve.wait_ge(s["rstd"], it)
                    dve.wait_ge(s["rstd_psum"], it - 1)
                    dve.tensor_copy(g.cspread[:, :, :], g.crs[:, :].unsqueeze(2).broadcast_to([P, CH, P]))\
                       .then_inc(s["spread"], 1)
                if n == 8:
                    dve.wait_ge(s["rstd_psum"], it)
                    dve.wait_ge(s["h"], it - 1)
                    dve.tensor_tensor(g.cxh[:, :], g.cxc[:, :], YB[:, :], ALU.mult).then_inc(s["xh"], 1)
                    dve.wait_ge(s["xh"], it)
                    dve.wait_ge(s["y2"], it - 1)
                    dve.tensor_scalar(g.lh[:, :], g.cxh[:, :], col(0), col(1), ALU.mult, ALU.add)\
                       .then_inc(s["h"], 1)
                if 9 <= n < 9 + HC:
                    j = n - 9
                    w, at = min(P, HID - j * P), 3 + HC + j
                    dve.wait_ge(s["gate_psum"], (it - 1) * HC + j + 1)
                    dve.wait_ge(s["gelu"], it - 1)
                    dve.tensor_scalar(g.graw[0:w, j, :], YB[0:w, :], g.lcol[0:w, layer, at:at + 1], None, ALU.add)\
                       .then_inc(s["gate"], 1)
                if 12 <= n < 12 + HC:
                    j = n - 12
                    w = min(P, HID - j * P)
                    dve.wait_ge(s["value_psum"], (it - 1) * HC + j + 1)
                    dve.wait_ge(s["gelu"], it)
                    dve.wait_ge(s["y2"], it - 1)
                    dve.scalar_tensor_tensor(out=g.hm[0:w, j, :], in0=YB[0:w, :],
                                             scalar=g.lcol[0:w, layer, 3 + j:4 + j], in1=g.gl[0:w, j, :],
                                             op0=ALU.add, op1=ALU.mult).then_inc(s["hidden"], 1)
                if n == 15:
                    x2 = g.xo if layer == 0 else g.x2l
                    dve.wait_ge(s["y2"], it)
                    dve.wait_ge(s["stored"], (it - 1) * 16)
                    dve.scalar_tensor_tensor(out=x2[:, :], in0=YB[:, :], scalar=col(2), in1=g.x1l[:, :],
                                             op0=ALU.add, op1=ALU.add).then_inc(s["x2"], 1)
                    if layer == 1:
                        gate = g.mod[:, 5, bass.ds(it - 1, 1)] if not isinstance(it, int) else g.mod[:, 5, it - 1:it]
                        dve.wait_ge(s["x2"], it)
                        dve.wait_ge(s["xf_loaded"], (it - lo) * 16)
                        dve.scalar_tensor_tensor(out=g.xo[:, :], in0=x2[:, :], scalar=gate, in1=g.xf[:, :],
                                                 op0=ALU.mult, op1=ALU.add).then_inc(s["final"], 1)

            def batch(it, first, last):
                for n in range(NU):
                    t, j = divmod(n, 4)
                    maxima(it, n)
                    if n or not first:
                        inverse_sum(it, n - 1)
                    if kept(t, last):
                        projections(it, t + 2, j)
                    if not first:
                        chain(it, n)

            def drain(it):
                inverse_sum(it, -1)
                for n in range(NU):
                    chain(it, n)

            for a in range(2):
                for j in range(4):
                    projections(lo, a, j)
            passes(dve, batch, drain)


def build(nc, ins, out, stop=None):
    with ExitStack() as ctx:
        g = Program(nc, ctx, ins)
        g.qk_dram = g.dram("qk_dram", [2 * B, 2, UNITS, PARTS, D, UH, N], BF16)
        g.v_dram = g.dram("v_dram", [2 * B, CH, P, H * VW])
        g.m_dram = g.dram("m_dram", [UH, PARTS, N], BF16)
        x1, x2, x3, hx, hy = (g.dram(n, [B, P, N]) for n in ("x1", "x2", "x3", "hx", "hy"))
        g.slots = g.dram("slots", [E * CAP, C])
        g.answers = g.dram("answers", [E * CAP, C])
        g.slots_by_expert = g.slots.rearrange("(e s p) c -> e p s c", e=E, p=P)
        g.answers_by_expert = g.answers.rearrange("(e s p) c -> e p s c", e=E, p=P)
        setup(g)
        with g.memory():
            setup_projection(g)
            with g.memory():
                setup_attention(g)
                project(g, 0, ins["xT"])
                attend(g, 0, ins["xT"], out if stop == "att0" else x1)
            if stop == "att0":
                return
            with g.memory():
                setup_experts(g)
                gate(g, x1)
                route(g)
                setup_expert_loop(g)
                experts(g)
                combine(g, x1, out if stop == "moe" else x2)
            if stop == "moe":
                return
            with g.memory():
                setup_attention(g)
                project(g, 1, x2)
                attend(g, 1, x2, out if stop == "att1" else x3)
            if stop == "att1":
                return
            local_input(g, x3, out if stop == "h7" else hx)
            if stop == "h7":
                return
        with g.memory():
            setup_local(g)
            local_layer(g, 0, hx, hy, x3)
            local_layer(g, 1, hy, out, x3)


def heads_to_partitions(w):
    lead = w.shape[:-1]
    return np.ascontiguousarray(
        np.moveaxis(w.reshape(*lead, UNITS, UH, D), -1, -2).reshape(*lead, C))


def constants():
    i = np.arange(P)
    sel = np.zeros((P, P), np.float32)
    for h in range(UH):
        sel[VW * h + D, VW * h:VW * (h + 1)] = -1.0
    later = (i[None, :] > i[:, None])
    masks = np.stack([np.where(later, NEG, 0.0), np.where(later.T, NEG, 0.0)], 1).astype(np.float32)
    pos = np.arange(N, dtype=np.float32)
    freqs = (1.0 / np.float32(10000.0) ** (np.arange(0, D, 2, dtype=np.float32) / np.float32(D))).astype(np.float32)
    ang = (pos[:, None] * freqs[None, :]).astype(np.float32)
    cos, sin = np.cos(ang).T, np.sin(ang).T
    c8, s8 = np.concatenate([cos, -cos]), np.concatenate([sin, sin])
    rope = np.stack([heads_to_partitions(np.tile(t, (H, 1)).T).T for t in (c8, s8)], 1).astype(np.float32)
    tri = (i[:, None] <= i[None, :]).astype(np.float32)
    e = np.arange(E, dtype=np.float32)
    route_c = np.concatenate([tri, np.tile(np.concatenate([E - e, e * CAP, np.ones(E)]), (P, 1))], 1)
    half = np.arange(0, HD, 2, dtype=np.float32)
    f = 1.0 / np.float32(10000.0) ** (half / np.float32(HD))
    ang = (pos[:, None] * f[None, :]).astype(np.float32)
    ang = np.concatenate([ang, ang], -1)
    power = (pos - N // 2) / np.float32(W // 2)
    xs = ((half + np.float32(0.4 * HD)) / np.float32(1.4 * HD))[None, :] ** power[:, None]
    xs = np.concatenate([xs, xs], -1)
    sign = np.concatenate([-np.ones(HD // 2), np.ones(HD // 2)])
    tables = [np.cos(ang) * xs, np.sin(ang) * sign * xs, np.cos(ang) / xs, np.sin(ang) * sign / xs]
    xpos = np.stack([t.reshape(CH, P, HD).transpose(1, 0, 2) for t in tables], 1).astype(np.float32)
    j = np.arange(WIN)
    seen = (j[None, :] >= i[:, None]) & (j[None, :] <= i[:, None] + W)
    band = np.stack([np.where(seen & (j >= W)[None, :], 0.0, NEG), np.where(seen, 0.0, NEG)], 1)
    return {"route_c": route_c.astype(np.float32), "xpos": np.ascontiguousarray(xpos),
            "band": band.astype(np.float32),
            "ident": np.eye(P, dtype=np.float32), "mean_w": np.full((P, P), 1.0 / C, np.float32), "sel_sum": sel,
            "masks": masks, "rope": np.ascontiguousarray(rope)}


def layouts(a):
    h2p = heads_to_partitions
    turn = np.r_[D // 2:D, 0:D // 2]

    def turned(w):
        return w.reshape(*w.shape[:-1], H, D)[..., turn].reshape(w.shape)

    def heads(w):
        return np.tile(w, (1,) * (w.ndim - 1) + (H,))

    wq, wk, wv = a["L0_attn_Wq"], heads(a["L0_attn_Wk"]), heads(a["L0_attn_Wv"])
    bq, bk = a["L0_attn_bq"], heads(a["L0_attn_bk"])
    zero = np.zeros((C, C), np.float32)
    w1 = a["L1_attn_qkv_w"].T
    wqkv = np.stack([
        np.stack([h2p(wq), h2p(turned(wq)), h2p(wk), h2p(turned(wk)), wv, zero], 1),
        np.stack([h2p(w1[:, 0:C]), h2p(w1[:, C:2 * C]), w1[:, 2 * C:3 * C], zero, zero, zero], 1)], 1)
    temp = np.repeat(a["L1_attn_temperature"].reshape(H), D)
    pcol = np.stack([h2p(bq), h2p(turned(bq)), h2p(bk), h2p(turned(bk)), h2p(temp)], 1)

    def padded(w):
        out = np.zeros((UH, VW, UNITS, C), np.float32)
        out[:, 0:D] = w.reshape(UNITS, UH, D, C).transpose(1, 2, 0, 3)
        return out.reshape(P, UNITS, C)

    turn_l = np.r_[HD // 2:HD, 0:HD // 2]

    def columns(w, n, width=P):
        out = np.zeros((P, 2, n), np.float32)
        for c in range(n):
            part = w[:, c * width:(c + 1) * width]
            out[:part.shape[1], :, c] = part.T
        return out

    qs, ks = a["L1_ffn_q_scale"], a["L1_ffn_k_scale"]
    b1 = a["L1_ffn_b1"]
    lcol = np.concatenate(
        [columns(a["L1_ffn_ln_g"], 1), columns(a["L1_ffn_ln_b"], 1), columns(a["L1_ffn_b2"], 1),
         columns(b1[:, 0:HID], HC), columns(b1[:, HID:], HC)], 2)
    lw2 = np.zeros((P, 2, HC, C), np.float32)
    for c in range(HC):
        part = a["L1_ffn_w2"][:, c * P:(c + 1) * P]
        lw2[:part.shape[1], :, c] = part.transpose(1, 0, 2)
    return {
        "wg": a["L0_ffn_wg"], "ew1": a["L0_ffn_w1"],
        "ew2": a["L0_ffn_w2"].reshape(E, F // P, P, C).transpose(0, 2, 1, 3),
        "eb1": a["L0_ffn_b1"].reshape(E, F // P, P).transpose(0, 2, 1),
        "eb2": np.repeat(a["L0_ffn_b2"][:, None, :], P, 1),
        "lw": a["L1_ffn_wqkv"].transpose(1, 0, 2),
        "lqk": np.tile(np.stack([qs, qs[:, turn_l], ks, ks[:, turn_l]], 1), (P, 1, 1, 1)),
        "lwo": a["L1_ffn_wo"].reshape(2, PAIRS, P, C).transpose(2, 0, 1, 3),
        "lw1": a["L1_ffn_w1"].transpose(1, 0, 2), "lw2": lw2, "lcol": lcol,
        "xT": a["L0_attn_x"].transpose(0, 2, 1),
        "cT": np.stack([a["L0_c"].T, a["L1_c"].T], 1),
        "wmod": np.stack([a["L0_wmod"], a["L1_wmod"]], 1),
        "wqkv": wqkv, "pcol": pcol, "bv": np.tile(heads(a["L0_attn_bv"]), (P, 1)),
        "wo": np.stack([padded(a["L0_attn_Wo"]), padded(a["L1_attn_proj_w"].T)], 1),
        "bo": np.stack([a["L0_attn_bo"], a["L1_attn_proj_b"]], 1),
    }


def kernel(**inputs):
    import concourse.bacc as bacc
    from concourse.bass_utils import run_bass_kernel_spmd

    nc = bacc.Bacc("TRN2", target_bir_lowering=False, num_devices=1)
    data = {k: np.asarray(v) for k, v in inputs.items()}
    arrays = {f"in_{k}": np.ascontiguousarray(v) for k, v in {**constants(), **layouts(data)}.items()}
    ins = {k[3:]: nc.dram_tensor(k, v.shape, mybir.dt.from_np(v.dtype), kind="ExternalInput").ap()
           for k, v in arrays.items()}
    out = nc.dram_tensor("out_0", (B, C, N), F32, kind="ExternalOutput").ap()
    build(nc, ins, out)
    r = run_bass_kernel_spmd(nc, [arrays], core_ids=[0])
    return np.ascontiguousarray(r.results[0]["out_0"].transpose(0, 2, 1))
```

```python
import math
from contextlib import ExitStack, contextmanager

import numpy as np

import concourse.bass as bass
from concourse import mybir

F32 = mybir.dt.float32
BF16 = mybir.dt.bfloat16
I32 = mybir.dt.int32
ALU = mybir.AluOpType
ACT = mybir.ActivationFunctionType
AX = mybir.AxisListType

P = 128
B, N, C = 8, 512, 128
NT = B * N
H, D = 16, 8
UNITS = 4
UH = H // UNITS
CH = N // P
PARTS = 3
TERMS = PARTS * PARTS
RK = TERMS * D
RM = RK + PARTS
VW = 32
NEG = -1.0e30
E, F = 8, 512
CAP = NT * 5 // 4 // E
PAIRS, HD = 4, 64
INNER = 2 * PAIRS * HD
W = 64
WIN = W + P
HID = C * 4 * 2 // 3
HC = -(-HID // P)
QK_SCALE = 8.0
LN_EPS = 1e-5
L2_EPS = 1e-12


class Program:

    def __init__(self, nc, ctx, ins):
        self.nc, self.ctx, self.ins, self.sems = nc, ctx, ins, {}
        self.held = [ctx]
        self.attention_setups = 0
        self.count = 0

    def sb(self, name, shape, dt=F32):
        self.count += 1
        return self.held[-1].enter_context(self.nc.sbuf_tensor(f"{name}_sb{self.count}", shape, dt))

    @contextmanager
    def memory(self):
        with ExitStack() as held:
            self.held.append(held)
            yield
            self.held.pop()

    def sem(self, name):
        if name not in self.sems:
            self.sems[name] = self.ctx.enter_context(self.nc.semaphore(name))
        return self.sems[name]

    def dram(self, name, shape, dt=F32):
        return self.nc.dram_tensor(name, shape, dt, kind="Internal").ap()


def setup(g):
    nc, ins = g.nc, g.ins
    g.bank = [g.ctx.enter_context(nc.psum_tensor(f"bank{i}", [P, 512], F32)) for i in range(8)]
    g.ident = g.sb("ident", [P, P])
    g.identb = g.sb("identb", [P, P], BF16)
    g.mean_w = g.sb("mean_w", [P, P])
    g.sel_sum = g.sb("sel_sum", [P, UH])
    g.maskf = g.sb("maskf", [P, 2, P])
    g.mask = g.sb("mask", [P, 2, P], BF16)
    g.mod = g.sb("mod", [P, 6, 2 * B])
    cT = g.sb("cT", [P, 2, B])
    sil = g.sb("sil", [P, 2, B])
    tmp = g.sb("mod_tmp", [P, 4, 2 * B])
    wmod = g.sb("wmod", [P, 2, 6 * C])
    ld, prod = g.sem("setup_loaded"), g.sem("mod_products")
    v, ex = g.sem("setup_vector"), g.sem("exp_of_c")
    with nc.Block() as block:
        @block.sync
        def _(sp):
            for dst, src in ((g.ident[:, :], ins["ident"]), (g.mean_w[:, :], ins["mean_w"]),
                             (g.sel_sum[:, :], ins["sel_sum"]), (g.maskf[:, :, :], ins["masks"]),
                             (cT[:, :, :], ins["cT"]), (wmod[:, :, :], ins["wmod"])):
                sp.dma_start(dst, src).then_inc(ld, 16)

        @block.scalar
        def _(act):
            act.wait_ge(ld, 96)
            act.activation(sil[:, :, :], cT[:, :, :], ACT.Exp, scale=-1.0).then_inc(ex, 1)

        @block.tensor
        def _(pe):
            pe.wait_ge(ld, 96)
            pe.wait_ge(v, 5)
            for layer in range(2):
                for j in range(6):
                    at = 16 * j + 8 * layer
                    mm = pe.matmul(g.bank[0][:, at:at + B], wmod[:, layer, j * C:(j + 1) * C],
                                   sil[:, layer, :], start=(layer + j == 0), stop=True, skip_group_check=True)
            mm.then_inc(prod, 1)

        @block.vector
        def _(dve):
            n = 0

            def step(ins_):
                nonlocal n
                n += 1
                ins_.then_inc(v, 1)
                dve.wait_ge(v, n)

            dve.wait_ge(ld, 96)
            step(dve.tensor_copy(g.identb[:, :], g.ident[:, :]))
            step(dve.tensor_copy(g.mask[:, :, :], g.maskf[:, :, :]))
            dve.wait_ge(ex, 1)
            step(dve.tensor_scalar(sil[:, :, :], sil[:, :, :], 1.0, None, ALU.add))
            step(dve.reciprocal(sil[:, :, :], sil[:, :, :]))
            step(dve.tensor_tensor(sil[:, :, :], sil[:, :, :], cT[:, :, :], ALU.mult))
            dve.wait_ge(prod, 1)
            step(dve.tensor_copy(g.mod[:, :, :], g.bank[0][:, 0:96].rearrange("p (j b) -> p j b", j=6)))
            for j in (1, 4):
                step(dve.tensor_scalar(g.mod[:, j, :], g.mod[:, j, :], 1.0, None, ALU.add))
            for j in (2, 5):
                step(dve.tensor_scalar(tmp[:, 0, :], g.mod[:, j, :], 0.0, 2.0, ALU.is_ge, ALU.mult))
                step(dve.tensor_scalar(tmp[:, 1, :], tmp[:, 0, :], -1.0, None, ALU.add))
                step(dve.scalar_tensor_tensor(out=tmp[:, 2, :], in0=g.mod[:, j, :], scalar=-1.0, in1=g.mod[:, j, :],
                                              op0=ALU.mult, op1=ALU.max))
                step(dve.scalar_tensor_tensor(out=g.mod[:, j, :], in0=tmp[:, 2, :], scalar=0.25, in1=tmp[:, 1, :],
                                              op0=ALU.max, op1=ALU.mult))


def setup_projection(g):
    nc = g.nc
    g.wq = g.sb("wq", [P, 2, 6, C])
    g.pcol = g.sb("pcol", [P, 6])
    g.rope = g.sb("rope", [P, 2, N])
    g.bv = g.sb("bv", [P, C])
    g.ones_w = g.sb("ones_w", [P, P])
    g.minus_half = g.sb("minus_half", [P, 2 * CH])
    g.x_in = g.sb("x_in", [P, N])
    g.xc = g.sb("xc", [P, N])
    g.xn = g.sb("x_norm", [P, 2, N])
    g.xnc = g.sb("xc_norm", [P, 2, N])
    g.nvar = g.sb("n_var", [P, CH])
    g.nrstd = g.sb("n_rstd", [P, CH])
    g.nspread = g.sb("n_spread", [P, CH, P])
    g.sq = g.sb("sq", [P, N])
    g.std = g.sb("std", [P, N])
    g.rstd = g.sb("rstd", [P, N])
    g.xh = g.sb("xh", [P, N])
    g.h = g.sb("h", [P, N])
    g.ra = g.sb("ra", [P, 2, N])
    g.rb = g.sb("rb", [P, 2, N])
    g.qk = g.sb("qk", [P, 4, N])
    g.res = g.sb("res", [P, 2, N])
    g.l2 = g.sb("l2", [P, 2 * CH])
    g.l2inv = g.sb("l2_inv", [P, 2 * CH])
    g.l2spread = g.sb("l2_spread", [P, 2 * CH, P])
    g.parts = g.sb("parts", [P, 2, PARTS, N], BF16)
    g.vpad = g.sb("vpad", [P, CH, H, VW])
    g.ns = {n: g.sem("n_" + n) for n in (
        "x_loaded0", "x_loaded1", "mean", "xc", "sq", "var", "veps", "rstd", "spread", "rstd_psum", "xh", "h")}
    g.ps = {n: g.sem("p_" + n) for n in (
        "setup", "setup_dve", "qk_psum", "v_psum", "ra", "rb", "rot", "l2_sq", "l2_sums", "l2_clip", "l2_inv",
        "l2_spread", "l2_psum", "part1", "res1", "part2", "part3", "parts_stored", "v_stored", "v_padded")}
    s = g.ps
    with nc.Block() as block:
        @block.sync
        def _(sp):
            for dst, src in ((g.wq[:, :, :, :], g.ins["wqkv"]), (g.pcol[:, 0:5], g.ins["pcol"]),
                             (g.rope[:, :, :], g.ins["rope"]), (g.bv[:, :], g.ins["bv"])):
                sp.dma_start(dst, src).then_inc(s["setup"], 16)

        @block.gpsimd
        def _(pool):
            pool.memset(g.ones_w[:, :], 1.0)
            pool.memset(g.minus_half[:, :], -0.5).then_inc(s["part3"], 2)
            pool.memset(g.vpad[:, :, :, :], 0.0).then_inc(s["v_padded"], 1)
            pool.wait_ge(s["v_padded"], 1)
            pool.memset(g.vpad[:, :, :, D:D + 1], 1.0)

        @block.vector
        def _(dve):
            dve.wait_ge(s["setup"], 64)
            dve.reciprocal(g.pcol[:, 5:6], g.pcol[:, 4:5]).then_inc(s["setup_dve"], 1)
            dve.wait_ge(s["setup_dve"], 1)
            dve.tensor_scalar(g.pcol[:, 5:6], g.pcol[:, 5:6], 1.0 / D, None, ALU.mult)


def paired(engine, lo, hi, batch):
    with engine.Fori(0, (hi - lo) // 2 - 1) as j:
        for slot in range(2):
            batch(j * 2 + (lo + slot), slot, False)
    batch(hi - 2, 0, False)
    batch(hi - 1, 1, True)


def norm_load(g, sp, m, slot, x):
    sp.dma_start(g.xn[:, slot, :], x).then_inc(g.ns[f"x_loaded{slot}"], 16)


def norm_mean(g, pe, m, slot):
    s = g.ns
    pe.wait_ge(s[f"x_loaded{slot}"], m * 8 + (16 - 8 * slot))
    pe.wait_ge(s["xc"], m)
    pe.matmul(g.bank[0][:, :], g.mean_w[:, :], g.xn[:, slot, :], start=True, stop=True).then_inc(s["mean"], 1)


def norm_center(g, dve, m, slot):
    s = g.ns
    dve.wait_ge(s["mean"], m + 1)
    if not isinstance(m, int) or m:
        dve.wait_ge(s["xh"], m - 1)
    dve.tensor_tensor(g.xnc[:, slot, :], g.xn[:, slot, :], g.bank[0][:, :], ALU.subtract).then_inc(s["xc"], 1)


def norm_square(g, act, m, slot):
    s = g.ns
    act.wait_ge(s["xc"], m + 1)
    act.wait_ge(s["var"], m)
    act.activation(g.sq[:, :], g.xnc[:, slot, :], ACT.Square).then_inc(s["sq"], 1)


def norm_variance(g, pe, m):
    s = g.ns
    pe.wait_ge(s["sq"], m + 1)
    pe.wait_ge(s["xh"], m)
    for c in range(CH):
        mm = pe.matmul(g.bank[1][:, c:c + 1], g.sq[:, c * P:(c + 1) * P], g.mean_w[:, 0:1],
                       start=True, stop=True, skip_group_check=True)
    mm.then_inc(s["var"], 1)


def norm_epsilon(g, dve, m):
    s = g.ns
    dve.wait_ge(s["var"], m + 1)
    dve.wait_ge(s["rstd"], m)
    dve.tensor_scalar(g.nvar[:, :], g.bank[1][:, 0:CH], LN_EPS, None, ALU.add).then_inc(s["veps"], 1)


def norm_power(g, pool, m):
    s = g.ns
    pool.wait_ge(s["veps"], m + 1)
    pool.wait_ge(s["spread"], m)
    pool.tensor_tensor(g.nrstd[:, :], g.nvar[:, :], g.minus_half[:, 0:CH], ALU.pow).then_inc(s["rstd"], 1)


def norm_repeat(g, dve, m):
    s = g.ns
    dve.wait_ge(s["rstd"], m + 1)
    dve.wait_ge(s["rstd_psum"], m)
    dve.tensor_copy(g.nspread[:, :, :], g.nrstd[:, :].unsqueeze(2).broadcast_to([P, CH, P]))\
       .then_inc(s["spread"], 1)


def norm_spread(g, pe, m):
    s = g.ns
    pe.wait_ge(s["spread"], m + 1)
    for c in range(CH):
        mm = pe.matmul(g.bank[1][:, c * P:(c + 1) * P], g.nspread[:, c, :], g.ident[:, :],
                       start=True, stop=True, skip_group_check=True)
    mm.then_inc(s["rstd_psum"], 1)


def norm_finish(g, dve, m, slot, scale, shift, col, readers):
    s = g.ns
    dve.wait_ge(s["rstd_psum"], m + 1)
    dve.wait_ge(s["h"], m)
    dve.tensor_tensor(g.xh[:, :], g.xnc[:, slot, :], g.bank[1][:, :], ALU.mult).then_inc(s["xh"], 1)
    dve.wait_ge(s["xh"], m + 1)
    for sem, value in readers:
        dve.wait_ge(sem, value)
    at = slice(col, col + 1) if isinstance(col, int) else bass.ds(col, 1)
    dve.tensor_scalar(g.h[:, :], g.xh[:, :], g.mod[:, scale, at], g.mod[:, shift, at], ALU.mult, ALU.add)\
       .then_inc(s["h"], 1)


def project(g, layer, x):
    nc, s = g.nc, g.ps
    lo, hi = B * layer, B * (layer + 1)
    base = B * layer

    def qk_bank(slot, w):
        return g.bank[2 + 2 * slot + w]

    with nc.Block() as block:
        @block.sync
        def _(sp):
            def batch(it, slot, last):
                if not isinstance(it, int):
                    sp.wait_ge(g.ns["xc"], it + (base + 1))
                    norm_load(g, sp, it + (base + 2), slot, x[it + (2 - lo)])
                sp.wait_ge(s["v_stored"], it * 17 + 1)
                sp.dma_start(g.v_dram[it].rearrange("c p m -> p c m"),
                             g.vpad[:, :, :, :].rearrange("p c h w -> p c (h w)")).then_inc(s["v_stored"], 16)
                for w in range(2):
                    sp.wait_ge(s["part3"], it * 2 + w + 3)
                    for part in range(PARTS):
                        sp.dma_start(g.qk_dram[it, w, :, part].rearrange("u d h n -> u (d h) n"),
                                     g.parts[:, w, part, :]).then_inc(s["parts_stored"], 16)

            for slot in range(2):
                norm_load(g, sp, lo + base + slot, slot, x[slot])
            paired(sp, lo, hi, batch)
            sp.wait_ge(s["parts_stored"], hi * 2 * PARTS * 16)
            sp.wait_ge(s["v_stored"], hi * 17)

        @block.tensor
        def _(pe):
            def columns(bank, at, tile):
                for c in range(CH):
                    mm = pe.matmul(bank[:, at + c:at + c + 1], tile[:, c * P:(c + 1) * P], g.ones_w[:, 0:1],
                                   start=True, stop=True, skip_group_check=True)
                return mm

            def batch(it, slot, last):
                nx = it + (base + 1)
                if not last:
                    norm_mean(g, pe, nx, slot ^ 1)
                pe.wait_ge(g.ns["h"], nx)
                if layer == 0:
                    for m in range(4):
                        pe.wait_ge(s["ra"] if m % 2 == 0 else s["rb"], it * 2)
                        pe.matmul(g.bank[2 + m][:, :], g.wq[:, 0, m, :], g.h[:, :],
                                  start=True, stop=True).then_inc(s["qk_psum"], 1)
                        if m == 1 and not last:
                            norm_variance(g, pe, nx)
                else:
                    for w in range(2):
                        pe.wait_ge(s["rot"], it * 2 - 2)
                        pe.matmul(qk_bank(slot, w)[:, :], g.wq[:, 1, w, :], g.h[:, :],
                                  start=True, stop=True).then_inc(s["qk_psum"], 2)
                    if not last:
                        norm_variance(g, pe, nx)
                pe.wait_ge(s["v_stored"], it * 17)
                for c in range(CH):
                    mm = pe.matmul(g.bank[6][:, c * C:(c + 1) * C], g.h[:, c * P:(c + 1) * P],
                                   g.wq[:, layer, 4 if layer == 0 else 2, :], start=(c == 0), stop=True,
                                   skip_group_check=True)
                mm.then_inc(s["v_psum"], 1)
                if layer == 1:
                    pe.wait_ge(s["rb"], it * 2)
                    for w in range(2):
                        pe.wait_ge(s["l2_sq"], (it - lo) * 2 + w + 1)
                        mm = columns(g.bank[7], CH * w, g.ra[:, w, :])
                    mm.then_inc(s["l2_sums"], 1)
                if not last:
                    norm_spread(g, pe, nx)
                if layer == 1:
                    for w in range(2):
                        pe.wait_ge(s["l2_spread"], (it - lo) * 2 + w + 1)
                        if w == 1:
                            pe.wait_ge(s["rb"], it * 2 + 1)
                        for c in range(CH):
                            mm = pe.matmul(g.bank[7][:, c * P:(c + 1) * P], g.l2spread[:, CH * w + c, :],
                                           g.ident[:, :], start=True, stop=True, skip_group_check=True)
                        mm.then_inc(s["l2_psum"], 1)

            norm_mean(g, pe, lo + base, 0)
            norm_variance(g, pe, lo + base)
            norm_spread(g, pe, lo + base)
            paired(pe, lo, hi, batch)

        ahead = 1 + layer

        def norm_ahead(link, it, slot, last):
            if not last if layer == 0 else not isinstance(it, int):
                link(it + (base + ahead), (slot + ahead) % 2)

        @block.scalar
        def _(act):
            def squares(it, slot):
                if layer == 1:
                    for w in range(2):
                        act.wait_ge(s["qk_psum"], it * 4 + 2 * w + 2)
                        act.wait_ge(s["l2_sums"], it - lo)
                        act.activation(g.ra[:, w, :], qk_bank(slot, w)[:, :], ACT.Square).then_inc(s["l2_sq"], 1)

            def square(m, slot):
                norm_square(g, act, m, slot)

            def batch(it, slot, last):
                if layer == 0:
                    norm_ahead(square, it, slot, last)
                for w in range(2):
                    act.wait_ge(s["rot"], it * 2 + w + 1)
                    act.wait_ge(s["parts_stored"], it * 2 * PARTS * 16)
                    act.activation(g.parts[:, w, 0, :], g.qk[:, 2 * slot + w, :], ACT.Copy).then_inc(s["part1"], 1)
                if layer == 1:
                    norm_ahead(square, it, slot, last)
                    if not last:
                        squares(it + 1, slot ^ 1)
                for w in range(2):
                    act.wait_ge(s["res1"], it * 2 + w + 1)
                    act.activation(g.parts[:, w, 1, :], g.res[:, w, :], ACT.Copy).then_inc(s["part2"], 1)

            for slot in range(ahead):
                norm_square(g, act, lo + base + slot, slot)
            squares(lo, 0)
            paired(act, lo, hi, batch)

        @block.gpsimd
        def _(pool):
            def power(it):
                if layer == 1:
                    pool.wait_ge(s["l2_clip"], it - (lo - 1))
                    pool.wait_ge(s["l2_spread"], (it - lo) * 2)
                    pool.tensor_tensor(g.l2inv[:, :], g.l2[:, :], g.minus_half[:, :], ALU.pow)\
                        .then_inc(s["l2_inv"], 1)

            def power_norm(m, slot):
                norm_power(g, pool, m)

            def batch(it, slot, last):
                if layer == 0:
                    norm_ahead(power_norm, it, slot, last)
                for w in range(2):
                    pool.wait_ge(s["part1"], it * 2 + w + 1)
                    pool.wait_ge(s["part3"], it * 2 + 2)
                    pool.tensor_tensor(g.res[:, w, :], g.qk[:, 2 * slot + w, :], g.parts[:, w, 0, :],
                                       ALU.subtract).then_inc(s["res1"], 1)
                if layer == 1:
                    norm_ahead(power_norm, it, slot, last)
                    if not last:
                        power(it + 1)
                for w in range(2):
                    pool.wait_ge(s["part2"], it * 2 + w + 1)
                    pool.tensor_tensor(g.parts[:, w, 2, :], g.res[:, w, :], g.parts[:, w, 1, :],
                                       ALU.subtract).then_inc(s["part3"], 1)

            for slot in range(ahead):
                norm_power(g, pool, lo + base + slot)
            power(lo)
            paired(pool, lo, hi, batch)

        @block.vector
        def _(dve):
            def rotate(it, w, slot):
                dve.wait_ge(s["qk_psum"], it * 4 + 2 * w + 1)
                dve.wait_ge(s["rot"], it * 2)
                dve.scalar_tensor_tensor(out=g.ra[:, w, :], in0=g.bank[2 + 2 * w][:, :],
                                         scalar=g.pcol[:, 2 * w:2 * w + 1], in1=g.rope[:, 0, :],
                                         op0=ALU.add, op1=ALU.mult).then_inc(s["ra"], 1)
                dve.wait_ge(s["qk_psum"], it * 4 + 2 * w + 2)
                dve.scalar_tensor_tensor(out=g.rb[:, w, :], in0=g.bank[3 + 2 * w][:, :],
                                         scalar=g.pcol[:, 2 * w + 1:2 * w + 2], in1=g.rope[:, 1, :],
                                         op0=ALU.add, op1=ALU.mult).then_inc(s["rb"], 1)
                dve.wait_ge(s["ra"], it * 2 + w + 1)
                dve.wait_ge(s["rb"], it * 2 + w + 1)
                dve.wait_ge(s["part3"], it * 2)
                dve.tensor_tensor(g.qk[:, 2 * slot + w, :], g.ra[:, w, :], g.rb[:, w, :], ALU.add).then_inc(s["rot"], 1)

            def clip_norms(it):
                dve.wait_ge(s["l2_sums"], it - (lo - 1))
                dve.wait_ge(s["l2_inv"], it - lo)
                dve.tensor_scalar(g.l2[:, :], g.bank[7][:, 0:2 * CH], L2_EPS * L2_EPS, None, ALU.max)\
                   .then_inc(s["l2_clip"], 1)

            def repeat_norms(it, w):
                dve.wait_ge(s["l2_inv"], it - (lo - 1))
                dve.wait_ge(s["l2_psum"], (it - lo) * 2)
                dve.tensor_copy(g.l2spread[:, CH * w:CH * (w + 1), :],
                                g.l2inv[:, CH * w:CH * (w + 1)].unsqueeze(2).broadcast_to([P, CH, P]))\
                   .then_inc(s["l2_spread"], 1)

            def over_norm(it, w, slot):
                dve.wait_ge(s["l2_psum"], (it - lo) * 2 + w + 1)
                dve.wait_ge(s["rb"], it * 2 + w)
                dve.tensor_copy(g.rb[:, w, :], g.bank[7][:, :]).then_inc(s["rb"], 1)
                dve.wait_ge(s["rb"], it * 2 + w + 1)
                dve.wait_ge(s["part3"], it * 2)
                dve.scalar_tensor_tensor(out=g.qk[:, 2 * slot + w, :], in0=qk_bank(slot, w)[:, :],
                                         scalar=g.pcol[:, 5:6] if w == 0 else 1.0, in1=g.rb[:, w, :],
                                         op0=ALU.mult, op1=ALU.mult).then_inc(s["rot"], 1)

            def copy_v(it):
                dve.wait_ge(s["v_psum"], it + 1)
                dve.wait_ge(s["v_stored"], it * 17)
                psum = g.bank[6][:, :].rearrange("p (c h d) -> p c h d", c=CH, d=D)
                out = g.vpad[:, :, :, 0:D]
                if layer == 0:
                    bv = g.bv[:, :].rearrange("p (h d) -> p h d", d=D)
                    for c in range(CH):
                        last = dve.tensor_tensor(out[:, c], psum[:, c], bv, ALU.add)
                else:
                    last = dve.tensor_copy(out, psum)
                last.then_inc(s["v_stored"], 1)

            def finish(it, nx, slot):
                norm_finish(g, dve, nx, slot, 1, 0, it + 1, [(s["v_psum"], it + 1)])

            def batch(it, slot, last):
                nx = it + (base + 1)
                if not last:
                    norm_center(g, dve, nx, slot ^ 1)
                if layer == 0:
                    rotate(it, 0, slot)
                    if not last:
                        norm_epsilon(g, dve, nx)
                    rotate(it, 1, slot)
                    if not last:
                        norm_repeat(g, dve, nx)
                    copy_v(it)
                else:
                    if not last:
                        norm_epsilon(g, dve, nx)
                    clip_norms(it)
                    copy_v(it)
                    if not last:
                        norm_repeat(g, dve, nx)
                    for w in range(2):
                        repeat_norms(it, w)
                    if not last:
                        finish(it, nx, slot ^ 1)
                    for w in range(2):
                        over_norm(it, w, slot)
                if layer == 0 and not last:
                    finish(it, nx, slot ^ 1)

            norm_center(g, dve, lo + base, 0)
            norm_epsilon(g, dve, lo + base)
            norm_repeat(g, dve, lo + base)
            norm_finish(g, dve, lo + base, 0, 1, 0, lo, [])
            paired(dve, lo, hi, batch)


def setup_attention(g):
    nc = g.nc
    g.Q = g.sb("Q", [RM, UNITS, UH, N], BF16)
    g.K = g.sb("K", [RM, UNITS, UH, N], BF16)
    g.V = g.sb("V", [P, UNITS, CH, UH * VW])
    g.wo = g.sb("wo", [P, 2, UNITS, C])
    g.bo = g.sb("bo", [P, 2])
    g.M = g.sb("M", [P, 2, CH, UH])
    g.mneg = g.sb("mneg", [UH, N])
    g.mres = g.sb("mres", [UH, N])
    g.mparts = g.sb("mparts", [UH, PARTS, N], BF16)
    g.probs = g.sb("probs", [P, 2, UH, N])
    g.osum = g.sb("osum", [P, N])
    g.rsum = g.sb("rsum", [P, CH * UH])
    g.rspread = g.sb("rspread", [P, CH * UH, VW])
    g.onorm = g.sb("onorm", [P, N])
    g.xres = g.sb("xres", [P, N])
    g.ytmp = g.sb("ytmp", [P, N])
    g.xnew = g.sb("xnew", [P, N])
    g.as_ = {n: g.sem("a_" + n) for n in (
        "setup", "a_scores", "a_max", "max_turned", "mneg", "mres", "mpart2", "mpart3", "m_stored",
        "m_loaded", "b_scores", "exp", "pv", "o_copied", "sums", "rsum", "rspread", "spread", "onorm", "yacc", "x_loaded", "ytmp", "xnew",
        "x_stored")}
    g.loaded = [g.sem(f"a_loaded{i}") for i in range(UNITS)]
    g.attention_setups += 1
    n_setup = g.attention_setups
    with nc.Block() as block:
        @block.sync
        def _(sp):
            sp.dma_start(g.wo[:, :, :, :], g.ins["wo"]).then_inc(g.as_["setup"], 16)
            sp.dma_start(g.bo[:, :], g.ins["bo"]).then_inc(g.as_["setup"], 16)
            sp.wait_ge(g.as_["setup"], 32 * n_setup)

        @block.gpsimd
        def _(pool):
            pool.memset(g.K[64:RM, :, :, :], 1.0)


def attend(g, layer, x, x_out):
    nc, s = g.nc, g.as_
    causal = layer == 0
    lo, hi = B * layer, B * (layer + 1)
    per = CH * UH
    scale = float(D) ** -0.5 if causal else 1.0
    SA, SB, OB, MB, YB = g.bank[0:3], g.bank[3:5], g.bank[5], g.bank[6], g.bank[7]
    hk = (lambda h: 0) if causal else (lambda h: h)
    LOADS = 13 * 16

    def first_query(k):
        return P * k if causal else 0

    def batches(engine, batch):
        batch(lo, True, False)
        with engine.Fori(lo + 1, hi - 1) as i:
            batch(i, False, False)
        batch(hi - 1, False, True)

    def a_unit(q, last):
        return q + 2 if not (last and q >= 2) else None

    def m_unit(q, first, last):
        return q + 1 if not (first and q == 0) and not (last and q == UNITS - 1) else None

    with nc.Block() as block:
        @block.sync
        def _(sp):
            def load(i, u):
                it, q = (i, u) if u < UNITS else (i + 1, u - UNITS)
                slot = q
                for part in range(PARTS):
                    src = g.qk_dram[it, 0, q, part].rearrange("d h n -> d (h n)")
                    for t in range(PARTS):
                        r = (PARTS * part + t) * D
                        sp.dma_start(g.Q[r:r + D, slot, :, :].rearrange("d h n -> d (h n)"), src)\
                          .then_inc(g.loaded[slot], 16)
                    src = g.qk_dram[it, 1, q].rearrange("s d h n -> (s d) h n")
                    r = PARTS * part * D
                    if causal:
                        sp.dma_start(g.K[r:r + PARTS * D, slot, 0, :], src[:, 0, :]).then_inc(g.loaded[slot], 16)
                    else:
                        sp.dma_start(g.K[r:r + PARTS * D, slot, :, :], src).then_inc(g.loaded[slot], 16)
                sp.dma_start(g.V[:, slot, :, :], g.v_dram[it].rearrange(
                    "c p (u m) -> p c u m", u=UNITS)[:, :, q, :]).then_inc(g.loaded[slot], 16)

            def move_max(i, u):
                at = i * 4 + u
                sp.wait_ge(s["mpart3"], at + 1)
                sp.dma_start(g.m_dram, g.mparts[:, :, :]).then_inc(s["m_stored"], 16)
                sp.wait_ge(s["m_stored"], at * 16 + 16)
                sp.dma_start(g.Q[RK:RM, u % UNITS, :, :], g.m_dram.rearrange("h s n -> s h n"))\
                    .then_inc(s["m_loaded"], 16)

            def store(i):
                sp.wait_ge(s["xnew"], i)
                sp.dma_start(x_out[i - lo - 1], g.xnew[:, :]).then_inc(s["x_stored"], 16)

            def batch(i, first, last):
                for q in range(UNITS):
                    if not last or q == 0:
                        if not (first and q == 0):
                            sp.wait_ge(s["pv"], i * 16 + 4 * q)
                        load(i, q + 3)
                    u = m_unit(q, first, last)
                    if u is not None:
                        move_max(i, u)
                    if q == 2:
                        if not first:
                            store(i)
                        sp.dma_start(g.xres[:, :], x[i - lo]).then_inc(s["x_loaded"], 16)

            for u in range(3):
                load(lo, u)
            for u in range(2):
                move_max(lo, u)
            batches(sp, batch)
            store(hi)
            sp.wait_ge(s["x_stored"], hi * 16)

        @block.tensor
        def _(pe):
            def a_tile(i, u, k, h):
                n = u * per + k * UH + h
                slot, ring = u % UNITS, n % (UNITS * per)
                out = SA[ring % 3]
                width = P * (k + 1) if causal else N
                if k + h == 0:
                    pe.wait_ge(g.loaded[slot], (i + u // UNITS) * LOADS + LOADS)
                if ring >= 3:
                    pe.wait_ge(s["a_max"], i * 64 + n - 2)
                elif ring == 0 and (u or lo):
                    pe.wait_ge(s["a_max"], i * 64 + n)
                mm = pe.matmul(out[:, 0:width], g.Q[0:RK, slot, h, k * P:(k + 1) * P],
                               g.K[0:RK, slot, hk(h), 0:width], start=True, stop=not causal)
                if causal:
                    mm = pe.matmul(out[:, width - P:width], g.identb[:, :], g.mask[:, 0, :], start=False, stop=True)
                mm.then_inc(s["a_scores"], 1)

            def turn_max(i, u):
                pe.wait_ge(s["a_max"], i * 64 + (u + 1) * per)
                pe.wait_ge(s["mneg"], 2 * (i * 4 + u))
                if u >= 2:
                    pe.wait_ge(s["onorm"], i * 4 + u - 2)
                for k in range(CH):
                    mm = pe.transpose(MB[0:UH, k * P:(k + 1) * P], g.M[:, u % 2, k, :], g.ident[:, :])
                mm.then_inc(s["max_turned"], 1)

            def b_tile(i, q, k, h):
                n = q * per + k * UH + h
                t0 = first_query(k)
                if k + h == 0:
                    pe.wait_ge(s["m_loaded"], i * 64 + 16 * q + 16)
                if n >= 2 or not isinstance(i, int) or i:
                    pe.wait_ge(s["exp"], i * 64 + n - 1)
                mm = pe.matmul(SB[n % 2][:, t0:N], g.K[0:RM, q, hk(h), k * P:(k + 1) * P],
                               g.Q[0:RM, q, h, t0:N], start=True, stop=not causal)
                if causal:
                    mm = pe.matmul(SB[n % 2][:, t0:t0 + P], g.identb[:, :], g.mask[:, 1, :], start=False, stop=True)
                mm.then_inc(s["b_scores"], 1)

            def pv(i, q, k):
                t0 = first_query(k)
                slot = q % UNITS
                pe.wait_ge(s["exp"], i * 64 + q * per + (k + 1) * UH)
                if k == 0:
                    pe.wait_ge(s["o_copied"], i * 4 + q)
                for h in range(UH):
                    mm = pe.matmul(OB[VW * h:VW * (h + 1), t0:N], g.V[:, slot, k, VW * h:VW * (h + 1)],
                                   g.probs[:, k % 2, h, t0:N], start=(k == 0), stop=(k == CH - 1),
                                   skip_group_check=True)
                mm.then_inc(s["pv"], 1)

            def turn_sums(i, q, m):
                pe.wait_ge(s["o_copied"], i * 4 + q + 1)
                pe.wait_ge(s["onorm"], i * 4 + q)
                if m is not None:
                    pe.wait_ge(s["mneg"], 2 * (i * 4 + m + 1))
                for k in range(CH):
                    mm = pe.matmul(MB[:, UH * k:UH * (k + 1)], g.osum[:, k * P:(k + 1) * P], g.sel_sum[:, :],
                                   start=True, stop=True, skip_group_check=True)
                mm.then_inc(s["sums"], 1)

            def spread_inverses(i, q):
                pe.wait_ge(s["rspread"], i * 4 + q + 1)
                for k in range(CH):
                    mm = pe.matmul(MB[:, k * P:(k + 1) * P],
                                   g.rspread[:, UH * k:UH * (k + 1), :].rearrange("p h w -> p (h w)"), g.ident[:, :],
                                   start=True, stop=True, skip_group_check=True)
                mm.then_inc(s["spread"], 1)

            def out_project(i, q):
                w = q % UNITS
                pe.wait_ge(s["onorm"], i * 4 + q + 1)
                if w == 0:
                    pe.wait_ge(s["ytmp"], i)
                pe.matmul(YB[:, :], g.wo[:, layer, w, :], g.onorm[:, :], start=(w == 0), stop=(w == UNITS - 1),
                          skip_group_check=True).then_inc(s["yacc"], 1)

            def batch(i, first, last):
                for q in range(UNITS):
                    u, m = a_unit(q, last), m_unit(q, first, last)
                    for k in range(CH):
                        for h in range(UH):
                            if u is not None:
                                a_tile(i, u, k, h)
                            b_tile(i, q, k, h)
                            if (k, h) == (0, 1) and m is not None:
                                turn_max(i, m)
                            if h == 1 and k:
                                pv(i, q, k - 1)
                            elif h == 1 and not (first and q == 0):
                                pv(i, q - 1, CH - 1)
                            if (k, h) == (0, 3) and not (first and q < 2):
                                out_project(i, q - 2)
                            if (k, h) == (2, 0) and not (first and q == 0):
                                turn_sums(i, q - 1, m)
                            if (k, h) == (2, 3) and not (first and q == 0):
                                spread_inverses(i, q - 1)

            for u in range(2):
                for k in range(CH):
                    for h in range(UH):
                        a_tile(lo, u, k, h)
                turn_max(lo, u)
            batches(pe, batch)
            pv(hi, -1, CH - 1)
            out_project(hi, -2)
            turn_sums(hi, -1, None)
            spread_inverses(hi, -1)
            out_project(hi, -1)

        @block.scalar
        def _(act):
            def exp(i, q, k, h):
                n = q * per + k * UH + h
                t0 = first_query(k)
                if h == 0 and (q * CH + k >= 2 or not isinstance(i, int) or i):
                    act.wait_ge(s["pv"], i * 16 + q * CH + k - 1)
                act.wait_ge(s["b_scores"], i * 64 + n + 1)
                act.activation(g.probs[:, k % 2, h, t0:N], SB[n % 2][:, t0:N], ACT.Exp, scale=scale)\
                   .then_inc(s["exp"], 1)

            def negate(i, u):
                act.wait_ge(s["max_turned"], i * 4 + u + 1)
                act.wait_ge(s["mpart3"], i * 4 + u)
                act.activation(g.mneg[:, :], MB[0:UH, :], ACT.Copy, scale=-1.0).then_inc(s["mneg"], 1)

            def first_part(i, u):
                act.wait_ge(s["max_turned"], i * 4 + u + 1)
                act.wait_ge(s["m_stored"], (i * 4 + u) * 16)
                act.activation(g.mparts[:, 0, :], MB[0:UH, :], ACT.Copy, scale=-1.0).then_inc(s["mneg"], 1)

            def copy_out(i, q):
                act.wait_ge(s["pv"], i * 16 + 4 * q + 4)
                act.wait_ge(s["onorm"], i * 4 + q)
                act.activation(g.osum[:, :], OB[:, :], ACT.Copy).then_inc(s["o_copied"], 1)

            def batch(i, first, last):
                for q in range(UNITS):
                    m = m_unit(q, first, last)
                    for k in range(CH):
                        for h in range(UH):
                            exp(i, q, k, h)
                            if not (first and q == 0):
                                if (k, h) == (0, 3):
                                    copy_out(i, q - 1)
                            if m is not None:
                                if (k, h) == (0, 1):
                                    negate(i, m)
                                if (k, h) == (0, 2):
                                    first_part(i, m)

            for u in range(2):
                negate(lo, u)
                first_part(lo, u)
            batches(act, batch)
            copy_out(hi, -1)

        @block.gpsimd
        def _(pool):
            def split_max(i, u):
                at = i * 4 + u
                pool.wait_ge(s["mneg"], 2 * at + 2)
                pool.wait_ge(s["mpart3"], at)
                pool.tensor_tensor(g.mres[:, :], g.mneg[:, :], g.mparts[:, 0, :], ALU.subtract).then_inc(s["mres"], 1)
                pool.wait_ge(s["m_stored"], at * 16)
                pool.tensor_tensor(g.mparts[:, 1, :], g.mneg[:, :], g.mparts[:, 0, :], ALU.subtract)\
                    .then_inc(s["mpart2"], 1)
                pool.wait_ge(s["mres"], at + 1)
                pool.wait_ge(s["mpart2"], at + 1)
                pool.wait_ge(s["m_loaded"], at * 16)
                pool.tensor_tensor(g.mparts[:, 2, :], g.mres[:, :], g.mparts[:, 1, :], ALU.subtract)\
                    .then_inc(s["mpart3"], 1)

            def residual(i):
                pool.wait_ge(s["ytmp"], i)
                pool.wait_ge(s["x_loaded"], i * 16)
                pool.wait_ge(s["x_stored"], (i - 1) * 16)
                pool.tensor_tensor(g.xnew[:, :], g.ytmp[:, :], g.xres[:, :], ALU.add).then_inc(s["xnew"], 1)

            def batch(i, first, last):
                for q in range(UNITS):
                    m = m_unit(q, first, last)
                    if m is not None:
                        split_max(i, m)
                    if q == 1 and not first:
                        residual(i)

            for u in range(2):
                split_max(lo, u)
            batches(pool, batch)
            residual(hi)

        @block.vector
        def _(dve):
            def maxima(i, u, k, h):
                n = u * per + k * UH + h
                ring = n % (UNITS * per)
                width = P * (k + 1) if causal else N
                if k + h == 0 and (u >= 2 or lo):
                    dve.wait_ge(s["max_turned"], i * 4 + u - 1)
                dve.wait_ge(s["a_scores"], i * 64 + n + 1)
                dve.reduce_max(g.M[:, u % 2, k, h:h + 1], SA[ring % 3][:, 0:width], AX.X).then_inc(s["a_max"], 1)

            def invert_sums(i, q):
                dve.wait_ge(s["sums"], i * 4 + q + 1)
                dve.wait_ge(s["rspread"], i * 4 + q)
                dve.reciprocal(g.rsum[:, :], MB[:, 0:CH * UH]).then_inc(s["rsum"], 1)
                dve.wait_ge(s["rsum"], i * 4 + q + 1)
                dve.wait_ge(s["spread"], i * 4 + q)
                dve.tensor_copy(g.rspread[:, :, :], g.rsum[:, :].unsqueeze(2).broadcast_to([P, CH * UH, VW]))\
                   .then_inc(s["rspread"], 1)

            def normalise(i, q):
                dve.wait_ge(s["spread"], i * 4 + q + 1)
                dve.wait_ge(s["yacc"], i * 4 + q)
                dve.tensor_tensor(g.onorm[:, :], g.osum[:, :], MB[:, :], ALU.mult).then_inc(s["onorm"], 1)

            def output(i):
                gate = g.mod[:, 2, bass.ds(i - 1, 1)] if not isinstance(i, int) else g.mod[:, 2, i - 1:i]
                dve.wait_ge(s["yacc"], i * 4)
                dve.wait_ge(s["xnew"], i - 1)
                dve.tensor_scalar(g.ytmp[:, :], YB[:, :], g.bo[:, layer:layer + 1], gate, ALU.add, ALU.mult)\
                   .then_inc(s["ytmp"], 1)

            def batch(i, first, last):
                for q in range(UNITS):
                    u = a_unit(q, last)
                    for k in range(CH):
                        for h in range(UH):
                            if u is not None:
                                maxima(i, u, k, h)
                            if (k, h) == (1, 1) and q == 1 and not first:
                                output(i)
                            if (k, h) == (2, 1) and not (first and q == 0):
                                invert_sums(i, q - 1)
                            if (k, h) == (3, 1) and not (first and q == 0):
                                normalise(i, q - 1)

            for u in range(2):
                for k in range(CH):
                    for h in range(UH):
                        maxima(lo, u, k, h)
            batches(dve, batch)
            invert_sums(hi, -1)
            normalise(hi, -1)
            output(hi)


def setup_experts(g):
    nc = g.nc
    g.wg = g.sb("wg", [P, E])
    g.route_c = g.sb("route_c", [P, P + 3 * E])
    g.htok = g.sb("htok", [P, NT // P, C])
    g.logits = g.sb("logits", [P, NT // P, E])
    g.gate_w = g.sb("gate_w", [P, NT // P])
    g.slot_in = g.sb("slot_in", [P, NT // P], I32)
    g.slot_out = g.sb("slot_out", [P, NT // P], I32)
    g.gs = {n: g.sem("g_" + n) for n in (
        "setup", "x_loaded", "sq", "turned", "htok", "lpsum", "logits",
        "vec", "counts", "zeros", "zeroed", "scattered", "picked", "pturned", "pscaled", "x2", "x2_stored")}
    s = g.gs
    with nc.Block() as block:
        @block.gpsimd
        def _(pool):
            pool.memset(g.htok[:, :, :], 0.0).then_inc(s["zeros"], 1)

        @block.sync
        def _(sp):
            sp.wait_ge(s["zeros"], 1)
            rows = g.slots.rearrange("(p r) c -> p r c", p=P)
            n = NT // P
            sp.dma_start(rows[:, 0:n, :], g.htok[:, :, :]).then_inc(s["zeroed"], 16)
            sp.dma_start(rows[:, n:, :], g.htok[:, 0:E * CAP // P - n, :]).then_inc(s["zeroed"], 16)
            sp.wait_ge(s["zeroed"], 32)


def gate(g, x):
    nc, s = g.nc, g.gs
    base = B

    with nc.Block() as block:
        @block.sync
        def _(sp):
            def batch(it, slot, last):
                if not isinstance(it, int):
                    sp.wait_ge(g.ns["xc"], it + (base + 1))
                    norm_load(g, sp, it + (base + 2), slot, x[it + 2])

            sp.dma_start(g.wg[:, :], g.ins["wg"]).then_inc(s["setup"], 16)
            sp.dma_start(g.route_c[:, :], g.ins["route_c"]).then_inc(s["setup"], 16)
            for slot in range(2):
                norm_load(g, sp, base + slot, slot, x[slot])
            paired(sp, 0, B, batch)

        @block.tensor
        def _(pe):
            def batch(it, slot, last):
                if not last:
                    norm_mean(g, pe, it + (base + 1), slot ^ 1)
                norm_spread(g, pe, it + base)
                if not last:
                    norm_variance(g, pe, it + (base + 1))
                pe.wait_ge(g.ns["h"], it + (base + 1))
                pe.wait_ge(s["htok"], it)
                for c in range(CH):
                    mm = pe.transpose(g.bank[2][:, c * P:(c + 1) * P], g.h[:, c * P:(c + 1) * P], g.ident[:, :])
                mm.then_inc(s["turned"], 1)
                pe.wait_ge(s["logits"], it)
                for c in range(CH):
                    mm = pe.matmul(g.bank[3][:, c * E:(c + 1) * E], g.h[:, c * P:(c + 1) * P], g.wg[:, :],
                                   start=(c == 0), stop=True, skip_group_check=True)
                mm.then_inc(s["lpsum"], 1)

            pe.wait_ge(s["setup"], 32)
            norm_mean(g, pe, base, 0)
            norm_variance(g, pe, base)
            paired(pe, 0, B, batch)

        @block.scalar
        def _(act):
            def batch(it, slot, last):
                if not last:
                    norm_square(g, act, it + (base + 1), slot ^ 1)

            norm_square(g, act, base, 0)
            paired(act, 0, B, batch)

        @block.gpsimd
        def _(pool):
            def batch(it, slot, last):
                norm_power(g, pool, it + base)

            paired(pool, 0, B, batch)

        @block.vector
        def _(dve):
            def chunks(tile, it):
                return tile[:, it * CH:(it + 1) * CH, :] if isinstance(it, int) else tile[:, bass.ds(it * CH, CH), :]

            def batch(it, slot, last):
                norm_repeat(g, dve, it + base)
                if not last:
                    norm_center(g, dve, it + (base + 1), slot ^ 1)
                norm_finish(g, dve, it + base, slot, 4, 3, it, [(s["lpsum"], it)])
                if not last:
                    norm_epsilon(g, dve, it + (base + 1))
                dve.wait_ge(s["turned"], it + 1)
                dve.tensor_scalar(chunks(g.htok, it), g.bank[2][:, :].rearrange("p (c n) -> p c n", c=CH),
                                  1.0, None, ALU.mult).then_inc(s["htok"], 1)
                dve.wait_ge(s["lpsum"], it + 1)
                dve.tensor_scalar(chunks(g.logits, it), g.bank[3][:, 0:CH * E].rearrange("p (c n) -> p c n", c=CH),
                                  1.0, None, ALU.mult).then_inc(s["logits"], 1)

            norm_center(g, dve, base, 0)
            norm_epsilon(g, dve, base)
            paired(dve, 0, B, batch)


def route(g):
    nc, s = g.nc, g.gs
    T = NT // P
    big = g.xc[:, 0:T * E].rearrange("p (t e) -> p t e", e=E)
    ex = g.sq[:, 0:T * E].rearrange("p (t e) -> p t e", e=E)
    hot = g.std[:, 0:T * E].rearrange("p (t e) -> p t e", e=E)
    cum = g.xh[:, 0:T * E].rearrange("p (t e) -> p t e", e=E)
    r = g.rstd[:, 0:10 * T].rearrange("p (n t) -> p n t", n=10)
    top, den, pick, pos, keep, slot = (r[:, n, :] for n in range(6))
    tri, rev = g.route_c[:, 0:P], g.route_c[:, P:P + E]
    base, ones = g.route_c[:, P + E:P + 2 * E], g.ones_w[:, 0:T]

    def wide(col):
        return col.unsqueeze(2).broadcast_to([P, T, E])

    def rows(c):
        return c.unsqueeze(1).broadcast_to([P, T, E])

    with nc.Block() as block:
        @block.vector
        def _(dve):
            n = 0

            def step(i):
                nonlocal n
                n += 1
                i.then_inc(s["vec"], 1)
                dve.wait_ge(s["vec"], n)

            step(dve.reduce_max(top, g.logits[:, :, :], AX.X))
            step(dve.tensor_tensor(big, g.logits[:, :, :], wide(top), ALU.subtract))
            dve.wait_ge(s["sq"], 1)
            step(dve.reduce_sum(den, ex, AX.X))
            step(dve.reduce_max(top, ex, AX.X))
            step(dve.reciprocal(den, den))
            step(dve.tensor_tensor(g.gate_w[:, :], top, den, ALU.mult))
            step(dve.tensor_tensor(big, ex, wide(top), ALU.is_equal))
            step(dve.tensor_tensor(big, big, rows(rev), ALU.mult))
            step(dve.reduce_max(pick, big, AX.X))
            step(dve.tensor_tensor(hot, big, wide(pick), ALU.is_equal))
            dve.wait_ge(s["counts"], 1)
            step(dve.tensor_copy(big, g.bank[5][:, 0:T * E].rearrange("p (t e) -> p t e", e=E)))
            for e in range(E):
                scan = dve.tensor_tensor_scan(ex[:, :, e], ones, big[:, :, e], 0.0, ALU.mult, ALU.add)
                step(scan)
            step(dve.tensor_tensor(ex, ex, big, ALU.subtract))
            step(dve.tensor_tensor(cum, ex, g.bank[4][:, 0:T * E].rearrange("p (t e) -> p t e", e=E), ALU.add))
            step(dve.tensor_tensor(big, cum, hot, ALU.mult))
            step(dve.reduce_sum(pos, big, AX.X))
            step(dve.tensor_scalar(keep, pos, float(CAP), None, ALU.is_le))
            step(dve.tensor_tensor(g.gate_w[:, :], g.gate_w[:, :], keep, ALU.mult))
            step(dve.tensor_tensor(big, hot, rows(base), ALU.mult))
            step(dve.reduce_sum(slot, big, AX.X))
            step(dve.scalar_tensor_tensor(out=slot, in0=slot, scalar=-1.0, in1=pos, op0=ALU.add, op1=ALU.add))
            step(dve.tensor_tensor(slot, slot, keep, ALU.mult))
            step(dve.tensor_copy(g.slot_out[:, :], slot))
            step(dve.tensor_scalar(keep, keep, -float(E * CAP), float(E * CAP), ALU.mult, ALU.add))
            step(dve.tensor_tensor(slot, slot, keep, ALU.add))
            step(dve.tensor_copy(g.slot_in[:, :], slot))
            g.route_steps = n

        @block.scalar
        def _(act):
            act.wait_ge(s["vec"], 2)
            act.activation(ex, big, ACT.Exp).then_inc(s["sq"], 1)

        @block.tensor
        def _(pe):
            pe.wait_ge(s["vec"], 10)
            flat = g.std[:, 0:T * E]
            pe.matmul(g.bank[4][:, 0:T * E], tri, flat, start=True, stop=True)
            pe.matmul(g.bank[5][:, 0:T * E], g.ones_w[:, :], flat, start=True, stop=True).then_inc(s["counts"], 1)

    with nc.Block() as block:
        @block.gpsimd
        def _(pool):
            for t in range(T):
                pool.indirect_dma_start(g.slots, bass.IndirectOffsetOnAxis(ap=g.slot_in[:, t:t + 1], axis=0),
                                        g.htok[:, t, :], None, bounds_check=E * CAP - 1, oob_is_err=False)\
                    .then_inc(s["scattered"], 16)
            pool.wait_ge(s["scattered"], 16 * T)


def setup_expert_loop(g):
    g.ew1 = g.sb("ew1", [P, 2, F])
    g.ew2 = g.sb("ew2", [P, 2, F])
    g.eb1 = g.sb("eb1", [P, 2, F // P])
    g.eb2 = g.sb("eb2", [P, 2, C])
    g.eh = g.sb("eh", [P, F // P, CAP])
    g.exT = g.sb("exT", [P, CAP])
    g.es = {n: g.sem("e_" + n) for n in ("turned", "xT", "hidden", "relu", "answer", "biased", "stored")}
    g.eload = [g.sem(f"e_loaded{i}") for i in range(2)]


def experts(g):
    nc, s = g.nc, g.es
    ST = CAP // P
    HALF = CAP // 2
    xs = [g.qk[:, :, :], g.ra[:, :, :]]
    ys = [g.rb[:, :, :], g.res[:, :, :]]

    def tile(t):
        return t.rearrange("p a n -> p (a n)")[:, 0:CAP].rearrange("p (s c) -> p s c", c=C)

    with nc.Block() as block:
        @block.sync
        def _(sp):
            def load(e, par):
                sp.dma_start(g.ew1[:, par, :], g.ins["ew1"][e]).then_inc(g.eload[par], 16)
                sp.dma_start(g.ew2[:, par, :].rearrange("p (f c) -> p f c", c=C), g.ins["ew2"][e])\
                  .then_inc(g.eload[par], 16)
                sp.dma_start(g.eb1[:, par, :], g.ins["eb1"][e]).then_inc(g.eload[par], 16)
                sp.dma_start(g.eb2[:, par, :], g.ins["eb2"][e]).then_inc(g.eload[par], 16)
                sp.dma_start(tile(xs[par]), g.slots_by_expert[e]).then_inc(g.eload[par], 16)

            def two(i, last):
                for par in range(2):
                    if par == 0:
                        sp.wait_ge(s["answer"], i * 2 * ST)
                        load(i * 2 + 1, 1)
                    sp.wait_ge(s["biased"], (i * 2 + par + 1) * ST)
                    sp.dma_start(g.answers_by_expert[i * 2 + par], tile(ys[par])).then_inc(s["stored"], 16)
                    if par == 0 and not last:
                        load(i * 2 + 2, 0)

            load(0, 0)
            with sp.Fori(0, E // 2 - 1) as i:
                two(i, False)
            two(E // 2 - 1, True)
            sp.wait_ge(s["stored"], 16 * E)

        @block.tensor
        def _(pe):
            with pe.Fori(0, E // 2) as i:
                for par in range(2):
                    pe.wait_ge(g.eload[par], i * 80 + 80)
                    pe.wait_ge(s["xT"], (i * 2 + par) * 2)
                    for t in range(ST):
                        bank, col = (g.bank[0], t * P) if t < 4 else (g.bank[1], 0)
                        mm = pe.transpose(bank[:, col:col + P], tile(xs[par])[:, t, :], g.ident[:, :])
                    mm.then_inc(s["turned"], 1)
                    pe.wait_ge(s["xT"], (i * 2 + par) * 2 + 2)
                    for f in range(F // P):
                        for half in range(2):
                            n = f * 2 + half
                            pe.wait_ge(s["relu"], (i * 2 + par) * 8 + n - 3) if n >= 4 else None
                            pe.matmul(g.bank[2 + n % 4][:, 0:HALF], g.ew1[:, par, f * P:(f + 1) * P],
                                      g.exT[:, half * HALF:(half + 1) * HALF], start=True, stop=True)\
                              .then_inc(s["hidden"], 1)
                    pe.wait_ge(s["relu"], (i * 2 + par) * 8 + 8)
                    for t in range(ST):
                        if t >= 2:
                            pe.wait_ge(s["biased"], (i * 2 + par) * ST + t - 1)
                        for f in range(F // P):
                            mm = pe.matmul(g.bank[6 + t % 2][:, 0:C], g.eh[:, f, t * P:(t + 1) * P],
                                           g.ew2[:, par, f * C:(f + 1) * C], start=(f == 0), stop=(f == F // P - 1))
                        mm.then_inc(s["answer"], 1)
                    pe.wait_ge(s["biased"], (i * 2 + par + 1) * ST)

        @block.scalar
        def _(act):
            with act.Fori(0, E // 2) as i:
                for par in range(2):
                    act.wait_ge(s["answer"], (i * 2 + par) * ST)
                    for f in range(F // P):
                        for half in range(2):
                            n = f * 2 + half
                            act.wait_ge(s["hidden"], (i * 2 + par) * 8 + n + 1)
                            act.activation(g.eh[:, f, half * HALF:(half + 1) * HALF], g.bank[2 + n % 4][:, 0:HALF],
                                           ACT.Relu, bias=g.eb1[:, par, f:f + 1]).then_inc(s["relu"], 1)

        @block.vector
        def _(dve):
            with dve.Fori(0, E // 2) as i:
                for par in range(2):
                    dve.wait_ge(s["turned"], i * 2 + par + 1)
                    dve.wait_ge(s["hidden"], (i * 2 + par) * 8)
                    dve.tensor_copy(g.exT[:, 0:512], g.bank[0][:, :]).then_inc(s["xT"], 1)
                    dve.tensor_copy(g.exT[:, 512:CAP], g.bank[1][:, 0:CAP - 512]).then_inc(s["xT"], 1)
                    dve.wait_ge(s["stored"], (i * 2 + par) * 16)
                    for t in range(ST):
                        dve.wait_ge(s["answer"], (i * 2 + par) * ST + t + 1)
                        dve.tensor_tensor(tile(ys[par])[:, t, :], g.bank[6 + t % 2][:, 0:C], g.eb2[:, par, :],
                                          ALU.add).then_inc(s["biased"], 1)


def combine(g, x1, x2):
    nc, s = g.nc, g.gs
    gathered = [g.sem(f"g_gathered{i}") for i in range(2)]
    with nc.Block() as block:
        @block.gpsimd
        def _(pool):
            for it in range(B):
                if it >= 2:
                    pool.wait_ge(s["picked"], it - 1)
                for t in range(it * CH, (it + 1) * CH):
                    pool.indirect_dma_start(g.htok[:, t, :], None, g.answers,
                                            bass.IndirectOffsetOnAxis(ap=g.slot_out[:, t:t + 1], axis=0))\
                        .then_inc(gathered[it % 2], 16)

        @block.sync
        def _(sp):
            def batch(it, slot, last):
                sp.wait_ge(s["x2"], it)
                sp.dma_start(g.x_in[:, :], x1[it]).then_inc(s["x_loaded"], 16)
                sp.wait_ge(s["x2"], it + 1)
                sp.dma_start(x2[it], g.xh[:, :]).then_inc(s["x2_stored"], 16)

            paired(sp, 0, B, batch)
            sp.wait_ge(s["x2_stored"], B * 16)

        @block.vector
        def _(dve):
            def batch(it, slot, last):
                at, col = slice(it * CH, (it + 1) * CH), slice(it, it + 1)
                if not isinstance(it, int):
                    at, col = bass.ds(it * CH, CH), bass.ds(it, 1)
                dve.wait_ge(gathered[slot], it * (8 * CH) + 8 * CH * (2 - slot))
                dve.wait_ge(s["pturned"], it)
                dve.tensor_tensor(g.xc[:, :].rearrange("p (c n) -> p c n", c=CH), g.htok[:, at, :],
                                  g.gate_w[:, at].unsqueeze(2).broadcast_to([P, CH, C]), ALU.mult)\
                   .then_inc(s["picked"], 1)
                dve.wait_ge(s["pturned"], it + 1)
                dve.wait_ge(s["x2"], it)
                dve.tensor_scalar(g.sq[:, :], g.bank[2][:, :], g.mod[:, 5, col], None, ALU.mult)\
                   .then_inc(s["pscaled"], 1)
                dve.wait_ge(s["pscaled"], it + 1)
                dve.wait_ge(s["x_loaded"], it * 16 + 16)
                dve.wait_ge(s["x2_stored"], it * 16)
                dve.tensor_tensor(g.xh[:, :], g.sq[:, :], g.x_in[:, :], ALU.add).then_inc(s["x2"], 1)

            paired(dve, 0, B, batch)

        @block.tensor
        def _(pe):
            with pe.Fori(0, B) as it:
                pe.wait_ge(s["picked"], it + 1)
                pe.wait_ge(s["pscaled"], it)
                for c in range(CH):
                    mm = pe.transpose(g.bank[2][:, c * P:(c + 1) * P], g.xc[:, c * P:(c + 1) * P], g.ident[:, :])
                mm.then_inc(s["pturned"], 1)


def setup_local(g):
    nc = g.nc
    g.lw = g.sb("lw", [P, 2, 3 * INNER])
    g.lwo = g.sb("lwo", [P, 2, PAIRS, C])
    g.lw1 = g.sb("lw1", [P, 2, 2 * HID])
    g.lw2 = g.sb("lw2", [P, 2, HC, C])
    g.lcol = g.sb("lcol", [P, 2, 3 + 2 * HC])
    g.lqk = g.sb("lqk", [P, 2, 4, HD])
    g.xpos = g.sb("xpos", [P, 4, CH, HD])
    g.turn = g.sb("l_turn", [P, 2, 4, CH, HD])
    g.minus_half = g.sb("l_minus_half", [P, 2 * PAIRS])
    g.bandf = g.sb("bandf", [P, 2, WIN])
    g.band = g.sb("band", [P, 2, WIN], BF16)
    g.xs = g.sb("l_xs", [P, N])
    g.lsq = g.sb("l_sq", [P, 2, 2 * PAIRS, HD])
    g.lt1 = g.sb("l_t1", [P, 2 * PAIRS, HD])
    g.lt2 = g.sb("l_t2", [P, 2 * PAIRS, HD])
    g.lts = g.sb("l_ts", [P, 2, 2 * PAIRS, HD])
    g.lss = g.sb("l_ss", [P, 2, 2 * PAIRS])
    g.lclip = g.sb("l_clip", [P, 2, 2 * PAIRS])
    g.linv = g.sb("l_inv", [P, 2, CH, 2 * PAIRS])
    g.lkn = g.sb("l_kn", [P, 2 * PAIRS, HD])
    g.qr = g.sb("l_qr", [P, 2, PAIRS, N])
    g.kr = g.sb("l_kr", [P, PAIRS, W + N])
    g.vt = g.sb("l_vt", [P, CH, INNER])
    g.lmx = g.sb("l_mx", [P, 4, 2])
    g.lnb = g.sb("l_nb", [P, 4, 2])
    g.lsm = g.sb("l_sm", [P, 4, 2])
    g.lrs = g.sb("l_rs", [P, 4, 2])
    g.pe_ = g.sb("l_p", [P, 2, 2, WIN])
    g.pn = g.sb("l_pn", [P, 2, 2, 2 * P])
    g.pt = g.sb("l_pt", [P, 2, 4, P])
    g.ot = g.sb("l_ot", [P, PAIRS, N])
    g.xr = g.sb("l_x", [P, N])
    g.x1l = g.sb("l_x1", [P, N])
    g.s2 = g.sb("l_s2", [P, N])
    g.cxc = g.sb("c_xc", [P, N])
    g.csq = g.sb("c_sq", [P, N])
    g.cvar = g.sb("c_var", [P, CH])
    g.crs = g.sb("c_rs", [P, CH])
    g.cspread = g.sb("c_spread", [P, CH, P])
    g.cxh = g.sb("c_xh", [P, N])
    g.lh = g.sb("l_h", [P, N])
    g.graw = g.sb("l_graw", [P, HC, N])
    g.gl = g.sb("l_gl", [P, HC, N])
    g.hm = g.sb("l_hm", [P, HC, N])
    g.x2l = g.sb("l_x2", [P, N])
    g.xo = g.sb("l_xo", [P, N])
    g.xf = g.sb("l_xf", [P, N])
    g.ls = {n: g.sem("l_" + n) for n in (
        "setup", "xs_loaded", "xr_loaded", "xf_loaded", "proj", "sq", "ss", "clip", "inv", "t1", "t2", "tsum", "kn",
        "qk_turned", "qk", "v_psum", "v", "scores", "max", "nbias", "exp", "rsum", "pnorm",
        "turned", "pt", "pv", "o", "wo", "x1", "s2", "mean", "xc", "sq2", "var", "veps", "rstd", "spread", "rstd_psum",
        "xh", "h", "gate_psum", "gate", "gelu", "value_psum", "hidden", "y2", "x2", "final", "stored")}
    s = g.ls
    with nc.Block() as block:
        @block.sync
        def _(sp):
            for dst, src in ((g.lw[:, :, :], g.ins["lw"]), (g.lwo[:, :, :, :], g.ins["lwo"]),
                             (g.lw1[:, :, :], g.ins["lw1"]), (g.lw2[:, :, :, :], g.ins["lw2"]),
                             (g.lcol[:, :, :], g.ins["lcol"]), (g.xpos[:, :, :, :], g.ins["xpos"]),
                             (g.lqk[:, :, :, :], g.ins["lqk"]), (g.bandf[:, :, :], g.ins["band"])):
                sp.dma_start(dst, src).then_inc(s["setup"], 16)
            sp.wait_ge(s["setup"], 8 * 16)

        @block.vector
        def _(dve):
            dve.memset(g.minus_half[:, :], -0.5)
            dve.memset(g.graw[:, :, :], 0.0)
            dve.wait_ge(s["setup"], 8 * 16)
            dve.tensor_copy(g.band[:, :, :], g.bandf[:, :, :])
            for layer in range(2):
                dve.tensor_tensor(g.turn[:, layer, :, :, :], g.xpos[:, :, :, :],
                                  g.lqk[:, layer, :, :].unsqueeze(2).broadcast_to([P, 4, CH, HD]), ALU.mult)

        @block.gpsimd
        def _(pool):
            pool.memset(g.pn[:, :, :, :], 0.0)
            pool.memset(g.kr[:, :, 0:W], 0.0)
            pool.memset(g.qr[:, :, :, :], 0.0)
            pool.memset(g.xs[:, :], 0.0)
            pool.memset(g.s2[:, :], 0.0)


def local_input(g, x, h_out):
    nc, stored = g.nc, g.sem("h_stored")
    base = 3 * B
    with nc.Block() as block:
        @block.sync
        def _(sp):
            def batch(it, slot, last):
                if not isinstance(it, int):
                    sp.wait_ge(g.ns["xc"], it + (base + 1))
                    norm_load(g, sp, it + (base + 2), slot, x[it + 2])
                sp.wait_ge(g.ns["h"], it + (base + 1))
                sp.dma_start(h_out[it], g.h[:, :]).then_inc(stored, 16)

            for slot in range(2):
                norm_load(g, sp, base + slot, slot, x[slot])
            paired(sp, 0, B, batch)
            sp.wait_ge(stored, B * 16)

        @block.tensor
        def _(pe):
            def batch(it, slot, last):
                if not last:
                    norm_mean(g, pe, it + (base + 1), slot ^ 1)
                norm_spread(g, pe, it + base)
                if not last:
                    norm_variance(g, pe, it + (base + 1))

            norm_mean(g, pe, base, 0)
            norm_variance(g, pe, base)
            paired(pe, 0, B, batch)

        @block.scalar
        def _(act):
            def batch(it, slot, last):
                if not last:
                    norm_square(g, act, it + (base + 1), slot ^ 1)

            norm_square(g, act, base, 0)
            paired(act, 0, B, batch)

        @block.gpsimd
        def _(pool):
            def batch(it, slot, last):
                norm_power(g, pool, it + base)

            paired(pool, 0, B, batch)

        @block.vector
        def _(dve):
            def batch(it, slot, last):
                norm_repeat(g, dve, it + base)
                if not last:
                    norm_center(g, dve, it + (base + 1), slot ^ 1)
                norm_finish(g, dve, it + base, slot, 4, 3, it + B, [(stored, it * 16)])
                if not last:
                    norm_epsilon(g, dve, it + (base + 1))

            norm_center(g, dve, base, 0)
            norm_epsilon(g, dve, base)
            paired(dve, 0, B, batch)


def local_layers(g, x_in, x_mid, x_out, x3):
    nc, s = g.nc, g.ls
    lo, hi = 0, 2 * B
    NU, NH, HH = CH * PAIRS, 2 * PAIRS, HD // 2
    S, TB, OB, PB, KB, XB, YB = g.bank[0:2], g.bank[2], g.bank[3], g.bank[4], g.bank[5], g.bank[6], g.bank[7]
    MB = (PB, KB)
    col = lambda layer, n: g.lcol[:, layer, n:n + 1]

    def heads(ap):
        return ap.rearrange("p (h d) -> p h d", d=HD)

    def after(it, per, n):
        return it * per + n if not isinstance(it, int) else max(it * per + n, 0)

    def kept(t, last):
        return t < 2 or not last

    def passes(engine, batch, drain):
        batch(0, 0, 0, True, False)
        with engine.Fori(1, B - 1) as it:
            batch(it, 0, 0, False, False)
        batch(B - 1, 1, 0, False, False)
        batch(B, 1, 0, False, False)
        with engine.Fori(B + 1, 2 * B - 1) as it:
            batch(it, 1, 1, False, False)
        batch(2 * B - 1, 1, 1, False, True)
        drain(2 * B, 1)

    def layer_of(it, new):
        return (0 if it < B else 1) if isinstance(it, int) else new

    with nc.Block() as block:
        @block.sync
        def _(sp):
            def source(b, layer):
                return x_in[b] if layer == 0 else x_mid[b - B]

            def load_xs(b, layer):
                if layer == 1:
                    sp.wait_ge(s["stored"], (b - (B - 1)) * 16)
                x = source(b, layer)
                sp.dma_start(g.xs[0:C // 2, :], x[0:C // 2, :]).then_inc(s["xs_loaded"], 16)
                sp.dma_start(g.xs[C // 2:C, 1:N], x[C // 2:C, 0:N - 1]).then_inc(s["xs_loaded"], 16)

            def load_xf(it, old):
                if old == 1:
                    sp.wait_ge(s["final"], it - (1 + B))
                    sp.dma_start(g.xf[:, :], x3[it - (1 + B)]).then_inc(s["xf_loaded"], 16)

            def store(it, old):
                if old == 1:
                    sp.wait_ge(s["final"], it - B)
                    sp.dma_start(x_out[it - (1 + B)], g.xo[:, :]).then_inc(s["stored"], 16)
                else:
                    sp.wait_ge(s["x2"], it)
                    sp.dma_start(x_mid[it - 1], g.xo[:, :]).then_inc(s["stored"], 16)

            def batch(it, new, old, first, last):
                if not first:
                    load_xf(it, old)
                if not last:
                    sp.wait_ge(s["v_psum"], it * CH + CH)
                    load_xs(it + 1, new)
                if not first:
                    sp.wait_ge(s["x1"], it)
                sp.dma_start(g.xr[:, :], source(it, layer_of(it, new))).then_inc(s["xr_loaded"], 16)
                if not first:
                    store(it, old)

            def drain(it, old):
                load_xf(it, old)
                store(it, old)

            load_xs(0, 0)
            passes(sp, batch, drain)
            sp.wait_ge(s["stored"], hi * 16)

        @block.tensor
        def _(pe):
            def project(it, a, w, layer):
                c = a % CH
                if c == 0 and w == 0:
                    pe.wait_ge(s["xs_loaded"], (it + a // CH) * 32 + 32)
                pe.wait_ge(s["t2"], after(it, 4 * CH, 4 * a + 2 * w - 2))
                if w == 0:
                    pe.wait_ge(s["v"], it * CH + a)
                pe.matmul(MB[w][:, :], g.xs[:, c * P:(c + 1) * P], g.lw[:, layer, w * INNER:(w + 1) * INNER],
                          start=True, stop=True).then_inc(s["proj"], 1)

            def values(it, a, layer):
                c = a % CH
                pe.wait_ge(s["t2"], it * 4 * CH + 4 * a + 2)
                pe.matmul(PB[:, :], g.xs[:, c * P:(c + 1) * P], g.lw[:, layer, 2 * INNER:3 * INNER],
                          start=True, stop=True).then_inc(s["v_psum"], 1)

            def turn_item(it, a, w):
                m = it * 2 * CH + 2 * a + w
                if w == 0:
                    pe.wait_ge(s["tsum"], m + 1)
                else:
                    pe.wait_ge(s["kn"], it * CH + a + 1)
                pe.wait_ge(s["qk"], m)
                src = g.lts[:, 0, :, :] if w == 0 else g.lkn[:, :, :]
                for p in range(PAIRS):
                    mm = pe.transpose(XB[:, p * P:(p + 1) * P],
                                      src[:, 2 * p:2 * p + 2, :].rearrange("p h d -> p (h d)"), g.ident[:, :])
                mm.then_inc(s["qk_turned"], 1)

            def projections(it, a, j, layer):
                if j == 0:
                    project(it, a, 0, layer)
                if j == 1:
                    project(it, a, 1, layer)
                if j == 2:
                    values(it, a, layer)
                if j == 3:
                    turn_item(it, a, 0)
                if j == 5:
                    turn_item(it, a, 1)

            def scores(it, n, first):
                t, p = divmod(n, PAIRS)
                if p == 0:
                    pe.wait_ge(s["qk"], it * 2 * CH + 2 * t + 2)
                if n > 1 or not first:
                    pe.wait_ge(s["exp"], it * NU + n - 1)
                for e in range(2):
                    out = S[n % 2][:, WIN * e:WIN * (e + 1)]
                    pe.matmul(out, g.qr[:, e, p, t * P:(t + 1) * P], g.kr[:, p, t * P:t * P + WIN],
                              start=True, stop=False, skip_group_check=True)
                    mm = pe.matmul(out, g.identb[:, :], g.band[:, min(t, 1), :], start=False, stop=True,
                                   skip_group_check=True)
                mm.then_inc(s["scores"], 1)

            def turn(it, n):
                pe.wait_ge(s["pnorm"], it * NU + n + 1)
                pe.wait_ge(s["pt"], it * NU + n)
                for j in range(4):
                    mm = pe.transpose(TB[:, j * P:(j + 1) * P],
                                      g.pn[:, n % 2, j // 2, (j % 2) * P:(j % 2 + 1) * P], g.ident[:, :])
                mm.then_inc(s["turned"], 1)

            def pv(it, n):
                t, p = n // PAIRS % CH, n % PAIRS
                pe.wait_ge(s["pt"], it * NU + n + 1)
                if p == 0:
                    pe.wait_ge(s["o"], it * CH + n // PAIRS)
                    pe.wait_ge(s["v"], it * CH + n // PAIRS + 1)
                for j in (1, 0) if t else (1,):
                    for e in range(2):
                        at = (2 * p + e) * HD
                        mm = pe.matmul(OB[HD * e:HD * (e + 1), p * P:(p + 1) * P], g.vt[:, t - 1 + j, at:at + HD],
                                       g.pt[:, n % 2, 2 * e + j, :], start=(j == 1), stop=(j == 0 or t == 0),
                                       skip_group_check=True)
                mm.then_inc(s["pv"], 1)

            def chain(it, n, layer):
                if n == 4:
                    pe.wait_ge(s["o"], it * CH)
                    pe.wait_ge(s["x2"], it - 1)
                    for p in range(PAIRS):
                        mm = pe.matmul(YB[:, :], g.lwo[:, layer, p, :], g.ot[:, p, :], start=(p == 0),
                                       stop=(p == PAIRS - 1), skip_group_check=True)
                    mm.then_inc(s["wo"], 1)
                if n == 5:
                    pe.wait_ge(s["x1"], it)
                    pe.matmul(YB[:, :], g.mean_w[:, :], g.s2[:, :], start=True, stop=True).then_inc(s["mean"], 1)
                if n == 6:
                    pe.wait_ge(s["sq2"], it)
                    for c in range(CH):
                        mm = pe.matmul(YB[:, c:c + 1], g.csq[:, c * P:(c + 1) * P], g.mean_w[:, 0:1],
                                       start=True, stop=True, skip_group_check=True)
                    mm.then_inc(s["var"], 1)
                if n == 8:
                    pe.wait_ge(s["spread"], it)
                    for c in range(CH):
                        mm = pe.matmul(YB[:, c * P:(c + 1) * P], g.cspread[:, c, :], g.ident[:, :],
                                       start=True, stop=True, skip_group_check=True)
                    mm.then_inc(s["rstd_psum"], 1)
                if 9 <= n < 9 + HC:
                    j = n - 9
                    w, at = min(P, HID - j * P), HID + j * P
                    pe.wait_ge(s["h"], it)
                    pe.wait_ge(s["gate"], (it - 1) * HC + j)
                    pe.matmul(YB[0:w, :], g.lw1[:, layer, at:at + w], g.lh[:, :], start=True, stop=True)\
                      .then_inc(s["gate_psum"], 1)
                if 12 <= n < 12 + HC:
                    j = n - 12
                    w, at = min(P, HID - j * P), j * P
                    pe.wait_ge(s["gate"], it * HC)
                    pe.wait_ge(s["hidden"], (it - 1) * HC + j)
                    pe.matmul(YB[0:w, :], g.lw1[:, layer, at:at + w], g.lh[:, :], start=True, stop=True)\
                      .then_inc(s["value_psum"], 1)
                if n == 15:
                    pe.wait_ge(s["hidden"], it * HC)
                    for j in range(HC):
                        w = min(P, HID - j * P)
                        mm = pe.matmul(YB[:, :], g.lw2[0:w, layer, j, :], g.hm[0:w, j, :], start=(j == 0),
                                       stop=(j == HC - 1), skip_group_check=True)
                    mm.then_inc(s["y2"], 1)

            def batch(it, new, old, first, last):
                for n in range(NU):
                    t, j = divmod(n, 4)
                    scores(it, n, first)
                    if j < 2 and kept(t - 1, last):
                        projections(it, t + 1, 4 + j, layer_of(it, new) if t + 1 < CH else new)
                    if kept(t, last):
                        projections(it, t + 2, j, layer_of(it, new) if t + 2 < CH else new)
                    if not first or n >= 3:
                        pv(it, n - 3)
                    if not first or n >= 2:
                        turn(it, n - 2)
                    if not first:
                        chain(it, n, old)

            def drain(it, old):
                for n in range(NU):
                    if n < 2:
                        turn(it, n - 2)
                    if n < 3:
                        pv(it, n - 3)
                    chain(it, n, old)

            for a in range(2):
                for j in range(6 if a == 0 else 4):
                    projections(0, a, j, 0)
            passes(pe, batch, drain)

        @block.scalar
        def _(act):
            def square(it, a, w):
                m = it * 2 * CH + 2 * a + w
                act.wait_ge(s["proj"], m + 1)
                act.wait_ge(s["ss"], after(it, 2 * CH, 2 * a + w - 1))
                act.activation(g.lsq[:, w, :, :], heads(MB[w][:, :]), ACT.Square).then_inc(s["sq"], 1)

            def copy_item(it, a, w):
                m, c = it * 2 * CH + 2 * a + w, a % CH
                act.wait_ge(s["qk_turned"], m + 1)
                src = XB[:, :].rearrange("p (h n) -> p h n", h=PAIRS)
                if w == 0:
                    act.activation(g.qr[0:HD, 0, :, c * P:(c + 1) * P], src[0:HD], ACT.Copy)
                    last = act.activation(g.qr[HD:P, 1, :, c * P:(c + 1) * P], src[HD:P], ACT.Copy)
                else:
                    last = act.activation(g.kr[:, :, W + c * P:W + (c + 1) * P], src, ACT.Copy)
                last.then_inc(s["qk"], 1)

            def projections(it, a, j, layer):
                if j < 2:
                    square(it, a, j)
                if j == 3:
                    copy_item(it, a, 0)
                if j == 5:
                    copy_item(it, a, 1)

            def exps(it, n, first):
                act.wait_ge(s["nbias"], it * NU + n + 1)
                if n > 1 or not first:
                    act.wait_ge(s["pnorm"], it * NU + n - 1)
                for e in range(2):
                    last = act.activation(g.pe_[:, n % 2, e, :], S[n % 2][:, WIN * e:WIN * (e + 1)], ACT.Exp,
                                          bias=g.lnb[:, n % 4, e:e + 1],
                                          scale=g.linv[:, 0, n // PAIRS, 2 * (n % PAIRS) + e:2 * (n % PAIRS) + e + 1],
                                          accum_out=g.lsm[:, n % 4, e:e + 1])
                last.then_inc(s["exp"], 1)

            def copy_pt(it, n):
                act.wait_ge(s["turned"], it * NU + n + 1)
                act.wait_ge(s["pv"], after(it, NU, n - 1))
                act.activation(g.pt[:, n % 2, :, :], TB[:, :].rearrange("p (j n) -> p j n", j=4),
                               ACT.Copy).then_inc(s["pt"], 1)

            def copy_o(it, t):
                act.wait_ge(s["pv"], it * NU + 4 * t + 4)
                act.wait_ge(s["wo"], it if t >= 0 else it - 1)
                c = t % CH
                act.activation(g.ot[:, :, c * P:(c + 1) * P], OB[:, :].rearrange("p (h n) -> p h n", h=PAIRS),
                               ACT.Copy).then_inc(s["o"], 1)

            def chain(it, n, layer):
                if n == 6:
                    act.wait_ge(s["xc"], it)
                    act.wait_ge(s["var"], it - 1)
                    act.activation(g.csq[:, :], g.cxc[:, :], ACT.Square).then_inc(s["sq2"], 1)
                if n == 12:
                    act.wait_ge(s["gate"], it * HC)
                    act.wait_ge(s["hidden"], (it - 1) * HC)
                    act.activation(g.gl[:, :, :], g.graw[:, :, :], ACT.Gelu).then_inc(s["gelu"], 1)

            def batch(it, new, old, first, last):
                for n in range(NU):
                    t, j = divmod(n, 4)
                    if j == 3 and not (first and t == 0):
                        copy_o(it, t - 1)
                    exps(it, n, first)
                    if j < 2 and kept(t, last):
                        projections(it, t + 2, j, layer_of(it, new) if t + 2 < CH else new)
                    if not first:
                        chain(it, n, old)
                    if not first or n >= 2:
                        copy_pt(it, n - 2)
                    if j < 2 and kept(t - 1, last):
                        projections(it, t + 1, 4 + j, layer_of(it, new) if t + 1 < CH else new)
                    if j >= 2 and kept(t, last):
                        projections(it, t + 2, j, layer_of(it, new) if t + 2 < CH else new)

            def drain(it, old):
                for n in range(NU):
                    if n < 2:
                        copy_pt(it, n - 2)
                    if n == 2:
                        copy_o(it, -1)
                    chain(it, n, old)

            for a in range(2):
                for j in range(6 if a == 0 else 4):
                    projections(0, a, j, 0)
            passes(act, batch, drain)

        @block.gpsimd
        def _(pool):
            def add_turned(it, a, w):
                m = it * 2 * CH + 2 * a + w
                pool.wait_ge(s["t1"], m + 1)
                pool.wait_ge(s["t2"], 2 * m + 2)
                if w == 0:
                    pool.wait_ge(s["qk_turned"], after(it, 2 * CH, 2 * a - 1))
                else:
                    pool.wait_ge(s["kn"], it * CH + a)
                pool.tensor_tensor(g.lts[:, w, :, :], g.lt1[:, :, :], g.lt2[:, :, :], ALU.add).then_inc(s["tsum"], 1)

            def invert_norms(it, a, w):
                pool.wait_ge(s["clip"], it * 2 * CH + 2 * a + w + 1)
                if w == 0:
                    pool.wait_ge(s["exp"], after(it, NU, 4 * (a - 3)))
                else:
                    pool.wait_ge(s["kn"], it * CH + a)
                pool.tensor_tensor(g.linv[:, w, a % CH, :], g.lclip[:, w, :], g.minus_half[:, :], ALU.pow)\
                    .then_inc(s["inv"], 1)

            def projections(it, a, j, layer):
                if j == 1:
                    add_turned(it, a, 0)
                if j == 2:
                    add_turned(it, a, 1)
                if j == 3:
                    invert_norms(it, a, 1)
                if j == 4:
                    invert_norms(it, a, 0)

            def normalise(it, n):
                pool.wait_ge(s["exp"], it * NU + n + 1)
                pool.wait_ge(s["turned"], after(it, NU, n - 1))
                pool.wait_ge(s["rsum"], it * NU + n + 1)
                pool.tensor_tensor(g.pn[:, n % 2, :, W:2 * P], g.pe_[:, n % 2, :, :],
                                   g.lrs[:, n % 4, :].unsqueeze(2).broadcast_to([P, 2, WIN]), ALU.mult)\
                    .then_inc(s["pnorm"], 1)

            def chain(it, n, layer):
                if n == 7:
                    pool.wait_ge(s["veps"], it)
                    pool.wait_ge(s["spread"], it - 1)
                    pool.tensor_tensor(g.crs[:, :], g.cvar[:, :], g.minus_half[:, 0:CH], ALU.pow)\
                        .then_inc(s["rstd"], 1)

            def batch(it, new, old, first, last):
                for n in range(NU):
                    t, j = divmod(n, 4)
                    if not first or n:
                        normalise(it, n - 1)
                    if not first:
                        chain(it, n, old)
                    if j < 2 and kept(t - 1, last):
                        projections(it, t + 1, 4 + j, layer_of(it, new) if t + 1 < CH else new)
                    if kept(t, last):
                        projections(it, t + 2, j, layer_of(it, new) if t + 2 < CH else new)

            def drain(it, old):
                normalise(it, -1)
                chain(it, 7, old)

            for a in range(2):
                for j in range(6 if a == 0 else 4):
                    projections(0, a, j, 0)
            passes(pool, batch, drain)

        @block.vector
        def _(dve):
            def rotate(it, a, w, layer):
                m, c = it * 2 * CH + 2 * a + w, a % CH
                table = lambda k, d: g.turn[:, layer, 2 * w + k, c, d].unsqueeze(1)
                psum = heads(MB[w][:, :])
                dve.wait_ge(s["sq"], m + 1)
                dve.wait_ge(s["tsum"], m)
                dve.tensor_tensor(g.lt1[:, :, :], psum, table(0, slice(0, HD)).broadcast_to([P, NH, HD]),
                                  ALU.mult).then_inc(s["t1"], 1)
                for lower, upper in ((slice(0, HH), slice(HH, HD)), (slice(HH, HD), slice(0, HH))):
                    dve.tensor_tensor(g.lt2[:, :, lower], psum[:, :, upper],
                                      table(1, lower).broadcast_to([P, NH, HH]), ALU.mult).then_inc(s["t2"], 1)

            def sum_squares(it, a, w):
                m = it * 2 * CH + 2 * a + w
                dve.wait_ge(s["sq"], m + 1)
                dve.wait_ge(s["clip"], after(it, 2 * CH, 2 * a + w - 1))
                dve.reduce_sum(g.lss[:, w, :], g.lsq[:, w, :, :], AX.X).then_inc(s["ss"], 1)
                dve.wait_ge(s["ss"], m + 1)
                dve.wait_ge(s["inv"], it * 2 * CH + 2 * a)
                dve.tensor_scalar(g.lclip[:, w, :], g.lss[:, w, :], L2_EPS * L2_EPS, None, ALU.max)\
                   .then_inc(s["clip"], 1)

            def over_norm(it, a):
                dve.wait_ge(s["inv"], it * 2 * CH + 2 * a + 1)
                dve.wait_ge(s["tsum"], it * 2 * CH + 2 * a + 2)
                dve.wait_ge(s["qk_turned"], it * 2 * CH + 2 * a)
                dve.tensor_tensor(g.lkn[:, :, :], g.lts[:, 1, :, :],
                                  g.linv[:, 1, a % CH, :].unsqueeze(2).broadcast_to([P, NH, HD]), ALU.mult)\
                   .then_inc(s["kn"], 1)

            def copy_v(it, a):
                dve.wait_ge(s["v_psum"], it * CH + a + 1)
                dve.wait_ge(s["pv"], after(it, NU, 4 * (a - 2)))
                dve.tensor_copy(g.vt[:, a % CH, :], PB[:, :]).then_inc(s["v"], 1)

            def projections(it, a, j, layer):
                if j in (1, 2):
                    sum_squares(it, a, j - 1)
                    rotate(it, a, j - 1, layer)
                if j == 3:
                    copy_v(it, a)
                if j == 4:
                    over_norm(it, a)

            def maxima(it, n):
                at = it * NU + n
                dve.wait_ge(s["scores"], at + 1)
                dve.reduce_max(g.lmx[:, n % 4, :], S[n % 2][:, 0:2 * WIN].rearrange("p (e n) -> p e n", e=2),
                               AX.X).then_inc(s["max"], 1)
                dve.wait_ge(s["max"], at + 1)
                if n % PAIRS == 0:
                    dve.wait_ge(s["inv"], it * 2 * CH + 2 * (n // PAIRS) + 2)
                dve.scalar_tensor_tensor(out=g.lnb[:, n % 4, :], in0=g.lmx[:, n % 4, :], scalar=-1.0,
                                         in1=g.linv[:, 0, n // PAIRS, 2 * (n % PAIRS):2 * (n % PAIRS) + 2],
                                         op0=ALU.mult, op1=ALU.mult).then_inc(s["nbias"], 1)

            def inverse_sum(it, n):
                dve.wait_ge(s["exp"], it * NU + n + 1)
                dve.reciprocal(g.lrs[:, n % 4, :], g.lsm[:, n % 4, :]).then_inc(s["rsum"], 1)

            def mlp(it, n, layer):
                if 10 <= n < 10 + HC:
                    j = n - 10
                    w, at = min(P, HID - j * P), 3 + HC + j
                    dve.wait_ge(s["gate_psum"], (it - 1) * HC + j + 1)
                    dve.wait_ge(s["gelu"], it - 1)
                    dve.tensor_scalar(g.graw[0:w, j, :], YB[0:w, :], g.lcol[0:w, layer, at:at + 1], None, ALU.add)\
                       .then_inc(s["gate"], 1)
                if 13 <= n < 13 + HC:
                    j = n - 13
                    w = min(P, HID - j * P)
                    dve.wait_ge(s["value_psum"], (it - 1) * HC + j + 1)
                    dve.wait_ge(s["gelu"], it)
                    dve.wait_ge(s["y2"], it - 1)
                    dve.scalar_tensor_tensor(out=g.hm[0:w, j, :], in0=YB[0:w, :],
                                             scalar=g.lcol[0:w, layer, 3 + j:4 + j], in1=g.gl[0:w, j, :],
                                             op0=ALU.add, op1=ALU.mult).then_inc(s["hidden"], 1)

            def chain(it, n, layer):
                if n == 4:
                    dve.wait_ge(s["wo"], it)
                    dve.wait_ge(s["xr_loaded"], it * 16)
                    dve.wait_ge(s["x2"], it - 1)
                    dve.wait_ge(s["xc"], it - 1)
                    dve.tensor_tensor(g.s2[0:C // 2, :], g.xr[0:C // 2, :], YB[0:C // 2, :], ALU.add)\
                       .then_inc(s["s2"], 1)
                    dve.tensor_tensor(g.s2[C // 2:C, 1:N], g.xr[C // 2:C, 0:N - 1], YB[C // 2:C, 0:N - 1], ALU.add)\
                       .then_inc(s["s2"], 1)
                    dve.tensor_tensor(g.x1l[:, :], g.xr[:, :], YB[:, :], ALU.add).then_inc(s["x1"], 1)
                if n == 5:
                    dve.wait_ge(s["mean"], it)
                    dve.wait_ge(s["xh"], it - 1)
                    dve.tensor_tensor(g.cxc[:, :], g.s2[:, :], YB[:, :], ALU.subtract).then_inc(s["xc"], 1)
                if n == 6:
                    dve.wait_ge(s["var"], it)
                    dve.wait_ge(s["rstd"], it - 1)
                    dve.tensor_scalar(g.cvar[:, :], YB[:, 0:CH], LN_EPS, None, ALU.add).then_inc(s["veps"], 1)
                if n == 7:
                    dve.wait_ge(s["rstd"], it)
                    dve.wait_ge(s["rstd_psum"], it - 1)
                    dve.tensor_copy(g.cspread[:, :, :], g.crs[:, :].unsqueeze(2).broadcast_to([P, CH, P]))\
                       .then_inc(s["spread"], 1)
                if n == 8:
                    dve.wait_ge(s["rstd_psum"], it)
                    dve.wait_ge(s["h"], it - 1)
                    dve.tensor_tensor(g.cxh[:, :], g.cxc[:, :], YB[:, :], ALU.mult).then_inc(s["xh"], 1)
                    dve.wait_ge(s["xh"], it)
                    dve.wait_ge(s["y2"], it - 1)
                    dve.tensor_scalar(g.lh[:, :], g.cxh[:, :], col(layer, 0), col(layer, 1), ALU.mult, ALU.add)\
                       .then_inc(s["h"], 1)
                if n == 15:
                    x2 = g.xo if layer == 0 else g.x2l
                    dve.wait_ge(s["y2"], it)
                    dve.wait_ge(s["stored"], (it - 1) * 16)
                    dve.scalar_tensor_tensor(out=x2[:, :], in0=YB[:, :], scalar=col(layer, 2), in1=g.x1l[:, :],
                                             op0=ALU.add, op1=ALU.add).then_inc(s["x2"], 1)
                    if layer == 1:
                        gate = g.mod[:, 5, bass.ds(it - 1, 1)] if not isinstance(it, int) else g.mod[:, 5, it - 1:it]
                        dve.wait_ge(s["x2"], it)
                        dve.wait_ge(s["xf_loaded"], (it - B) * 16)
                        dve.scalar_tensor_tensor(out=g.xo[:, :], in0=x2[:, :], scalar=gate, in1=g.xf[:, :],
                                                 op0=ALU.mult, op1=ALU.add).then_inc(s["final"], 1)

            def batch(it, new, old, first, last):
                for n in range(NU):
                    t, j = divmod(n, 4)
                    maxima(it, n)
                    if n or not first:
                        inverse_sum(it, n - 1)
                    if not first:
                        mlp(it, n, old)
                        chain(it, n - 1, old)
                    if j < 2 and kept(t - 1, last):
                        projections(it, t + 1, 4 + j, layer_of(it, new) if t + 1 < CH else new)
                    if kept(t, last):
                        projections(it, t + 2, j, layer_of(it, new) if t + 2 < CH else new)
                    if n == NU - 1 and not first:
                        chain(it, n, old)

            def drain(it, old):
                inverse_sum(it, -1)
                for n in range(NU):
                    mlp(it, n, old)
                    chain(it, n, old)

            for a in range(2):
                for j in range(6 if a == 0 else 4):
                    projections(0, a, j, 0)
            passes(dve, batch, drain)


def build(nc, ins, out):
    with ExitStack() as ctx:
        g = Program(nc, ctx, ins)
        g.qk_dram = g.dram("qk_dram", [2 * B, 2, UNITS, PARTS, D, UH, N], BF16)
        g.v_dram = g.dram("v_dram", [2 * B, CH, P, H * VW])
        g.m_dram = g.dram("m_dram", [UH, PARTS, N], BF16)
        x1, x2, x3, hx, hy = (g.dram(n, [B, P, N]) for n in ("x1", "x2", "x3", "hx", "hy"))
        g.slots = g.dram("slots", [E * CAP, C])
        g.answers = g.dram("answers", [E * CAP, C])
        g.slots_by_expert = g.slots.rearrange("(e s p) c -> e p s c", e=E, p=P)
        g.answers_by_expert = g.answers.rearrange("(e s p) c -> e p s c", e=E, p=P)
        setup(g)
        with g.memory():
            setup_projection(g)
            with g.memory():
                setup_attention(g)
                project(g, 0, ins["xT"])
                attend(g, 0, ins["xT"], x1)
            with g.memory():
                setup_experts(g)
                gate(g, x1)
                route(g)
                setup_expert_loop(g)
                experts(g)
                combine(g, x1, x2)
            with g.memory():
                setup_attention(g)
                project(g, 1, x2)
                attend(g, 1, x2, x3)
            local_input(g, x3, hx)
        with g.memory():
            setup_local(g)
            local_layers(g, hx, hy, out, x3)


def heads_to_partitions(w):
    lead = w.shape[:-1]
    return np.ascontiguousarray(
        np.moveaxis(w.reshape(*lead, UNITS, UH, D), -1, -2).reshape(*lead, C))


def constants():
    i = np.arange(P)
    sel = np.zeros((P, UH), np.float32)
    for h in range(UH):
        sel[VW * h + D, h] = 1.0
    later = (i[None, :] > i[:, None])
    masks = np.stack([np.where(later, NEG, 0.0), np.where(later.T, NEG, 0.0)], 1).astype(np.float32)
    pos = np.arange(N, dtype=np.float32)
    freqs = (1.0 / np.float32(10000.0) ** (np.arange(0, D, 2, dtype=np.float32) / np.float32(D))).astype(np.float32)
    ang = (pos[:, None] * freqs[None, :]).astype(np.float32)
    cos, sin = np.cos(ang).T, np.sin(ang).T
    c8, s8 = np.concatenate([cos, -cos]), np.concatenate([sin, sin])
    rope = np.stack([heads_to_partitions(np.tile(t, (H, 1)).T).T for t in (c8, s8)], 1).astype(np.float32)
    tri = (i[:, None] <= i[None, :]).astype(np.float32)
    e = np.arange(E, dtype=np.float32)
    route_c = np.concatenate([tri, np.tile(np.concatenate([E - e, e * CAP, np.ones(E)]), (P, 1))], 1)
    half = np.arange(0, HD, 2, dtype=np.float32)
    f = 1.0 / np.float32(10000.0) ** (half / np.float32(HD))
    ang = (pos[:, None] * f[None, :]).astype(np.float32)
    ang = np.concatenate([ang, ang], -1)
    power = (pos - N // 2) / np.float32(W // 2)
    xs = ((half + np.float32(0.4 * HD)) / np.float32(1.4 * HD))[None, :] ** power[:, None]
    xs = np.concatenate([xs, xs], -1)
    sign = np.concatenate([-np.ones(HD // 2), np.ones(HD // 2)])
    xs_q = xs * QK_SCALE
    tables = [np.cos(ang) * xs_q, np.sin(ang) * sign * xs_q, np.cos(ang) / xs, np.sin(ang) * sign / xs]
    xpos = np.stack([t.reshape(CH, P, HD).transpose(1, 0, 2) for t in tables], 1).astype(np.float32)
    j = np.arange(WIN)
    seen = (j[None, :] >= i[:, None]) & (j[None, :] <= i[:, None] + W)
    band = np.stack([np.where(seen & (j >= W)[None, :], 0.0, NEG), np.where(seen, 0.0, NEG)], 1)
    return {"route_c": route_c.astype(np.float32), "xpos": np.ascontiguousarray(xpos),
            "band": band.astype(np.float32),
            "ident": np.eye(P, dtype=np.float32), "mean_w": np.full((P, P), 1.0 / C, np.float32), "sel_sum": sel,
            "masks": masks, "rope": np.ascontiguousarray(rope)}


def layouts(a):
    h2p = heads_to_partitions
    turn = np.r_[D // 2:D, 0:D // 2]

    def turned(w):
        return w.reshape(*w.shape[:-1], H, D)[..., turn].reshape(w.shape)

    def heads(w):
        return np.tile(w, (1,) * (w.ndim - 1) + (H,))

    wq, wk, wv = a["L0_attn_Wq"], heads(a["L0_attn_Wk"]), heads(a["L0_attn_Wv"])
    bq, bk = a["L0_attn_bq"], heads(a["L0_attn_bk"])
    zero = np.zeros((C, C), np.float32)
    w1 = a["L1_attn_qkv_w"].T
    wqkv = np.stack([
        np.stack([h2p(wq), h2p(turned(wq)), h2p(wk), h2p(turned(wk)), wv, zero], 1),
        np.stack([h2p(w1[:, 0:C]), h2p(w1[:, C:2 * C]), w1[:, 2 * C:3 * C], zero, zero, zero], 1)], 1)
    temp = np.repeat(a["L1_attn_temperature"].reshape(H), D)
    pcol = np.stack([h2p(bq), h2p(turned(bq)), h2p(bk), h2p(turned(bk)), h2p(temp)], 1)

    def padded(w):
        out = np.zeros((UH, VW, UNITS, C), np.float32)
        out[:, 0:D] = w.reshape(UNITS, UH, D, C).transpose(1, 2, 0, 3)
        return out.reshape(P, UNITS, C)

    turn_l = np.r_[HD // 2:HD, 0:HD // 2]

    def columns(w, n, width=P):
        out = np.zeros((P, 2, n), np.float32)
        for c in range(n):
            part = w[:, c * width:(c + 1) * width]
            out[:part.shape[1], :, c] = part.T
        return out

    qs, ks = a["L1_ffn_q_scale"], a["L1_ffn_k_scale"]
    b1 = a["L1_ffn_b1"]
    lcol = np.concatenate(
        [columns(a["L1_ffn_ln_g"], 1), columns(a["L1_ffn_ln_b"], 1), columns(a["L1_ffn_b2"], 1),
         columns(b1[:, 0:HID], HC), columns(b1[:, HID:], HC)], 2)
    lw2 = np.zeros((P, 2, HC, C), np.float32)
    for c in range(HC):
        part = a["L1_ffn_w2"][:, c * P:(c + 1) * P]
        lw2[:part.shape[1], :, c] = part.transpose(1, 0, 2)
    return {
        "wg": a["L0_ffn_wg"], "ew1": a["L0_ffn_w1"],
        "ew2": a["L0_ffn_w2"].reshape(E, F // P, P, C).transpose(0, 2, 1, 3),
        "eb1": a["L0_ffn_b1"].reshape(E, F // P, P).transpose(0, 2, 1),
        "eb2": np.repeat(a["L0_ffn_b2"][:, None, :], P, 1),
        "lw": a["L1_ffn_wqkv"].transpose(1, 0, 2),
        "lqk": np.tile(np.stack([qs, qs[:, turn_l], ks, ks[:, turn_l]], 1), (P, 1, 1, 1)),
        "lwo": a["L1_ffn_wo"].reshape(2, PAIRS, P, C).transpose(2, 0, 1, 3),
        "lw1": a["L1_ffn_w1"].transpose(1, 0, 2), "lw2": lw2, "lcol": lcol,
        "xT": a["L0_attn_x"].transpose(0, 2, 1),
        "cT": np.stack([a["L0_c"].T, a["L1_c"].T], 1),
        "wmod": np.stack([a["L0_wmod"], a["L1_wmod"]], 1),
        "wqkv": wqkv, "pcol": pcol, "bv": np.tile(heads(a["L0_attn_bv"]), (P, 1)),
        "wo": np.stack([padded(a["L0_attn_Wo"]), padded(a["L1_attn_proj_w"].T)], 1),
        "bo": np.stack([a["L0_attn_bo"], a["L1_attn_proj_b"]], 1),
    }


def kernel(**inputs):
    import concourse.bacc as bacc
    from concourse.bass_utils import run_bass_kernel_spmd

    nc = bacc.Bacc("TRN2", target_bir_lowering=False, num_devices=1)
    data = {k: np.asarray(v) for k, v in inputs.items()}
    arrays = {f"in_{k}": np.ascontiguousarray(v) for k, v in {**constants(), **layouts(data)}.items()}
    ins = {k[3:]: nc.dram_tensor(k, v.shape, mybir.dt.from_np(v.dtype), kind="ExternalInput").ap()
           for k, v in arrays.items()}
    out = nc.dram_tensor("out_0", (B, C, N), F32, kind="ExternalOutput").ap()
    build(nc, ins, out)
    r = run_bass_kernel_spmd(nc, [arrays], core_ids=[0])
    return np.ascontiguousarray(r.results[0]["out_0"].transpose(0, 2, 1))
```
